# Optimizing a Trainium2 kernel written in Bass

```python
import numpy as np
import jax
import jax.numpy as jnp

def _softmax(x, axis=-1):
    return jax.nn.softmax(x, axis=axis)

def _gelu(x):
    return jax.nn.gelu(x, approximate=True)

def _silu(x):
    return jax.nn.silu(x)

def _sigmoid(x):
    return jax.nn.sigmoid(x)

def _layernorm(x, axis=-1, eps=1e-05):
    m = jnp.mean(x, axis=axis, keepdims=True)
    v = jnp.var(x, axis=axis, keepdims=True)
    return (x - m) / jnp.sqrt(v + eps)

def _scatter_add(tgt, idx, src, axis=0):
    return tgt.at[idx].add(src)

def _segment_sum(src, seg, n):
    return jax.ops.segment_sum(src, seg, n)
kernel_name = 'mk_lm_tower_d1_tok_ids256_r4_841f17'

def setup_inputs(seed: int=0):
    np.random.seed(seed)
    _w = jnp.asarray

    def _rec_inputs():
        import jax
        import jax.numpy as jnp
        _rk = jax.random.key(seed)
        x = jax.random.randint(jax.random.fold_in(_rk, 1), (32, 128), 0, 64, jnp.int32)
        itok_BS_0_255 = jax.random.randint(jax.random.fold_in(_rk, 21), (32, 128), 0, 64, jnp.int32)
        itok_BS_0_511 = jax.random.randint(jax.random.fold_in(_rk, 22), (32, 128), 0, 128, jnp.int32)
        itok_BS_0_127 = jax.random.randint(jax.random.fold_in(_rk, 23), (32, 128), 0, 128, jnp.int32)
        itok_BS_0_63 = jax.random.randint(jax.random.fold_in(_rk, 24), (32, 128), 0, 64, jnp.int32)
        itok_BS_0_3 = jax.random.randint(jax.random.fold_in(_rk, 25), (32, 128), 0, 4, jnp.int32)
        return (x, itok_BS_0_255, itok_BS_0_511, itok_BS_0_127, itok_BS_0_63, itok_BS_0_3)
    x, itok_BS_0_255, itok_BS_0_511, itok_BS_0_127, itok_BS_0_63, itok_BS_0_3 = _rec_inputs()

    def _L0_tok_setup():
        import jax, jax.numpy as jnp
        import numpy as np
        B, S = (128, 512)
        D_OUT = 64
        EMB = 16
        EPS_W = 1e-08
        EPS_LN = 1e-05

        def ternary_linear(x, W, b):
            scale = jnp.mean(jnp.abs(W))
            w_q = jnp.clip(jnp.round(W / (scale + EPS_W)), -1.0, 1.0) * scale
            w_eff = W + jax.lax.stop_gradient(w_q - W)
            return jnp.einsum('bsk,ok->bso', x, w_eff) + b

        def layer_norm(x, gamma, beta):
            mu = jnp.mean(x, axis=-1, keepdims=True)
            var = jnp.mean(jnp.square(x - mu), axis=-1, keepdims=True)
            return (x - mu) * jax.lax.rsqrt(var + EPS_LN) * gamma + beta
        key = jax.random.key(seed)
        ks = jax.random.split(key, 16)
        vocabs = {'event_type': 64, 'fault_class': 64, 'syscall_class': 128, 'opcode_family': 128, 'transition_type': 64, 'result_class': 4}
        inp = {}
        for i, (name, v) in enumerate(vocabs.items()):
            inp[name] = jax.random.randint(ks[i], (B, S), 0, v, dtype=jnp.int64)
        inp['E_et'] = jax.random.normal(ks[6], (64, EMB), dtype=jnp.float32)
        inp['E_fc'] = jax.random.normal(ks[7], (64, EMB), dtype=jnp.float32)
        inp['E_sc'] = jax.random.normal(ks[8], (128, EMB), dtype=jnp.float32)
        inp['E_of'] = jax.random.normal(ks[9], (128, EMB), dtype=jnp.float32)
        inp['E_tt'] = jax.random.normal(ks[10], (64, EMB), dtype=jnp.float32)
        inp['E_rc'] = jax.random.normal(ks[11], (4, EMB), dtype=jnp.float32)
        inp['W'] = jax.random.normal(ks[12], (D_OUT, 96), dtype=jnp.float32) * 0.1
        inp['b'] = jnp.zeros((D_OUT,), dtype=jnp.float32)
        inp['gamma'] = jnp.ones((D_OUT,), dtype=jnp.float32)
        inp['beta'] = jnp.zeros((D_OUT,), dtype=jnp.float32)
        return inp
    _L0_tok_all = _L0_tok_setup()
    _L0_tok_in = {k: v for k, v in _L0_tok_all.items() if k in ('E_et', 'E_fc', 'E_sc', 'E_of', 'E_tt', 'E_rc', 'W', 'b', 'gamma', 'beta')}
    del _L0_tok_all

    def _L0_attn_setup():
        import jax, jax.numpy as jnp
        import numpy as np
        key = jax.random.key(seed)
        k1, k2, k3 = jax.random.split(key, 3)
        b, n_t, n, n_h = (8, 256, 64, 8)
        s = jax.random.normal(k1, (b, n_t, n), dtype=jnp.float32)
        Q = jax.random.normal(k2, (n_h, n, n), dtype=jnp.float32) * 0.02
        E = jax.random.normal(k3, (n_h, n, n), dtype=jnp.float32) * 0.02
        return {'s': s, 'Q': Q, 'E': E}
    _L0_attn_all = _L0_attn_setup()
    _L0_attn_in = {k: v for k, v in _L0_attn_all.items() if k in ('Q', 'E')}
    del _L0_attn_all

    def _L0_ffn_setup():
        import jax, jax.numpy as jnp
        import numpy as np
        E = 8
        K = 2
        D = 64
        H = 128
        DOUT = 64
        EPS = 1e-05
        key = jax.random.key(seed)
        ks = jax.random.split(key, 9)
        s = 0.02
        return {'x': jax.random.normal(ks[0], (4, 2048, D), jnp.float32), 'gamma': 1.0 + 0.05 * jax.random.normal(ks[1], (D,), jnp.float32), 'beta': 0.05 * jax.random.normal(ks[2], (D,), jnp.float32), 'Wr': 0.01 * jax.random.normal(ks[3], (D, E), jnp.float32), 'br': jnp.zeros((E,), jnp.float32), 'W1': s * jax.random.normal(ks[4], (E, D, H), jnp.float32), 'b1': s * jax.random.normal(ks[5], (E, H), jnp.float32), 'W2': s * jax.random.normal(ks[6], (E, H, DOUT), jnp.float32), 'b2': s * jax.random.normal(ks[7], (E, DOUT), jnp.float32)}
    _L0_ffn_all = _L0_ffn_setup()
    _L0_ffn_in = {k: v for k, v in _L0_ffn_all.items() if k in ('gamma', 'beta', 'Wr', 'br', 'W1', 'b1', 'W2', 'b2')}
    del _L0_ffn_all
    return {'x': x, 'itok_BS_0_255': itok_BS_0_255, 'itok_BS_0_511': itok_BS_0_511, 'itok_BS_0_127': itok_BS_0_127, 'itok_BS_0_63': itok_BS_0_63, 'itok_BS_0_3': itok_BS_0_3, 'L0_tok_E_et': _L0_tok_in['E_et'], 'L0_tok_E_fc': _L0_tok_in['E_fc'], 'L0_tok_E_sc': _L0_tok_in['E_sc'], 'L0_tok_E_of': _L0_tok_in['E_of'], 'L0_tok_E_tt': _L0_tok_in['E_tt'], 'L0_tok_E_rc': _L0_tok_in['E_rc'], 'L0_tok_W': _L0_tok_in['W'], 'L0_tok_b': _L0_tok_in['b'], 'L0_tok_gamma': _L0_tok_in['gamma'], 'L0_tok_beta': _L0_tok_in['beta'], 'L0_attn_Q': _L0_attn_in['Q'], 'L0_attn_E': _L0_attn_in['E'], 'L0_ffn_gamma': _L0_ffn_in['gamma'], 'L0_ffn_beta': _L0_ffn_in['beta'], 'L0_ffn_Wr': _L0_ffn_in['Wr'], 'L0_ffn_br': _L0_ffn_in['br'], 'L0_ffn_W1': _L0_ffn_in['W1'], 'L0_ffn_b1': _L0_ffn_in['b1'], 'L0_ffn_W2': _L0_ffn_in['W2'], 'L0_ffn_b2': _L0_ffn_in['b2']}

def reference(x, itok_BS_0_255, itok_BS_0_511, itok_BS_0_127, itok_BS_0_63, itok_BS_0_3, L0_tok_E_et, L0_tok_E_fc, L0_tok_E_sc, L0_tok_E_of, L0_tok_E_tt, L0_tok_E_rc, L0_tok_W, L0_tok_b, L0_tok_gamma, L0_tok_beta, L0_attn_Q, L0_attn_E, L0_ffn_gamma, L0_ffn_beta, L0_ffn_Wr, L0_ffn_br, L0_ffn_W1, L0_ffn_b1, L0_ffn_W2, L0_ffn_b2):
    import jax
    import jax.numpy as jnp

    def _L0_tok_ref(event_type, fault_class, syscall_class, opcode_family, transition_type, result_class, E_et, E_fc, E_sc, E_of, E_tt, E_rc, W, b, gamma, beta):
        import jax, jax.numpy as jnp
        import numpy as np
        B, S = (128, 512)
        D_OUT = 64
        EMB = 16
        EPS_W = 1e-08
        EPS_LN = 1e-05

        def ternary_linear(x, W, b):
            scale = jnp.mean(jnp.abs(W))
            w_q = jnp.clip(jnp.round(W / (scale + EPS_W)), -1.0, 1.0) * scale
            w_eff = W + jax.lax.stop_gradient(w_q - W)
            return jnp.einsum('bsk,ok->bso', x, w_eff) + b

        def layer_norm(x, gamma, beta):
            mu = jnp.mean(x, axis=-1, keepdims=True)
            var = jnp.mean(jnp.square(x - mu), axis=-1, keepdims=True)
            return (x - mu) * jax.lax.rsqrt(var + EPS_LN) * gamma + beta
        combined = jnp.concatenate([E_et[event_type], E_fc[fault_class], E_sc[syscall_class], E_of[opcode_family], E_tt[transition_type], E_rc[result_class]], axis=-1)
        z = ternary_linear(combined, W, b)
        return layer_norm(z, gamma, beta)

    def _L0_attn_ref(s, Q, E):
        import jax, jax.numpy as jnp
        import numpy as np
        n_t = s.shape[1]
        qs = jnp.einsum('bti,hij->bhtj', s, Q)
        Omega = jnp.einsum('bhtj,buj->bhtu', qs, s)
        mask = jnp.tril(jnp.ones((n_t, n_t), dtype=s.dtype))
        Omega = Omega * mask
        es = jnp.einsum('hij,buj->bhui', E, s)
        r = jnp.einsum('bhtu,bhui->bti', Omega, es)
        return r

    def _L0_ffn_ref(x, gamma, beta, Wr, br, W1, b1, W2, b2):
        import jax, jax.numpy as jnp
        import numpy as np
        E = 8
        K = 2
        D = 64
        H = 128
        DOUT = 64
        EPS = 1e-05
        mu = jnp.mean(x, axis=-1, keepdims=True)
        var = jnp.mean(jnp.square(x - mu), axis=-1, keepdims=True)
        xn = (x - mu) * jax.lax.rsqrt(var + EPS) * gamma + beta
        logits = jnp.einsum('bsd,de->bse', xn, Wr) + br
        top_vals, top_idx = jax.lax.top_k(logits, K)
        w = jax.nn.softmax(top_vals, axis=-1)
        w_full = jnp.einsum('bsk,bske->bse', w, jax.nn.one_hot(top_idx, E, dtype=w.dtype))
        y = jnp.zeros(x.shape[:-1] + (DOUT,), x.dtype)
        for e in range(E):
            h = jax.nn.gelu(jnp.einsum('bsd,dh->bsh', xn, W1[e]) + b1[e], approximate=False)
            y_e = jnp.einsum('bsh,hd->bsd', h, W2[e]) + b2[e]
            y = y + y_e * w_full[..., e, None]
        return y
    h = _L0_tok_ref(x, itok_BS_0_255, itok_BS_0_511, itok_BS_0_127, itok_BS_0_63, itok_BS_0_3, L0_tok_E_et, L0_tok_E_fc, L0_tok_E_sc, L0_tok_E_of, L0_tok_E_tt, L0_tok_E_rc, L0_tok_W, L0_tok_b, L0_tok_gamma, L0_tok_beta)
    h = h + _L0_attn_ref(_layernorm(h, axis=-1), L0_attn_Q, L0_attn_E)
    h = h + _L0_ffn_ref(_layernorm(h, axis=-1), L0_ffn_gamma, L0_ffn_beta, L0_ffn_Wr, L0_ffn_br, L0_ffn_W1, L0_ffn_b1, L0_ffn_W2, L0_ffn_b2)
    return h

_drawn_inputs = setup_inputs


def setup_inputs(seed=0):
    import zlib

    import numpy as np

    out = dict(_drawn_inputs(seed))
    spreads = {'L0_tok_b': (0.0, 0.1),
     'L0_tok_gamma': (1.0, 0.2),
     'L0_tok_beta': (0.0, 0.1),
     'L0_ffn_br': (0.0, 0.8)}
    factors = {'L0_ffn_gamma': 8.0,
     'L0_ffn_beta': 8.0,
     'L0_ffn_Wr': 8.0,
     'L0_ffn_W1': 8.0,
     'L0_ffn_b1': 36.295,
     'L0_ffn_W2': 8.0,
     'L0_ffn_b2': 49.047}
    for name, (base, spread) in spreads.items():
        noise = np.random.default_rng([zlib.crc32(name.encode()), seed]).standard_normal(out[name].shape)
        drawn = base * np.exp(spread * noise) if base else spread * noise
        out[name] = jnp.asarray(drawn.astype(out[name].dtype))
    for name, factor in factors.items():
        out[name] = (out[name] * factor).astype(out[name].dtype)
    return out
```

```python
from contextlib import ExitStack

import concourse.bass as bass
from concourse import mybir

P = 128
ALU = mybir.AluOpType
ACT = mybir.ActivationFunctionType
AX = mybir.AxisListType
F32 = mybir.dt.float32
F16 = mybir.dt.float16
BF16 = mybir.dt.bfloat16
I32 = mybir.dt.int32
RMAX = bass.bass_isa.ReduceOp.max


class Steps:

    def __init__(self, eng, sem, base=0, per_iteration=None):
        self.eng, self.sem, self.base, self.n, self.per = eng, sem, base, 0, per_iteration

    def done(self, instruction):
        instruction.then_inc(self.sem, 1)
        self.n += 1

    def settle(self):
        self.eng.wait_ge(self.sem, self.base + self.n)

    def close(self):
        assert self.per is None or self.n == self.per, (self.n, self.per)


def lm_tower(nc, idx, tables, W, b, gamma, beta, Q, E, fgamma, fbeta, Wr, br, W1, b1, W2, b2, out):
    B, S = idx[0].shape
    N = B * S
    NT = N // P
    TG = 4
    NG = NT // TG
    GC = TG * P
    D, KW = W.shape
    EMB = KW // len(tables)
    H = Q.shape[0]
    NX, _, FH = W1.shape
    HP = H // 2
    NC = 4
    EPS = 1e-5
    LIFT = (16.0, 1024.0, 1024.0)
    assert S == P and D == 64 and FH == P and H * D == 512 and NX * D == 512

    place = [(0, 0), (0, 64), (1, 0), (2, 0), (3, 0), (3, 64)]
    half_row = [0, 1, 2, 2, 3, 3, 4, 5]

    with ExitStack() as ctx:
        def sb(name, shape, dt=F32):
            return ctx.enter_context(nc.sbuf_tensor(name, shape, dt))

        def sem(name):
            return ctx.enter_context(nc.semaphore(name))

        bank = [ctx.enter_context(nc.psum_tensor(f"bank{i}", [P, 512], F32)) for i in range(8)]

        ident = sb("ident", [P, P])
        ident16 = sb("ident16", [P, P], F16)
        fold = sb("fold", [P, D])
        causal = sb("causal", [P, P])
        causal_q = sb("causal_q", [P, P])
        ones = sb("ones", [P, P])
        sel = sb("sel", [96, NC * P], BF16)
        row_i = sb("row_i", [P, NC], I32)
        row_id = sb("row_id", [P, NC])
        rank = sb("rank", [P, NX])
        rank_i = sb("rank_i", [P, NX], I32)
        sel_w = sb("sel_w", [96, NX, P], F16)
        idx_i = sb("idx_i", [6, N], I32)
        idx_b = sb("idx_b", [96, N], BF16)
        emb = sb("emb", [P, NC, KW + 1])
        embT = sb("embT", [KW + 1, NC, P])
        w_raw = sb("w_raw", [D, KW])
        w_abs = sb("w_abs", [D, 1])
        w_s = sb("w_s", [P, 4])
        w_pos = sb("w_pos", [D, KW])
        w_neg = sb("w_neg", [D, KW])
        wT = sb("wT", [KW + 1, D])
        tab_f = sb("tab_f", [P, NC, D])
        tab = sb("tab", [P, NC, 3, D], BF16)
        gam = sb("gam", [P, D])
        bet = sb("bet", [P, D])
        q_raw = sb("q_raw", [P, H, D])
        e_raw = sb("e_raw", [D, H, D])
        w1_raw = sb("w1_raw", [P, NX, FH])
        wr_raw = sb("wr_raw", [P, NX])
        fg = sb("fg", [P, 1])
        fb = sb("fb", [P, 1])
        b1_raw = sb("b1_raw", [NX, FH])
        br_raw = sb("br_raw", [1, NX])
        b2_raw = sb("b2_raw", [96, D])
        b2_h = sb("b2_h", [96, D], BF16)
        b2_m = sb("b2_m", [96, D], BF16)
        b2_p = sb("b2_p", [96, D], BF16)
        w2 = sb("w2", [FH, NX, D])
        peak = sb("peak", [P, 3])
        peak_all = sb("peak_all", [P, 3])
        pow2 = sb("pow2", [P, 3])
        up = sb("up", [P, 3])
        down = sb("down", [P, 3])
        q_hi = sb("q_hi", [P, H * D], F16)
        q_lo = sb("q_lo", [P, H * D], F16)
        eT = sb("eT", [P, HP, D])
        w1_hi = sb("w1_hi", [P, NX, FH], F16)
        w1_lo = sb("w1_lo", [P, NX, FH], F16)
        wr_hi = sb("wr_hi", [P, NX], F16)
        wr_lo = sb("wr_lo", [P, NX], F16)
        b1_f = sb("b1_f", [FH, NX])
        br_f = sb("br_f", [P, NX])
        beta_row = sb("beta_row", [D, P])
        z = sb("z", [P, NT, D])
        h = sb("h", [P, NT, D])
        stats = sb("stats", [P, NT, 6])
        mean = sb("mean", [P, NT])
        var = sb("var", [P, NT])
        rstd = sb("rstd", [P, NT])
        tmp = sb("tmp", [P, NT])
        tmp2 = sb("tmp2", [P, NT])
        xT = sb("xT", [P, N], F16)
        hot = sb("hot", [P, 2, NC, GC], BF16)
        idx_c = sb("idx_c", [P, 2, NC, GC], BF16)
        s32 = sb("s32", [P, 2, TG, D])
        s16 = sb("s16", [P, TG, 4, D], F16)
        sTm = sb("sTm", [P, GC], F16)
        sTh = sb("sTh", [P, GC], F16)
        sTl = sb("sTl", [P, GC], F16)
        qh = sb("qh", [P, HP, GC], F16)
        ql = sb("ql", [P, HP, GC], F16)
        om8 = sb("om8", [P, 2 * TG, HP, P])
        aT = sb("aT", [P, HP, GC])
        rT = sb("rT", [P, GC])
        x32 = sb("x32", [P, 2, TG, D])
        x16 = sb("x16", [P, 2, TG, 2, D], F16)
        hid = sb("hid", [P, NX, GC])
        hw = sb("hw", [P, NX, GC])
        gT = sb("gT", [96, 2, GC], F16)
        yT = sb("yT", [P, GC])
        res = sb("res", [P, NT, D])
        lg = sb("lg", [P, NT, NX])
        lg2 = sb("lg2", [P, NT, NX])
        pick = sb("pick", [P, NT, NX])
        sel1 = sb("sel1", [P, NT, NX])
        sel2 = sb("sel2", [P, NT, NX])
        gate = sb("gate", [P, NT, NX])
        gate16 = sb("gate16", [P, NT, 3, 4, NX], F16)
        top1 = sb("top1", [P, NT])
        top2 = sb("top2", [P, NT])
        best = sb("best", [P, NT])
        ratio = sb("ratio", [P, NT])
        wt1 = sb("wt1", [P, NT])
        wt2 = sb("wt2", [P, NT])

        s_idx = sem("s_idx"); s_w = sem("s_w"); s_emb = sem("s_emb"); s_wgt = sem("s_wgt")
        s_gam = sem("s_gam"); s_b2 = sem("s_b2"); s_out = sem("s_out")
        s_ones = sem("s_ones"); s_pool = sem("s_pool"); pool_step = sem("pool_step")
        s_sel = sem("s_sel"); s_id = sem("s_id"); s_amax = sem("s_amax"); pool_h = sem("pool_h")
        emb_zero = sem("emb_zero"); b2_zero = sem("b2_zero"); dve_setup = sem("dve_setup")
        pe_wabs = sem("pe_wabs"); w_sum = sem("w_sum"); w_ready = sem("w_ready")
        pe_embT = sem("pe_embT"); embT_ready = sem("embT_ready"); pe_tab = sem("pe_tab")
        tab_ready = sem("tab_ready"); idx_zero = sem("idx_zero"); idx_ready = sem("idx_ready")
        pe_eT = sem("pe_eT"); e_ready = sem("e_ready"); s_peak = sem("s_peak")
        q_ready = sem("q_ready"); beta_ready = sem("beta_ready"); pe_bias = sem("pe_bias")
        w1_ready = sem("w1_ready"); one_ready = sem("one_ready"); w1_scaled = sem("w1_scaled"); b2_ready = sem("b2_ready"); scale_ready = sem("scale_ready")
        q_hi_ready = sem("q_hi_ready"); w1_hi_ready = sem("w1_hi_ready"); bias_read = sem("bias_read")
        spread = sem("spread"); copied = sem("copied"); hot_ready = sem("hot_ready")
        z_done = sem("z_done"); z_ready = sem("z_ready"); z_stats = sem("z_stats")
        ln1_var = sem("ln1_var"); ln1_sd = sem("ln1_sd"); zn_ready = sem("zn_ready")
        h_ready = sem("h_ready"); h_stats = sem("h_stats"); ln2_var = sem("ln2_var"); ln2_sd = sem("ln2_sd")
        dve_ln = sem("dve_ln")
        dve_s = sem("dve_s"); s_ready = sem("s_ready"); t_done = sem("t_done")
        sTm_ready = sem("sTm_ready"); sT_ready = sem("sT_ready")
        q_done = sem("q_done"); qh_ready = sem("qh_ready"); q_used = sem("q_used")
        om_done = sem("om_done"); om_ready = sem("om_ready")
        a_done = sem("a_done"); a_ready = sem("a_ready")
        r_done = sem("r_done"); rT_ready = sem("rT_ready"); back_done = sem("back_done")
        back_ready = sem("back_ready"); h2_stats = sem("h2_stats")
        ln3_var = sem("ln3_var"); ln3_sd = sem("ln3_sd"); x_ready = sem("x_ready")
        xt_done = sem("xt_done"); xT_ready = sem("xT_ready"); lg_done = sem("lg_done")
        lg_read = sem("lg_read"); r_exp = sem("r_exp"); exp_done = sem("exp_done")
        dve_ln3 = sem("dve_ln3"); dve_gate = sem("dve_gate"); gate_zero = sem("gate_zero")
        gate_ready = sem("gate_ready"); gt_done = sem("gt_done"); gT_ready = sem("gT_ready")
        hid_done = sem("hid_done"); hid_ready = sem("hid_ready"); w_done = sem("w_done")
        hw_ready = sem("hw_ready"); y_part = sem("y_part"); y_done = sem("y_done")
        yT_ready = sem("yT_ready"); fin_done = sem("fin_done"); res_ready = sem("res_ready")

        block = ctx.enter_context(nc.Block())

        N_WGT = 16 * 13
        OM_BANK = [0, 1, 2, 0, 1, 2, 0, 1]
        Q_BANK = [0, 1, 1, 0]
        A_BANK = [0, 1, 0, 1]

        def tiles(g):
            return bass.ds(g * TG, TG)

        def wait(eng, s, value):
            if not isinstance(value, int) or value > 0:
                eng.wait_ge(s, value)

        @block.sync
        def _(sp):
            for n, a in enumerate(idx):
                sp.dma_start(idx_i[n:n + 1, :], a.rearrange("(a b) s -> a (b s)", a=1)).then_inc(s_idx, 16)
            sp.wait_ge(emb_zero, 1)
            for n, (t, (c, r)) in enumerate(zip(tables, place)):
                v = t.shape[0]
                sp.dma_start(emb[r:r + v, c, n * EMB:(n + 1) * EMB], t).then_inc(s_emb, 16)
            sp.dma_start(gam[:, :], gamma.rearrange("(a n) -> a n", a=1).broadcast_to([P, D])).then_inc(s_gam, 16)
            sp.dma_start(bet[:, :], beta.rearrange("(a n) -> a n", a=1).broadcast_to([P, D])).then_inc(s_gam, 16)
            sp.dma_start(q_raw[0:D, :, :], Q.rearrange("h i j -> i h j")).then_inc(s_wgt, 16)
            sp.dma_start(q_raw[D:P, :, :], Q.rearrange("h i j -> i h j")).then_inc(s_wgt, 16)
            sp.dma_start(e_raw[:, :, :], E.rearrange("h i j -> i h j")).then_inc(s_wgt, 16)
            for a in range(2):
                sp.dma_start(w1_raw[a * D:a * D + D, :, :], W1.rearrange("e d f -> d e f")).then_inc(s_wgt, 16)
                sp.dma_start(wr_raw[a * D:a * D + D, :], Wr).then_inc(s_wgt, 16)
                sp.dma_start(fg[a * D:a * D + D, :], fgamma.rearrange("(d a) -> d a", a=1)).then_inc(s_wgt, 16)
            sp.dma_start(fb[0:D, :], fbeta.rearrange("(d a) -> d a", a=1)).then_inc(s_wgt, 16)
            sp.dma_start(b1_raw[:, :], b1).then_inc(s_wgt, 16)
            sp.dma_start(br_raw[:, :], br.rearrange("(a n) -> a n", a=1)).then_inc(s_wgt, 16)
            sp.dma_start(w2[:, :, :], W2.rearrange("e f d -> f e d")).then_inc(s_wgt, 16)
            sp.wait_ge(b2_zero, 1)
            for k in (0, 8, 32, 40, 64, 72):
                sp.dma_start(b2_raw[k:k + NX, :], b2).then_inc(s_b2, 16)
            out_v = out.rearrange("(g t) p d -> p g t d", t=TG)
            res_v = res[:, :, :].rearrange("p (g t) d -> p g t d", t=TG)
            with sp.Fori(0, NG) as g:
                sp.wait_ge(res_ready, g + 1)
                sp.dma_start(out_v[:, bass.ds(g, 1), :, :].rearrange("p g t d -> p (g t) d"),
                             res_v[:, bass.ds(g, 1), :, :].rearrange("p g t d -> p (g t) d")).then_inc(s_out, 16)
            sp.wait_ge(s_out, 16 * NG)

        @block.gpsimd
        def _(pool):
            st = Steps(pool, pool_step)

            def link(ins):
                st.done(ins)
                st.settle()

            def select(a, pattern, base, slope, compare=ALU.not_equal, fill=1.0):
                link(pool.affine_select(out=a, in_=a, compare_op=compare, fill=fill, base=base, pattern=pattern,
                                        channel_multiplier=slope))

            pool.memset(emb[:, :, :], 0.0).then_inc(emb_zero, 1)
            link(pool.memset(ones[:, :], 1.0))
            pool.sem_inc(s_ones, 1)
            link(pool.memset(ident[:, :], 0.0))
            select(ident[:, :], [[-1, P]], 0, 1)
            pool.sem_inc(s_id, 1)
            link(pool.iota(row_i[:, :], pattern=[[0, NC]], base=0, channel_multiplier=1))
            for c in (0, 3):
                link(pool.iota(row_i[64:P, c:c + 1], pattern=[[0, 1]], base=0, channel_multiplier=1))
            link(pool.memset(sel[:, :], 0.0))
            for k, r in enumerate(half_row):
                select(sel[:, k * 64:(k + 1) * 64], [[0, 64]], -r, 1)
            pool.sem_inc(s_sel, 1)
            link(pool.tensor_copy(ident16[:, :], ident[:, :]))
            pool.memset(b2_raw[:, :], 0.0).then_inc(b2_zero, 1)
            link(pool.memset(fold[:, :], 0.0))
            select(fold[:, :], [[-1, D]], 0, 1)
            select(fold[:, :], [[-1, D]], -D, 1)
            link(pool.memset(causal[:, :], 1.0))
            select(causal[:, :], [[1, P]], 0, -1, ALU.is_ge, 0.0)
            link(pool.iota(rank_i[:, :], pattern=[[-1, NX]], base=NX, channel_multiplier=0))
            pool.sem_inc(s_pool, 1)
            pool.wait_ge(s_peak, 1)
            pool.partition_all_reduce(peak_all[:, 0:1], peak[:, 0:1], P, RMAX).then_inc(s_amax, 1)
            pool.wait_ge(s_gam, 32)
            for k in range(4):
                tt = slice(k * 8, k * 8 + 8)
                pool.wait_ge(zn_ready, k + 1)
                pool.tensor_tensor(h[:, tt, :], z[:, tt, :], gam[:, :].unsqueeze(1).broadcast_to([P, 8, D]),
                                   ALU.mult).then_inc(pool_h, 1)
                pool.wait_ge(pool_h, k + 1)
                pool.tensor_tensor(h[:, tt, :], h[:, tt, :], bet[:, :].unsqueeze(1).broadcast_to([P, 8, D]),
                                   ALU.add).then_inc(h_ready, 1)
            pool.wait_ge(s_peak, 3)
            pool.partition_all_reduce(peak_all[:, 1:3], peak[:, 1:3], P, RMAX).then_inc(s_amax, 1)
            link(pool.memset(sel_w[:, :, :], 0.0))
            for k in (0, NX):
                select(sel_w[:, :, :], [[-1, NX], [0, P]], -k, 1)
            pool.sem_inc(gate_zero, 1)
            pool.memset(gate16[:, :, :, :, :], 0.0).then_inc(gate_zero, 1)

        @block.vector
        def _(dve):
            st = Steps(dve, dve_setup)

            def link(ins):
                st.done(ins)
                st.settle()

            def row(a):
                return a.rearrange("p a d -> p (a d)")

            dve.memset(idx_b[:, :].bitcast(I32), 0).then_inc(idx_zero, 1)
            dve.wait_ge(emb_zero, 1)
            dve.memset(emb[64:68, 3, KW:KW + 1], 1.0).then_inc(one_ready, 1)
            dve.wait_ge(s_w, 16)
            dve.tensor_reduce(w_abs[:, :], w_raw[:, :], AX.X, ALU.add, apply_absolute_value=True).then_inc(w_sum, 1)
            dve.wait_ge(s_idx, 96)
            dve.wait_ge(idx_zero, 1)
            dve.tensor_copy(idx_b[0:6, 0:N // 2], idx_i[:, 0:N // 2]).then_inc(idx_ready, 1)
            dve.wait_ge(pe_wabs, 1)
            link(dve.tensor_scalar(w_s[:, 0:1], bank[0][:, 0:1], 1.0 / (D * KW), None, ALU.mult))
            st.done(dve.tensor_scalar(w_s[:, 1:2], w_s[:, 0:1], 1e-8, 0.5, ALU.add, ALU.mult))
            link(dve.tensor_scalar(w_s[:, 2:3], w_s[:, 0:1], 1e-8, -0.5, ALU.add, ALU.mult))
            st.done(dve.tensor_scalar(w_pos[:, :], w_raw[:, :], w_s[0:D, 1:2], None, ALU.is_gt))
            link(dve.tensor_scalar(w_neg[:, :], w_raw[:, :], w_s[0:D, 2:3], None, ALU.is_lt))
            link(dve.tensor_tensor(w_pos[:, :], w_pos[:, :], w_neg[:, :], ALU.subtract))
            link(dve.scalar_tensor_tensor(out=w_pos[:, :], in0=w_pos[:, :], scalar=w_s[0:D, 0:1], in1=w_raw[:, :],
                                          op0=ALU.mult, op1=ALU.subtract))
            dve.tensor_tensor(w_pos[:, :], w_pos[:, :], w_raw[:, :], ALU.add).then_inc(w_ready, 1)
            dve.wait_ge(pe_embT, 5)
            dve.tensor_copy(wT[0:KW, :], bank[5][0:KW, 0:D]).then_inc(embT_ready, 1)
            dve.wait_ge(s_sel, 1)
            link(dve.tensor_copy(row_id[:, :], row_i[:, :]))
            dve.wait_ge(pe_tab, 1)
            link(dve.tensor_copy(tab_f[:, :, :], bank[6][:, 0:NC * D].rearrange("p (c d) -> p c d", d=D)))
            for k in range(3):
                part = dve.tensor_copy(tab[:, :, k, :], tab_f[:, :, :])
                if k == 2:
                    part.then_inc(tab_ready, 1)
                    break
                link(part)
                link(dve.tensor_tensor(tab_f[:, :, :], tab_f[:, :, :], tab[:, :, k, :], ALU.subtract))

            def one_hot(g, u):
                for c in range(NC):
                    if c == 0:
                        dve.wait_ge(spread, g * NC + 1)
                        src = bank[0][:, :]
                    else:
                        dve.wait_ge(copied, g * 3 + c)
                        src = idx_c[:, u, c, :]
                    dve.tensor_scalar(hot[:, u, c, :], src, row_id[:, c:c + 1], None, ALU.is_equal).then_inc(hot_ready, 1)

            def z_moments(g):
                dve.wait_ge(z_ready, g + 1)
                for t in range(TG):
                    tt = bass.ds(g * TG + t, 1)
                    dve.bn_stats(row(stats[:, tt, :]), row(z[:, tt, :])).then_inc(z_stats, 1)

            def scales(x, y):
                link(dve.tensor_scalar(peak_all[:, x:y], peak_all[:, x:y], 1e-30, None, ALU.max))
                link(dve.tensor_scalar(pow2[:, x:y].bitcast(I32), peak_all[:, x:y].bitcast(I32), 0x7F800000, None,
                                       ALU.bitwise_and))
                link(dve.reciprocal(up[:, x:y], pow2[:, x:y]))
                for k in range(x, y):
                    dve.tensor_scalar(up[:, k:k + 1], up[:, k:k + 1], LIFT[k], None, ALU.mult).then_inc(scale_ready, 1)
                    st.done(dve.tensor_scalar(down[:, k:k + 1], pow2[:, k:k + 1], 1.0 / LIFT[k], None, ALU.mult))
                st.settle()

            one_hot(0, 0)
            one_hot(1, 1)
            dve.wait_ge(s_wgt, N_WGT)
            dve.tensor_reduce(peak[:, 0:1], q_raw[:, :, :], AX.XY, ALU.max, apply_absolute_value=True).then_inc(s_peak, 1)
            link(dve.tensor_copy(beta_row[:, :], fb[0:D, 0:1].broadcast_to([D, P])))
            dve.wait_ge(s_amax, 1)
            scales(0, 1)
            dve.wait_ge(q_hi_ready, 1)
            dve.scalar_tensor_tensor(out=q_lo[:, :], in0=q_raw[:, :, :].rearrange("p h j -> p (h j)"),
                                     scalar=up[:, 0:1], in1=q_hi[:, :], op0=ALU.mult,
                                     op1=ALU.subtract).then_inc(q_ready, 1)
            dve.wait_ge(s_pool, 1)
            link(dve.tensor_scalar(causal_q[:, :], causal[:, :], down[:, 0:1], None, ALU.mult))
            with dve.Fori(1, NG // 2) as i:
                for u in range(2):
                    dve.wait_ge(z_done, i * 2 + u - 1)
                    one_hot(i * 2 + u, u)
                    z_moments(i * 2 + u - 2)
            z_moments(NG - 2)
            z_moments(NG - 1)

            ch = Steps(dve, dve_ln)

            def moments(a, b):
                def f(k):
                    return stats[:, a:b, k]
                ch.done(dve.tensor_tensor(mean[:, a:b], f(1), f(4), ALU.add))
                ch.done(dve.tensor_tensor(tmp[:, a:b], f(1), f(4), ALU.subtract))
                ch.done(dve.tensor_tensor(var[:, a:b], f(2), f(5), ALU.add))
                ch.settle()
                ch.done(dve.tensor_scalar(mean[:, a:b], mean[:, a:b], 0.5, None, ALU.mult))
                ch.done(dve.scalar_tensor_tensor(out=tmp[:, a:b], in0=tmp[:, a:b], scalar=0.25, in1=tmp[:, a:b],
                                                 op0=ALU.mult, op1=ALU.mult))
                ch.settle()
                ch.done(dve.scalar_tensor_tensor(out=var[:, a:b], in0=var[:, a:b], scalar=1.0 / D, in1=tmp[:, a:b],
                                                 op0=ALU.mult, op1=ALU.add))
                ch.settle()

            def over(a, x, y):
                return a[:, x:y].unsqueeze(2).broadcast_to([P, y - x, D])

            dve.wait_ge(z_stats, NT)
            moments(0, NT)
            dve.tensor_scalar(tmp[:, :], var[:, :], EPS, None, ALU.add).then_inc(ln1_var, 1)
            dve.wait_ge(ln1_sd, 1)
            ch.done(dve.reciprocal(rstd[:, :], tmp2[:, :]))
            ch.settle()
            for k in range(4):
                x, y = k * 8, k * 8 + 8
                ch.done(dve.tensor_tensor(z[:, x:y, :], z[:, x:y, :], over(mean, x, y), ALU.subtract))
                ch.settle()
                dve.tensor_tensor(z[:, x:y, :], z[:, x:y, :], over(rstd, x, y), ALU.mult).then_inc(zn_ready, 1)
            dve.wait_ge(pe_bias, 1)
            link(dve.tensor_copy(b1_f[:, :], bank[7][:, 0:NX]))
            st.done(dve.tensor_tensor(b1_f[:, :], b1_f[:, :], bank[7][:, NX:2 * NX], ALU.add))
            st.done(dve.tensor_copy(br_f[:, :], bank[7][:, 2 * NX:3 * NX]))
            dve.tensor_copy(eT[:, :, :], bank[7][:, 256:256 + HP * D].rearrange("p (a d) -> p a d", d=D)).then_inc(e_ready, 1)
            dve.wait_ge(w1_scaled, 2)
            dve.tensor_reduce(peak[:, 1:2], w1_raw[:, :, :], AX.XY, ALU.max, apply_absolute_value=True).then_inc(s_peak, 1)
            dve.tensor_reduce(peak[:, 2:3], wr_raw[:, :], AX.X, ALU.max, apply_absolute_value=True).then_inc(s_peak, 1)

            def h_moments(half):
                for k in (2 * half, 2 * half + 1):
                    dve.wait_ge(h_ready, k + 1)
                    for t in range(8 * k, 8 * k + 8):
                        dve.bn_stats(stats[:, t, :], h[:, t, :]).then_inc(h_stats, 1)
                x, y = half * NT // 2, (half + 1) * NT // 2
                dve.wait_ge(h_stats, y)
                moments(x, y)
                dve.tensor_scalar(tmp[:, x:y], var[:, x:y], EPS, None, ALU.add).then_inc(ln2_var, 1)
                dve.wait_ge(ln2_sd, half + 1)
                ch.done(dve.reciprocal(rstd[:, x:y], tmp2[:, x:y]))
                ch.settle()

            SP = 3

            def normal(g, u):
                lc = Steps(dve, dve_s, g * SP, SP)
                wait(dve, t_done, g)
                wait(dve, a_done, (g - 1) * TG)
                lc.done(dve.tensor_tensor(s32[:, u, :, :], h[:, tiles(g), :],
                                          mean[:, tiles(g)].unsqueeze(2).broadcast_to([P, TG, D]), ALU.subtract))
                lc.settle()
                lc.done(dve.tensor_tensor(s32[:, u, :, :], s32[:, u, :, :],
                                          rstd[:, tiles(g)].unsqueeze(2).broadcast_to([P, TG, D]), ALU.mult))
                lc.settle()
                twice = s32[:, u, :, :].unsqueeze(2).broadcast_to([P, TG, 2, D])
                lc.done(dve.tensor_copy(s16[:, :, 0:2, :], twice))
                lc.settle()
                lc.close()
                dve.tensor_tensor(s16[:, :, 2:4, :], twice, s16[:, :, 0:2, :], ALU.subtract).then_inc(s_ready, 1)

            def mask(g, t):
                wait(dve, a_done, (g - 1) * TG + t + 1)
                dve.wait_ge(om_done, g * TG + t + 1)
                for n in (2 * t, 2 * t + 1):
                    dve.tensor_tensor(om8[:, n, :, :], bank[5 + OM_BANK[n]][:, :].rearrange("p (h t) -> p h t", t=P),
                                      causal_q[:, :].unsqueeze(1).broadcast_to([P, HP, P]), ALU.mult).then_inc(om_ready, 1)

            def back(g):
                dve.wait_ge(back_done, g + 1)
                dve.tensor_tensor(h[:, tiles(g), :], h[:, tiles(g), :],
                                  bank[1][:, 256:512].rearrange("p (t d) -> p t d", d=D), ALU.add).then_inc(back_ready, 1)
                dve.wait_ge(back_ready, g + 1)
                for t in range(TG):
                    tt = bass.ds(g * TG + t, 1)
                    dve.bn_stats(row(stats[:, tt, :]), row(h[:, tt, :])).then_inc(h2_stats, 1)

            def sT_copy(g):
                dve.wait_ge(t_done, g + 1)
                dve.wait_ge(sTm_ready, g + 1)
                wait(dve, om_done, g * TG)
                dve.tensor_copy(sTh[:, :], bank[0][:, 256:512].bitcast(F16)).then_inc(sT_ready, 1)
                dve.tensor_copy(sTl[:, :], bank[1][:, 0:256].bitcast(F16)).then_inc(sT_ready, 1)

            def q_lower(g):
                for n in range(HP):
                    dve.wait_ge(qh_ready, g * HP + n + 1)
                    dve.tensor_tensor(ql[:, n, :], bank[3 + Q_BANK[n]][:, :], qh[:, n, :],
                                      ALU.subtract).then_inc(q_used, 1)

            def attend(g, u, first=False, last=False):
                mask(g, 0)
                if not last:
                    normal(g + 1, 1 - u)
                mask(g, 1)
                if not first:
                    back(g - 1)
                mask(g, 2)
                mask(g, 3)
                if not last:
                    sT_copy(g + 1)
                    q_lower(g + 1)

            h_moments(0)
            normal(0, 0)
            sT_copy(0)
            q_lower(0)
            h_moments(1)
            dve.wait_ge(s_amax, 2)
            scales(1, 3)
            attend(0, 0, first=True)
            dve.wait_ge(w1_hi_ready, 2)
            dve.scalar_tensor_tensor(out=w1_lo[:, :, :], in0=w1_raw[:, :, :], scalar=up[:, 1:2], in1=w1_hi[:, :, :],
                                     op0=ALU.mult, op1=ALU.subtract).then_inc(w1_ready, 1)
            dve.scalar_tensor_tensor(out=wr_lo[:, :], in0=wr_raw[:, :], scalar=up[:, 2:3], in1=wr_hi[:, :],
                                     op0=ALU.mult, op1=ALU.subtract).then_inc(w1_ready, 1)
            dve.wait_ge(s_b2, 96)
            link(dve.tensor_copy(b2_h[:, :], b2_raw[:, :]))
            link(dve.tensor_tensor(b2_raw[:, :], b2_raw[:, :], b2_h[:, :], ALU.subtract))
            link(dve.tensor_copy(b2_m[:, :], b2_raw[:, :]))
            link(dve.tensor_tensor(b2_raw[:, :], b2_raw[:, :], b2_m[:, :], ALU.subtract))
            dve.tensor_copy(b2_p[0:32, :], b2_h[0:32, :]).then_inc(b2_ready, 1)
            dve.tensor_copy(b2_p[32:64, :], b2_m[32:64, :]).then_inc(b2_ready, 1)
            dve.tensor_copy(b2_p[64:96, :], b2_raw[64:96, :]).then_inc(b2_ready, 1)
            link(dve.tensor_copy(rank[:, :], rank_i[:, :]))
            with dve.Fori(0, (NG - 2) // 2) as i:
                for u in (1, 0):
                    attend(i * 2 + (1 if u else 2), u)
            attend(NG - 1, 1, last=True)
            back(NG - 1)

            dve.wait_ge(h2_stats, NT)
            moments(0, NT)
            dve.tensor_scalar(tmp[:, :], var[:, :], EPS, None, ALU.add).then_inc(ln3_var, 1)
            dve.wait_ge(ln3_sd, 1)
            ch.done(dve.reciprocal(rstd[:, :], tmp2[:, :]))
            ch.settle()
            ch.done(dve.tensor_tensor(tmp[:, :], rstd[:, :], rstd[:, :], ALU.mult))
            ch.settle()
            ch.done(dve.tensor_tensor(tmp[:, :], tmp[:, :], var[:, :], ALU.mult))
            ch.settle()
            dve.tensor_scalar(tmp[:, :], tmp[:, :], EPS, None, ALU.add).then_inc(ln3_var, 1)
            dve.wait_ge(ln3_sd, 2)
            ch.done(dve.reciprocal(tmp[:, :], tmp2[:, :]))
            ch.settle()
            ch.done(dve.tensor_tensor(rstd[:, :], rstd[:, :], tmp[:, :], ALU.mult))
            ch.settle()

            def expert_input(g, u, first=False):
                lc = Steps(dve, dve_ln3, g * SP, SP)
                if not first:
                    dve.wait_ge(xt_done, g - 1)
                    dve.wait_ge(x_ready, g - 1)
                lc.done(dve.tensor_tensor(x32[:, u, :, :], h[:, tiles(g), :],
                                          mean[:, tiles(g)].unsqueeze(2).broadcast_to([P, TG, D]), ALU.subtract))
                lc.settle()
                lc.done(dve.tensor_tensor(x32[:, u, :, :], x32[:, u, :, :],
                                          rstd[:, tiles(g)].unsqueeze(2).broadcast_to([P, TG, D]), ALU.mult))
                lc.settle()
                lc.done(dve.tensor_copy(x16[:, u, :, 0, :], x32[:, u, :, :]))
                lc.settle()
                lc.close()
                dve.tensor_tensor(x16[:, u, :, 1, :], x32[:, u, :, :], x16[:, u, :, 0, :],
                                  ALU.subtract).then_inc(x_ready, 1)

            expert_input(0, 0, True)
            expert_input(1, 1, True)
            with dve.Fori(1, NG // 2) as i:
                for u in range(2):
                    expert_input(i * 2 + u, u)

            gs = Steps(dve, dve_gate)
            halves = [slice(0, NT // 2), slice(NT // 2, NT)]

            def both(f):
                for x in halves:
                    gs.done(f(x))
                gs.settle()

            def wide(a, x):
                return a[:, x].unsqueeze(2).broadcast_to([P, NT // 2, NX])

            rank_w = rank[:, :].unsqueeze(1).broadcast_to([P, NT // 2, NX])
            dve.wait_ge(lg_done, NG)
            dve.tensor_scalar(lg[:, :, :], bank[2][:, 0:NT * NX].rearrange("p (t e) -> p t e", e=NX),
                              down[:, 2:3], None, ALU.mult).then_inc(lg_read, 1)
            dve.wait_ge(lg_read, 1)
            both(lambda x: dve.tensor_tensor(lg[:, x, :], lg[:, x, :],
                                             br_f[:, :].unsqueeze(1).broadcast_to([P, NT // 2, NX]), ALU.add))

            def pick_top(src, top, chosen):
                both(lambda x: dve.tensor_reduce(top[:, x], src[:, x, :], AX.X, ALU.max))
                both(lambda x: dve.tensor_tensor(pick[:, x, :], src[:, x, :], wide(top, x), ALU.is_equal))
                both(lambda x: dve.tensor_tensor(pick[:, x, :], pick[:, x, :], rank_w, ALU.mult))
                both(lambda x: dve.tensor_reduce(best[:, x], pick[:, x, :], AX.X, ALU.max))
                both(lambda x: dve.tensor_tensor(chosen[:, x, :], pick[:, x, :], wide(best, x), ALU.is_equal))

            pick_top(lg, top1, sel1)
            both(lambda x: dve.scalar_tensor_tensor(out=lg2[:, x, :], in0=sel1[:, x, :], scalar=-3e38, in1=lg[:, x, :],
                                                    op0=ALU.mult, op1=ALU.add))
            pick_top(lg2, top2, sel2)
            dve.tensor_tensor(best[:, :], top2[:, :], top1[:, :], ALU.subtract).then_inc(r_exp, 1)
            dve.wait_ge(exp_done, 1)
            both(lambda x: dve.tensor_scalar(wt1[:, x], ratio[:, x], 1.0, None, ALU.add))
            both(lambda x: dve.reciprocal(wt1[:, x], wt1[:, x]))
            both(lambda x: dve.tensor_tensor(wt2[:, x], wt1[:, x], ratio[:, x], ALU.mult))
            for x in halves:
                gs.done(dve.tensor_tensor(sel1[:, x, :], sel1[:, x, :], wide(wt1, x), ALU.mult))
            both(lambda x: dve.tensor_tensor(sel2[:, x, :], sel2[:, x, :], wide(wt2, x), ALU.mult))
            both(lambda x: dve.tensor_tensor(gate[:, x, :], sel1[:, x, :], sel2[:, x, :], ALU.add))
            dve.wait_ge(gate_zero, 2)
            for k in range(3):
                gs.done(dve.tensor_copy(gate16[:, :, k, 0, :], gate[:, :, :]))
            gs.settle()
            for k in range(3):
                dve.tensor_tensor(gate16[:, :, k, 1, :], gate[:, :, :], gate16[:, :, k, 0, :],
                                  ALU.subtract).then_inc(gate_ready, 1)

            def finish(g):
                dve.wait_ge(fin_done, g + 1)
                dve.tensor_tensor(res[:, tiles(g), :], h[:, tiles(g), :],
                                  bank[7][:, 0:256].rearrange("p (t d) -> p t d", d=D), ALU.add).then_inc(res_ready, 1)

            def gated(g, first=False):
                for e in range(NX):
                    dve.wait_ge(hid_ready, g * NX + e + 1)
                    dve.wait_ge(w_done, g * NX + e + 1)
                    if not first:
                        dve.wait_ge(y_part, (g - 1) * NX + e + 1)
                    dve.tensor_tensor(hw[:, e, :], hid[:, e, :], bank[3 + e % 2][:, :], ALU.mult).then_inc(hw_ready, 1)
                    if e == 4 and not first:
                        finish(g - 1)

            gated(0, True)
            with dve.Fori(1, NG) as g:
                gated(g)
            finish(NG - 1)

        @block.scalar
        def _(act):
            act.dma_start(w_raw[:, :], W).then_inc(s_w, 16)
            act.dma_start(wT[KW:KW + 1, :], b.rearrange("(a n) -> a n", a=1)).then_inc(s_emb, 16)
            act.wait_ge(s_idx, 96)
            act.wait_ge(idx_zero, 1)
            act.activation(idx_b[0:6, N // 2:N], idx_i[:, N // 2:N], ACT.Copy).then_inc(idx_ready, 1)
            for c in range(NC):
                act.wait_ge(pe_embT, c + 1)
                act.activation(embT[:, c, :], bank[1 + c][0:KW + 1, 0:P], ACT.Copy).then_inc(embT_ready, 1)

            def copies(g, u, first=False):
                for c in range(1, NC):
                    if not first:
                        act.wait_ge(hot_ready, (g - 2) * NC + c + 1)
                    act.wait_ge(spread, g * NC + c + 1)
                    act.activation(idx_c[:, u, c, :], bank[c][:, :], ACT.Copy).then_inc(copied, 1)

            def z_copy(g, u):
                act.wait_ge(z_done, g + 1)
                act.activation(z[:, tiles(g), :], bank[4 + u][:, 0:TG * D].rearrange("p (t d) -> p t d", d=D),
                               ACT.Copy).then_inc(z_ready, 1)

            copies(0, 0, True)
            copies(1, 1, True)
            act.wait_ge(scale_ready, 1)
            act.activation(q_hi[:, :], q_raw[:, :, :].rearrange("p h j -> p (h j)"), ACT.Copy,
                           scale=up[:, 0:1]).then_inc(q_hi_ready, 1)
            with act.Fori(1, NG // 2) as i:
                for u in range(2):
                    copies(i * 2 + u, u)
                    z_copy(i * 2 + u - 2, u)
            z_copy(NG - 2, 0)
            z_copy(NG - 1, 1)

            act.wait_ge(pe_bias, 1)
            act.activation(w1_raw[:, :, :], w1_raw[:, :, :], ACT.Copy, scale=fg[:, 0:1]).then_inc(w1_scaled, 1)
            act.activation(wr_raw[:, :], wr_raw[:, :], ACT.Copy, scale=fg[:, 0:1]).then_inc(w1_scaled, 1)
            act.wait_ge(ln1_var, 1)
            act.activation(tmp2[:, :], tmp[:, :], ACT.Sqrt).then_inc(ln1_sd, 1)

            def root(k):
                x, y = k * NT // 2, (k + 1) * NT // 2
                act.wait_ge(ln2_var, k + 1)
                act.activation(tmp2[:, x:y], tmp[:, x:y], ACT.Sqrt).then_inc(ln2_sd, 1)

            def sTm_copy(g):
                act.wait_ge(t_done, g + 1)
                wait(act, q_done, g * HP)
                act.activation(sTm[:, :], bank[0][:, 0:256].bitcast(F16), ACT.Copy).then_inc(sTm_ready, 1)

            def q_upper(g, n):
                act.wait_ge(q_done, g * HP + n + 1)
                wait(act, om_done, g * TG)
                act.activation(qh[:, n, :], bank[3 + Q_BANK[n]][:, :], ACT.Copy).then_inc(qh_ready, 1)

            def a_copy(g, t):
                act.wait_ge(a_done, g * TG + t + 1)
                wait(act, r_done, g)
                act.activation(aT[:, :, t * P:(t + 1) * P], bank[3 + A_BANK[t]][:, :].rearrange("p (a t) -> p a t", t=P),
                               ACT.Copy).then_inc(a_ready, 1)

            def r_copy(g):
                act.wait_ge(r_done, g + 1)
                wait(act, back_done, g)
                act.activation(rT[:, :], bank[2][:, :], ACT.Copy).then_inc(rT_ready, 1)

            def attend(g, first=False, last=False):
                if not first:
                    r_copy(g - 1)
                a_copy(g, 0)
                if not last:
                    sTm_copy(g + 1)
                a_copy(g, 1)
                if not last:
                    q_upper(g + 1, 0)
                    q_upper(g + 1, 1)
                a_copy(g, 2)
                if not last:
                    q_upper(g + 1, 2)
                    q_upper(g + 1, 3)
                a_copy(g, 3)

            root(0)
            sTm_copy(0)
            for n in range(HP):
                q_upper(0, n)
            root(1)
            act.wait_ge(scale_ready, 3)
            act.activation(w1_hi[:, :, :], w1_raw[:, :, :], ACT.Copy, scale=up[:, 1:2]).then_inc(w1_hi_ready, 1)
            act.activation(wr_hi[:, :], wr_raw[:, :], ACT.Copy, scale=up[:, 2:3]).then_inc(w1_hi_ready, 1)
            attend(0, first=True)
            with act.Fori(1, NG - 1) as g:
                attend(g)
            attend(NG - 1, last=True)
            r_copy(NG - 1)

            for k in range(2):
                act.wait_ge(ln3_var, k + 1)
                act.activation(tmp2[:, :], tmp[:, :], ACT.Sqrt).then_inc(ln3_sd, 1)
            with act.Fori(0, NG // 2) as i:
                for u in range(2):
                    g = i * 2 + u
                    act.wait_ge(xt_done, g + 1)
                    act.activation(xT[:, bass.ds(g * GC, GC)], bank[u][:, 0:256].bitcast(F16),
                                   ACT.Copy).then_inc(xT_ready, 1)
            act.wait_ge(r_exp, 1)
            act.activation(ratio[:, :], best[:, :], ACT.Exp).then_inc(exp_done, 1)

            def gT_copy(g, u):
                act.wait_ge(gt_done, g + 1)
                wait(act, w_done, (g - 1) * NX)
                act.activation(gT[:, u, :], bank[7][0:96, 256:512].bitcast(F16), ACT.Copy).then_inc(gT_ready, 1)

            def yT_copy(g, u):
                act.wait_ge(y_part, (g + 1) * NX)
                wait(act, fin_done, g)
                act.activation(yT[:, :], bank[5 + u][:, :], ACT.Copy).then_inc(yT_ready, 1)

            def gelus(g, u, first=False, last=False):
                for e in range(NX):
                    act.wait_ge(hid_done, g * NX + e + 1)
                    if not first:
                        act.wait_ge(hw_ready, (g - 1) * NX + e + 1)
                    act.activation(hid[:, e, :], bank[e % 3][:, :], ACT.Gelu, bias=b1_f[:, e:e + 1],
                                   scale=down[:, 1:2]).then_inc(hid_ready, 1)
                    if first and e == 2:
                        gT_copy(0, 0)
                    if e == 1 and not first:
                        yT_copy(g - 1, 1 - u)
                    if e == 6 and not last:
                        gT_copy(g + 1, 1 - u)

            gelus(0, 0, first=True)
            with act.Fori(0, (NG - 2) // 2) as i:
                for u in (1, 0):
                    gelus(i * 2 + (1 if u else 2), u)
            gelus(NG - 1, 1, last=True)
            yT_copy(NG - 1, 1)

        @block.tensor
        def _(pe):
            pe.wait_ge(w_sum, 1)
            pe.wait_ge(s_ones, 1)
            pe.matmul(bank[0][:, 0:1], ones[0:D, :], w_abs[:, :], start=True, stop=True).then_inc(pe_wabs, 1)
            pe.wait_ge(s_id, 1)
            pe.wait_ge(s_emb, 16 * 7)
            pe.wait_ge(one_ready, 1)
            for c in range(NC):
                pe.transpose(bank[1 + c][0:KW + 1, 0:P], emb[:, c, :], ident[:, :]).then_inc(pe_embT, 1)
            pe.wait_ge(w_ready, 1)
            pe.transpose(bank[5][0:KW, 0:D], w_pos[:, :], ident[0:D, 0:D]).then_inc(pe_embT, 1)
            pe.wait_ge(embT_ready, 5)
            for c in range(NC):
                mm = pe.matmul(bank[6][:, c * D:(c + 1) * D], embT[:, c, :], wT[:, :], start=True, stop=True)
            mm.then_inc(pe_tab, 1)

            def spread_idx(g, first=False):
                for c in range(NC):
                    if not first:
                        if c == 0:
                            pe.wait_ge(hot_ready, (g - 1) * NC + 1)
                        else:
                            pe.wait_ge(copied, (g - 1) * 3 + c)
                    pe.matmul(bank[c][:, :], sel[:, c * P:(c + 1) * P],
                              idx_b[:, g * GC:(g + 1) * GC] if isinstance(g, int) else idx_b[:, bass.ds(g * GC, GC)],
                              start=True, stop=True).then_inc(spread, 1)

            def look_up(g, u):
                pe.wait_ge(hot_ready, (g + 1) * NC)
                wait(pe, z_ready, g - 1)
                for t in range(TG):
                    for c in range(NC):
                        for k in range(3):
                            mm = pe.matmul(bank[4 + u][:, t * D:(t + 1) * D], hot[:, u, c, t * P:(t + 1) * P],
                                           tab[:, c, k, :], start=(c == 0 and k == 0), stop=(c == NC - 1 and k == 2))
                mm.then_inc(z_done, 1)

            pe.wait_ge(idx_ready, 2)
            pe.wait_ge(s_sel, 1)
            spread_idx(0, True)
            spread_idx(1)
            pe.wait_ge(tab_ready, 1)
            look_up(0, 0)
            look_up(1, 1)
            with pe.Fori(1, NG // 2) as i:
                for u in range(2):
                    spread_idx(i * 2 + u)
                    look_up(i * 2 + u, u)

            pe.wait_ge(s_wgt, N_WGT)
            pe.wait_ge(q_ready, 1)
            pe.transpose(bank[7][:, 0:NX], b1_raw[:, :], ident[0:NX, 0:NX])
            for e in range(NX):
                pe.matmul(bank[7][:, NX + e:NX + e + 1], w1_raw[0:D, e, :], fb[0:D, 0:1], start=True, stop=True)
            pe.matmul(bank[7][:, 2 * NX:3 * NX], beta_row[:, :], wr_raw[0:D, :], start=True, stop=False)
            pe.matmul(bank[7][:, 2 * NX:3 * NX], ones[0:1, :], br_raw[:, :], start=False, stop=True)
            for n in range(HP):
                mm = pe.transpose(bank[7][:, 256 + n * D:256 + (n + 1) * D],
                                  e_raw[:, 2 * n:2 * n + 2, :].rearrange("p h d -> p (h d)"), ident[0:D, 0:D])
            mm.then_inc(pe_bias, 1)

            def turn(g):
                pe.wait_ge(s_ready, g + 1)
                wait(pe, back_ready, g - 1)
                wait(pe, sT_ready, 2 * g)
                for dst, k in ((bank[0][:, 0:256], 1), (bank[0][:, 256:512], 0), (bank[1][:, 0:256], 2)):
                    for t in range(TG):
                        mm = pe.transpose(dst[:, t * 64:(t + 1) * 64].bitcast(F16),
                                          s16[:, t, k:k + 2, :].rearrange("p k d -> p (k d)"), ident16[:, :])
                mm.then_inc(t_done, 1)

            def project(g, n):
                pe.wait_ge(sTm_ready, g + 1)
                for k, w in enumerate((q_hi, q_lo)):
                    mm = pe.matmul(bank[3 + Q_BANK[n]][:, :], w[:, n * P:(n + 1) * P], sTm[:, :],
                                   start=(k == 0), stop=(k == 1))
                mm.then_inc(q_done, 1)

            def omega(g, t, first=False):
                if not (first and t == 0):
                    pe.wait_ge(om_ready, g * 2 * TG + [0, 1, 3, 5][t] if not (first and t == 0) else 1)
                if t == 0:
                    pe.wait_ge(sT_ready, 2 * (g + 1))
                    pe.wait_ge(q_used, (g + 1) * HP)
                tt = slice(t * P, (t + 1) * P)
                for k, (sx, qx) in enumerate(((sTh, qh), (sTh, ql), (sTl, qh))):
                    for par in range(2):
                        r = slice(par * D, par * D + D)
                        mm = pe.matmul(bank[5 + OM_BANK[2 * t + par]][:, :], sx[r, tt], qx[r, :, tt],
                                       start=(k == 0), stop=(k == 2))
                mm.then_inc(om_done, 1)

            def weigh(g, u, t):
                pe.wait_ge(om_ready, (g * TG + t + 1) * 2)
                for par in range(2):
                    mm = pe.matmul(bank[3 + A_BANK[t]][par * D:par * D + D, :], s32[:, u, t, :],
                                   om8[:, 2 * t + par, :, :].rearrange("p a t -> p (a t)"), start=True, stop=True)
                mm.then_inc(a_done, 1)

            def mix(g):
                pe.wait_ge(a_ready, (g + 1) * TG)
                wait(pe, rT_ready, g)
                for n in range(HP):
                    o = n % 2 * D
                    mm = pe.matmul(bank[2][o:o + D, :], eT[:, n, :], aT[:, n, :], start=(n < 2), stop=(n >= 2))
                mm.then_inc(r_done, 1)

            def back(g):
                pe.wait_ge(rT_ready, g + 1)
                for t in range(TG):
                    mm = pe.matmul(bank[1][:, 256 + t * D:256 + (t + 1) * D], rT[:, t * P:(t + 1) * P], fold[:, :],
                                   start=True, stop=True)
                mm.then_inc(back_done, 1)

            def attend(g, u, first=False, last=False):
                omega(g, 0, first)
                if not first:
                    mix(g - 1)
                omega(g, 1, first)
                if not first:
                    back(g - 1)
                if not first:
                    pe.wait_ge(a_ready, g * TG)
                weigh(g, u, 0)
                omega(g, 2, first)
                if not last:
                    turn(g + 1)
                weigh(g, u, 1)
                omega(g, 3, first)
                if not last:
                    pe.wait_ge(a_ready, g * TG + 1)
                    project(g + 1, 0)
                    pe.wait_ge(a_ready, g * TG + 2)
                    project(g + 1, 1)
                    pe.wait_ge(q_used, (g + 1) * HP + 1)
                else:
                    pe.wait_ge(a_ready, g * TG + 1)
                weigh(g, u, 2)
                if not last:
                    pe.wait_ge(q_used, (g + 1) * HP + 2)
                    project(g + 1, 2)
                    pe.wait_ge(a_ready, g * TG + 3)
                    project(g + 1, 3)
                    pe.wait_ge(q_used, (g + 1) * HP + 3)
                else:
                    pe.wait_ge(a_ready, g * TG + 2)
                weigh(g, u, 3)

            pe.wait_ge(e_ready, 1)
            turn(0)
            project(0, 0)
            project(0, 1)
            pe.wait_ge(q_used, 2)
            project(0, 2)
            project(0, 3)
            attend(0, 0, first=True)
            with pe.Fori(0, (NG - 2) // 2) as i:
                for u in (1, 0):
                    attend(i * 2 + (1 if u else 2), u)
            attend(NG - 1, 1, last=True)
            mix(NG - 1)
            back(NG - 1)

            pe.wait_ge(w1_ready, 2)
            pe.wait_ge(back_ready, NG)

            def logits(g):
                pe.wait_ge(xT_ready, g + 1)
                for t in range(TG):
                    k = g * TG + t
                    o = bank[2][:, bass.ds(k * NX, NX)]
                    pe.matmul(o, xT[:, bass.ds(k * P, P)], wr_hi[:, :], start=True, stop=False)
                    mm = pe.matmul(o, xT[:, bass.ds(k * P, P)], wr_lo[:, :], start=False, stop=True)
                mm.then_inc(lg_done, 1)

            def turn_x(g, u):
                pe.wait_ge(x_ready, g + 1)
                for t in range(TG):
                    mm = pe.transpose(bank[u][:, t * 64:(t + 1) * 64].bitcast(F16),
                                      x16[:, u, t, :, :].rearrange("p k d -> p (k d)"), ident16[:, :])
                mm.then_inc(xt_done, 1)

            turn_x(0, 0)
            turn_x(1, 1)
            with pe.Fori(1, NG // 2) as i:
                for u in range(2):
                    logits(i * 2 + u - 2)
                    turn_x(i * 2 + u, u)
            logits(NG - 2)
            logits(NG - 1)

            def hidden(g, e):
                wait(pe, hid_ready, g * NX + [-1, 0, -2, 1, 2, 3, 4, 5][e])
                rhs = xT[:, g * GC:(g + 1) * GC] if isinstance(g, int) else xT[:, bass.ds(g * GC, GC)]
                for k, w in enumerate((w1_hi, w1_lo)):
                    mm = pe.matmul(bank[e % 3][:, :], w[:, e, :], rhs, start=(k == 0), stop=(k == 1))
                mm.then_inc(hid_done, 1)

            def turn_gate(g):
                wait(pe, res_ready, g - 1)
                for t in range(TG):
                    src = gate16[:, bass.ds(g * TG + t, 1), :, :, :].rearrange("p a x y e -> p (a x y e)")
                    mm = pe.transpose(bank[7][0:96, 256 + t * 64:256 + (t + 1) * 64].bitcast(F16), src, ident16[:, :])
                mm.then_inc(gt_done, 1)

            def spread_gate(g, u, e):
                if e == 0:
                    pe.wait_ge(gT_ready, g + 1)
                wait(pe, hw_ready, g * NX + e - 1)
                pe.matmul(bank[3 + e % 2][:, :], sel_w[:, e, :], gT[:, u, :], start=True, stop=True).then_inc(w_done, 1)

            def outer(g, u, e):
                pe.wait_ge(hw_ready, g * NX + e + 1)
                o = e % 2 * D
                if e == 0:
                    wait(pe, yT_ready, g - 1)
                    pe.matmul(bank[5 + u][0:D, :], b2_p[:, :], gT[:, u, :], start=True, stop=False)
                mm = pe.matmul(bank[5 + u][o:o + D, :], w2[:, e, :], hw[:, e, :], start=(e == 1), stop=(e >= NX - 2))
                mm.then_inc(y_part, 1)

            def finish(g):
                pe.wait_ge(yT_ready, g + 1)
                for t in range(TG):
                    mm = pe.matmul(bank[7][:, t * D:(t + 1) * D], yT[:, t * P:(t + 1) * P], fold[:, :],
                                   start=True, stop=True)
                mm.then_inc(fin_done, 1)

            def experts(g, u, first=False, last=False):
                for e in range(NX):
                    hidden(g, e)
                    if first and e < 2:
                        continue
                    if first and e == 2:
                        pe.wait_ge(gate_ready, 3)
                        turn_gate(0)
                        for n in range(2):
                            spread_gate(g, u, n)
                    spread_gate(g, u, e)
                    if e >= 2:
                        outer(g, u, e - 2)
                    elif not first:
                        outer(g - 1, 1 - u, NX - 2 + e)
                    if e == 4 and not first:
                        finish(g - 1)
                    if e == 6 and not last:
                        turn_gate(g + 1)

            pe.wait_ge(b2_ready, 3)
            pe.wait_ge(gate_zero, 1)
            pe.wait_ge(lg_read, 1)
            experts(0, 0, first=True)
            with pe.Fori(0, (NG - 2) // 2) as i:
                for u in (1, 0):
                    experts(i * 2 + (1 if u else 2), u)
            experts(NG - 1, 1, last=True)
            outer(NG - 1, 1, NX - 2)
            outer(NG - 1, 1, NX - 1)
            finish(NG - 1)


_INS = ['x', 'itok_BS_0_255', 'itok_BS_0_511', 'itok_BS_0_127', 'itok_BS_0_63', 'itok_BS_0_3',
        'L0_tok_E_et', 'L0_tok_E_fc', 'L0_tok_E_sc', 'L0_tok_E_of', 'L0_tok_E_tt', 'L0_tok_E_rc',
        'L0_tok_W', 'L0_tok_b', 'L0_tok_gamma', 'L0_tok_beta', 'L0_attn_Q', 'L0_attn_E',
        'L0_ffn_gamma', 'L0_ffn_beta', 'L0_ffn_Wr', 'L0_ffn_br', 'L0_ffn_W1', 'L0_ffn_b1', 'L0_ffn_W2', 'L0_ffn_b2']


def kernel(**inputs):
    import numpy as _np
    import concourse.bacc as _bacc
    from concourse import mybir as _mybir
    from concourse.bass_utils import run_bass_kernel_spmd as _run

    nc = _bacc.Bacc("TRN2", target_bir_lowering=False, num_devices=1)
    arrays, args = {}, []
    for name in _INS:
        a = _np.ascontiguousarray(inputs[name])
        arrays[f"in_{name}_dram"] = a
        args.append(nc.dram_tensor(f"in_{name}_dram", a.shape, _mybir.dt.from_np(a.dtype), kind="ExternalInput").ap())
    B, S = inputs['x'].shape
    D = inputs['L0_tok_W'].shape[0]
    out = nc.dram_tensor("out_dram", (B, S, D), _mybir.dt.float32, kind="ExternalOutput").ap()
    lm_tower(nc, args[0:6], args[6:12], *args[12:], out)
    r = _run(nc, [arrays], core_ids=[0])
    return r.results[0]["out_dram"]
```

```python
from contextlib import ExitStack

import concourse.bass as bass
from concourse import mybir

P = 128
ALU = mybir.AluOpType
ACT = mybir.ActivationFunctionType
AX = mybir.AxisListType
F32 = mybir.dt.float32
F16 = mybir.dt.float16
BF16 = mybir.dt.bfloat16
I32 = mybir.dt.int32
RMAX = bass.bass_isa.ReduceOp.max


class Steps:

    def __init__(self, eng, sem, base=0, per_iteration=None):
        self.eng, self.sem, self.base, self.n, self.per = eng, sem, base, 0, per_iteration

    def done(self, instruction):
        instruction.then_inc(self.sem, 1)
        self.n += 1

    def settle(self):
        self.eng.wait_ge(self.sem, self.base + self.n)

    def close(self):
        assert self.per is None or self.n == self.per, (self.n, self.per)


def lm_tower(nc, idx, tables, W, b, gamma, beta, Q, E, fgamma, fbeta, Wr, br, W1, b1, W2, b2, out):
    B, S = idx[0].shape
    N = B * S
    NT = N // P
    TG = 4
    NG = NT // TG
    GC = TG * P
    D, KW = W.shape
    EMB = KW // len(tables)
    H = Q.shape[0]
    NX, _, FH = W1.shape
    HP = H // 2
    NC = 4
    EPS = 1e-5
    LIFT = (16.0, 1024.0, 1024.0)
    assert S == P and D == 64 and FH == P and H * D == 512 and NX * D == 512

    place = [(0, 0), (0, 64), (1, 0), (2, 0), (3, 0), (3, 64)]
    half_row = [0, 1, 2, 2, 3, 3, 4, 5]

    with ExitStack() as ctx:
        def sb(name, shape, dt=F32):
            return ctx.enter_context(nc.sbuf_tensor(name, shape, dt))

        def sem(name):
            return ctx.enter_context(nc.semaphore(name))

        bank = [ctx.enter_context(nc.psum_tensor(f"bank{i}", [P, 512], F32)) for i in range(8)]

        ident = sb("ident", [P, P])
        ident16 = sb("ident16", [P, P], F16)
        fold = sb("fold", [P, D])
        causal = sb("causal", [P, P])
        causal_q = sb("causal_q", [P, P])
        ones = sb("ones", [P, P])
        sel = sb("sel", [96, NC * P], BF16)
        row_i = sb("row_i", [P, NC], I32)
        row_id = sb("row_id", [P, NC])
        rank = sb("rank", [P, NX])
        rank_i = sb("rank_i", [P, NX], I32)
        sel_w = sb("sel_w", [96, NX, P], F16)
        hid = sb("hid", [P, NX, GC])
        idx_i = hid[0:6, :, :].rearrange("p e t -> p (e t)").bitcast(I32)
        idx_b = sb("idx_b", [96, N], BF16)
        emb = sb("emb", [P, NC, KW + 1])
        embT = sb("embT", [KW + 1, NC, P])
        w_raw = sb("w_raw", [D, KW])
        w_abs = sb("w_abs", [D, 1])
        w_s = sb("w_s", [P, 4])
        w_pos = sb("w_pos", [D, KW])
        w_neg = sb("w_neg", [D, KW])
        wT = sb("wT", [KW + 1, D])
        tab_f = sb("tab_f", [P, NC, D])
        tab = sb("tab", [P, NC, 3, D], BF16)
        gam = sb("gam", [P, D])
        bet = sb("bet", [P, D])
        q_raw = sb("q_raw", [P, H, D])
        e_raw = sb("e_raw", [D, H, D])
        w1_raw = sb("w1_raw", [P, NX, FH])
        wr_raw = sb("wr_raw", [P, NX])
        fg = sb("fg", [P, 1])
        fb = sb("fb", [P, 1])
        b1_raw = sb("b1_raw", [NX, FH])
        br_raw = sb("br_raw", [1, NX])
        b2_raw = sb("b2_raw", [96, D])
        b2_h = sb("b2_h", [96, D], BF16)
        b2_m = sb("b2_m", [96, D], BF16)
        b2_p = sb("b2_p", [96, D], BF16)
        w2 = sb("w2", [FH, NX, D])
        peak = sb("peak", [P, 3])
        peak_all = sb("peak_all", [P, 3])
        pow2 = sb("pow2", [P, 3])
        up = sb("up", [P, 3])
        down = sb("down", [P, 3])
        q_hi = sb("q_hi", [P, H * D], F16)
        q_lo = sb("q_lo", [P, H * D], F16)
        eT = sb("eT", [P, HP, D])
        w1_hi = sb("w1_hi", [P, NX, FH], F16)
        w1_lo = sb("w1_lo", [P, NX, FH], F16)
        wr_hi = sb("wr_hi", [P, NX], F16)
        wr_lo = sb("wr_lo", [P, NX], F16)
        b1_f = sb("b1_f", [FH, NX])
        br_f = sb("br_f", [P, NX])
        beta_row = sb("beta_row", [D, P])
        z = sb("z", [P, NT, D])
        h = sb("h", [P, NT, D])
        stats = sb("stats", [P, NT, 6])
        hstats = sb("hstats", [P, NT, 6])
        mean1 = sb("mean1", [P, NT])
        rstd1 = sb("rstd1", [P, NT])
        mean = sb("mean", [P, NT])
        var = sb("var", [P, NT])
        rstd = sb("rstd", [P, NT])
        sd = sb("sd", [P, NT])
        mean3 = sb("mean3", [P, NT])
        rstd3 = sb("rstd3", [P, NT])
        tmp = sb("tmp", [P, NT])
        tmp2 = sb("tmp2", [P, NT])
        diff = sb("diff", [P, TG])
        hn = sb("hn", [P, TG, D])
        xT = sb("xT", [P, N], F16)
        hot = sb("hot", [P, 2, NC, GC], BF16)
        idx_c = sb("idx_c", [P, 2, NC, GC], BF16)
        s32 = sb("s32", [P, 2, TG, D])
        sn = sb("sn", [P, TG, D])
        s16 = sb("s16", [P, TG, 4, D], F16)
        sTm = sb("sTm", [P, 2, GC], F16)
        sTh = sb("sTh", [P, 2, GC], F16)
        sTl = sb("sTl", [P, 2, GC], F16)
        qh = sb("qh", [P, 2, HP, GC], F16)
        ql = sb("ql", [P, 2, HP, GC], F16)
        om8 = sb("om8", [P, 2 * TG, HP, P])
        aT = sb("aT", [P, HP, GC])
        rT = sb("rT", [P, GC])
        x32 = sb("x32", [P, 2, TG, D])
        x16 = sb("x16", [P, 2, TG, 2, D], F16)
        hw = sb("hw", [P, NX, GC])
        gT = sb("gT", [96, 2, GC], F16)
        yT = sb("yT", [P, GC])
        res = sb("res", [P, NT, D])
        lg = sb("lg", [P, NT, NX])
        lg2 = sb("lg2", [P, NT, NX])
        pick = sb("pick", [P, NT, NX])
        sel1 = sb("sel1", [P, NT, NX])
        sel2 = sb("sel2", [P, NT, NX])
        gate = sb("gate", [P, NT, NX])
        gate16 = sb("gate16", [P, NT, 3, 4, NX], F16)
        top1 = sb("top1", [P, NT])
        top2 = sb("top2", [P, NT])
        best = sb("best", [P, NT])
        ratio = sb("ratio", [P, NT])
        wt1 = sb("wt1", [P, NT])
        wt2 = sb("wt2", [P, NT])

        s_idx = sem("s_idx"); s_w = sem("s_w"); s_emb = sem("s_emb"); s_wgt = sem("s_wgt")
        s_gam = sem("s_gam"); s_b2 = sem("s_b2"); s_out = sem("s_out")
        s_ones = sem("s_ones"); s_pool = sem("s_pool"); pool_step = sem("pool_step")
        s_sel = sem("s_sel"); s_id = sem("s_id"); s_amax = sem("s_amax"); pool_h = sem("pool_h")
        emb_zero = sem("emb_zero"); b2_zero = sem("b2_zero"); dve_setup = sem("dve_setup")
        pe_wabs = sem("pe_wabs"); w_sum = sem("w_sum"); w_ready = sem("w_ready")
        pe_embT = sem("pe_embT"); embT_ready = sem("embT_ready"); pe_tab = sem("pe_tab")
        tab_ready = sem("tab_ready"); idx_zero = sem("idx_zero"); idx_ready = sem("idx_ready")
        pe_eT = sem("pe_eT"); e_ready = sem("e_ready"); s_peak = sem("s_peak")
        q_ready = sem("q_ready"); beta_ready = sem("beta_ready"); pe_bias = sem("pe_bias")
        w1_ready = sem("w1_ready"); one_ready = sem("one_ready"); w1_scaled = sem("w1_scaled"); b2_ready = sem("b2_ready"); scale_ready = sem("scale_ready")
        q_hi_ready = sem("q_hi_ready"); w1_hi_ready = sem("w1_hi_ready"); bias_read = sem("bias_read")
        spread = sem("spread"); copied = sem("copied"); hot_ready = sem("hot_ready")
        z_done = sem("z_done"); z_ready = sem("z_ready"); z_stats = sem("z_stats")
        batch_var = sem("batch_var"); batch_sd = sem("batch_sd"); sd_ready = sem("sd_ready")
        ln1_ready = sem("ln1_ready"); h_ready = sem("h_ready"); h_stats = sem("h_stats")
        var_ready = sem("var_ready"); rstd_ready = sem("rstd_ready"); sn_ready = sem("sn_ready")
        s_hi_ready = sem("s_hi_ready"); s32_ready = sem("s32_ready"); pool_ln = sem("pool_ln")
        dve_ln = sem("dve_ln"); sn_step = sem("sn_step")
        dve_s = sem("dve_s"); s_ready = sem("s_ready"); t_done = sem("t_done")
        sTm_ready = sem("sTm_ready"); sT_ready = sem("sT_ready")
        q_done = sem("q_done"); qh_ready = sem("qh_ready"); q_used = sem("q_used")
        om_done = sem("om_done"); om_ready = sem("om_ready")
        a_done = sem("a_done"); a_ready = sem("a_ready")
        r_done = sem("r_done"); rT_ready = sem("rT_ready"); back_done = sem("back_done")
        back_ready = sem("back_ready"); h2_stats = sem("h2_stats")
        ln3_var = sem("ln3_var"); ln3_sd = sem("ln3_sd"); x_ready = sem("x_ready")
        xt_done = sem("xt_done"); xT_ready = sem("xT_ready"); lg_done = sem("lg_done")
        lg_read = sem("lg_read"); r_exp = sem("r_exp"); exp_done = sem("exp_done")
        dve_ln3 = sem("dve_ln3"); dve_gate = sem("dve_gate"); gate_zero = sem("gate_zero")
        gate_ready = sem("gate_ready"); gt_done = sem("gt_done"); gT_ready = sem("gT_ready")
        hid_done = sem("hid_done"); hid_ready = sem("hid_ready"); w_done = sem("w_done")
        hw_ready = sem("hw_ready"); y_part = sem("y_part"); y_done = sem("y_done")
        yT_ready = sem("yT_ready"); fin_done = sem("fin_done"); res_ready = sem("res_ready")

        block = ctx.enter_context(nc.Block())

        N_WGT = 16 * 13
        OM_BANK = [0, 1, 2, 0, 1, 2, 0, 1]

        def q_bank(g, n):
            return bank[3 + n] if isinstance(g, int) and g == 0 else bank[4]

        def tiles(g):
            return bass.ds(g * TG, TG)

        def wait(eng, s, value):
            if not isinstance(value, int) or value > 0:
                eng.wait_ge(s, value)

        @block.sync
        def _(sp):
            for n, a in enumerate(idx):
                sp.dma_start(idx_i[n:n + 1, :], a.rearrange("(a b) s -> a (b s)", a=1)).then_inc(s_idx, 16)
            sp.wait_ge(emb_zero, 1)
            for n, (t, (c, r)) in enumerate(zip(tables, place)):
                v = t.shape[0]
                sp.dma_start(emb[r:r + v, c, n * EMB:(n + 1) * EMB], t).then_inc(s_emb, 16)
            sp.dma_start(gam[:, :], gamma.rearrange("(a n) -> a n", a=1).broadcast_to([P, D])).then_inc(s_gam, 16)
            sp.dma_start(bet[:, :], beta.rearrange("(a n) -> a n", a=1).broadcast_to([P, D])).then_inc(s_gam, 16)
            sp.dma_start(q_raw[0:D, :, :], Q.rearrange("h i j -> i h j")).then_inc(s_wgt, 16)
            sp.dma_start(q_raw[D:P, :, :], Q.rearrange("h i j -> i h j")).then_inc(s_wgt, 16)
            sp.dma_start(e_raw[:, :, :], E.rearrange("h i j -> i h j")).then_inc(s_wgt, 16)
            for a in range(2):
                sp.dma_start(w1_raw[a * D:a * D + D, :, :], W1.rearrange("e d f -> d e f")).then_inc(s_wgt, 16)
                sp.dma_start(wr_raw[a * D:a * D + D, :], Wr).then_inc(s_wgt, 16)
                sp.dma_start(fg[a * D:a * D + D, :], fgamma.rearrange("(d a) -> d a", a=1)).then_inc(s_wgt, 16)
            sp.dma_start(fb[0:D, :], fbeta.rearrange("(d a) -> d a", a=1)).then_inc(s_wgt, 16)
            sp.dma_start(b1_raw[:, :], b1).then_inc(s_wgt, 16)
            sp.dma_start(br_raw[:, :], br.rearrange("(a n) -> a n", a=1)).then_inc(s_wgt, 16)
            sp.dma_start(w2[:, :, :], W2.rearrange("e f d -> f e d")).then_inc(s_wgt, 16)
            sp.wait_ge(b2_zero, 1)
            for k in (0, 8, 32, 40, 64, 72):
                sp.dma_start(b2_raw[k:k + NX, :], b2).then_inc(s_b2, 16)
            out_v = out.rearrange("(g t) p d -> p g t d", t=TG)
            res_v = res[:, :, :].rearrange("p (g t) d -> p g t d", t=TG)
            with sp.Fori(0, NG) as g:
                sp.wait_ge(res_ready, g + 1)
                sp.dma_start(out_v[:, bass.ds(g, 1), :, :].rearrange("p g t d -> p (g t) d"),
                             res_v[:, bass.ds(g, 1), :, :].rearrange("p g t d -> p (g t) d")).then_inc(s_out, 16)
            sp.wait_ge(s_out, 16 * NG)

        @block.gpsimd
        def _(pool):
            st = Steps(pool, pool_step)

            def link(ins):
                st.done(ins)
                st.settle()

            def select(a, pattern, base, slope, compare=ALU.not_equal, fill=1.0):
                link(pool.affine_select(out=a, in_=a, compare_op=compare, fill=fill, base=base, pattern=pattern,
                                        channel_multiplier=slope))

            pool.memset(emb[:, :, :], 0.0).then_inc(emb_zero, 1)
            link(pool.memset(ones[:, :], 1.0))
            pool.sem_inc(s_ones, 1)
            link(pool.memset(ident[:, :], 0.0))
            select(ident[:, :], [[-1, P]], 0, 1)
            pool.sem_inc(s_id, 1)
            link(pool.iota(row_i[:, :], pattern=[[0, NC]], base=0, channel_multiplier=1))
            for c in (0, 3):
                link(pool.iota(row_i[64:P, c:c + 1], pattern=[[0, 1]], base=0, channel_multiplier=1))
            link(pool.memset(sel[:, :], 0.0))
            for k, r in enumerate(half_row):
                select(sel[:, k * 64:(k + 1) * 64], [[0, 64]], -r, 1)
            pool.sem_inc(s_sel, 1)
            link(pool.tensor_copy(ident16[:, :], ident[:, :]))
            pool.memset(b2_raw[:, :], 0.0).then_inc(b2_zero, 1)
            link(pool.memset(fold[:, :], 0.0))
            select(fold[:, :], [[-1, D]], 0, 1)
            select(fold[:, :], [[-1, D]], -D, 1)
            link(pool.memset(causal[:, :], 1.0))
            select(causal[:, :], [[1, P]], 0, -1, ALU.is_ge, 0.0)
            link(pool.iota(rank_i[:, :], pattern=[[-1, NX]], base=NX, channel_multiplier=0))
            pool.sem_inc(s_pool, 1)
            pool.wait_ge(s_peak, 1)
            pool.partition_all_reduce(peak_all[:, 0:1], peak[:, 0:1], P, RMAX).then_inc(s_amax, 1)
            pool.wait_ge(s_gam, 32)
            LN1, LN2 = 3, 7

            def over(a, g):
                return a[:, g * TG:(g + 1) * TG].unsqueeze(2).broadcast_to([P, TG, D])

            def embed_norm(g):
                lc = Steps(pool, pool_h, (g - 1) * LN1, LN1)
                wait(pool, h_ready, g - 1)
                lc.done(pool.tensor_tensor(hn[:, :, :], z[:, g * TG:(g + 1) * TG, :], over(mean1, g), ALU.subtract))
                lc.settle()
                lc.done(pool.tensor_tensor(hn[:, :, :], hn[:, :, :], over(rstd1, g), ALU.mult))
                lc.settle()
                lc.done(pool.tensor_tensor(hn[:, :, :], hn[:, :, :], gam[:, :].unsqueeze(1).broadcast_to([P, TG, D]),
                                           ALU.mult))
                lc.settle()
                lc.close()
                pool.tensor_tensor(h[:, g * TG:(g + 1) * TG, :], hn[:, :, :], bet[:, :].unsqueeze(1).broadcast_to([P, TG, D]),
                                   ALU.add).then_inc(h_ready, 1)

            def h_variance(g):
                lc = Steps(pool, pool_ln, (g - 2) * LN2, LN2)

                def f(k):
                    return hstats[:, g * TG:(g + 1) * TG, k]
                pool.wait_ge(h_stats, (g + 1) * TG)
                wait(pool, var_ready, g - 2)
                lc.done(pool.tensor_tensor(mean[:, g * TG:(g + 1) * TG], f(1), f(4), ALU.add))
                lc.settle()
                lc.done(pool.tensor_tensor(diff[:, :], f(1), f(4), ALU.subtract))
                lc.settle()
                lc.done(pool.tensor_tensor(var[:, g * TG:(g + 1) * TG], f(2), f(5), ALU.add))
                lc.settle()
                lc.done(pool.tensor_scalar(mean[:, g * TG:(g + 1) * TG], mean[:, g * TG:(g + 1) * TG], 0.5, None, ALU.mult))
                lc.settle()
                lc.done(pool.tensor_tensor(diff[:, :], diff[:, :], diff[:, :], ALU.mult))
                lc.settle()
                lc.done(pool.tensor_scalar(diff[:, :], diff[:, :], 0.25, None, ALU.mult))
                lc.settle()
                lc.done(pool.tensor_scalar(var[:, g * TG:(g + 1) * TG], var[:, g * TG:(g + 1) * TG], 1.0 / D, EPS, ALU.mult, ALU.add))
                lc.settle()
                lc.close()
                pool.tensor_tensor(var[:, g * TG:(g + 1) * TG], var[:, g * TG:(g + 1) * TG], diff[:, :], ALU.add).then_inc(var_ready, 1)

            def normal(g):
                pool.wait_ge(rstd_ready, g - 1)
                wait(pool, s_ready, g)
                wait(pool, s32_ready, g - 2)
                pool.tensor_tensor(sn[:, :, :], h[:, g * TG:(g + 1) * TG, :], over(mean, g), ALU.subtract).then_inc(sn_step, 1)
                pool.wait_ge(sn_step, g - 1)
                pool.tensor_tensor(sn[:, :, :], sn[:, :, :], over(rstd, g), ALU.mult).then_inc(sn_ready, 1)

            def keep(g, u):
                pool.wait_ge(sn_ready, g - 1)
                pool.wait_ge(a_done, (g - 1) * TG)
                pool.tensor_copy(s32[:, u, :, :], sn[:, :, :]).then_inc(s32_ready, 1)

            pool.wait_ge(ln1_ready, 1)
            embed_norm(1)
            embed_norm(2)
            h_variance(2)
            link(pool.memset(sel_w[:, :, :], 0.0))
            for k in (0, NX):
                select(sel_w[:, :, :], [[-1, NX], [0, P]], -k, 1)
            pool.sem_inc(gate_zero, 1)
            pool.memset(gate16[:, :, :, :, :], 0.0).then_inc(gate_zero, 1)
            pool.wait_ge(gate_zero, 2)
            for g in range(NG - 1):
                if g >= 1:
                    keep(g + 1, (g + 1) % 2)
                if g + 2 < NG:
                    normal(g + 2)
                if g == 1:
                    pool.wait_ge(ln1_ready, 2)
                if g + 3 < NG:
                    embed_norm(g + 3)
                    h_variance(g + 3)
            pool.wait_ge(s_peak, 3)
            pool.partition_all_reduce(peak_all[:, 1:3], peak[:, 1:3], P, RMAX).then_inc(s_amax, 1)

        @block.vector
        def _(dve):
            st = Steps(dve, dve_setup)

            def link(ins):
                st.done(ins)
                st.settle()

            def row(a):
                return a.rearrange("p a d -> p (a d)")

            dve.memset(idx_b[:, :].bitcast(I32), 0).then_inc(idx_zero, 1)
            dve.wait_ge(emb_zero, 1)
            dve.memset(emb[64:68, 3, KW:KW + 1], 1.0).then_inc(one_ready, 1)
            dve.wait_ge(s_w, 16)
            dve.tensor_reduce(w_abs[:, :], w_raw[:, :], AX.X, ALU.add, apply_absolute_value=True).then_inc(w_sum, 1)
            dve.wait_ge(s_idx, 96)
            dve.wait_ge(idx_zero, 1)
            dve.tensor_copy(idx_b[0:6, 0:N // 2], idx_i[:, 0:N // 2]).then_inc(idx_ready, 1)
            dve.wait_ge(pe_wabs, 1)
            link(dve.tensor_scalar(w_s[:, 0:1], bank[0][:, 0:1], 1.0 / (D * KW), None, ALU.mult))
            st.done(dve.tensor_scalar(w_s[:, 1:2], w_s[:, 0:1], 1e-8, 0.5, ALU.add, ALU.mult))
            link(dve.tensor_scalar(w_s[:, 2:3], w_s[:, 0:1], 1e-8, -0.5, ALU.add, ALU.mult))
            st.done(dve.tensor_scalar(w_pos[:, :], w_raw[:, :], w_s[0:D, 1:2], None, ALU.is_gt))
            link(dve.tensor_scalar(w_neg[:, :], w_raw[:, :], w_s[0:D, 2:3], None, ALU.is_lt))
            link(dve.tensor_tensor(w_pos[:, :], w_pos[:, :], w_neg[:, :], ALU.subtract))
            link(dve.scalar_tensor_tensor(out=w_pos[:, :], in0=w_pos[:, :], scalar=w_s[0:D, 0:1], in1=w_raw[:, :],
                                          op0=ALU.mult, op1=ALU.subtract))
            dve.tensor_tensor(w_pos[:, :], w_pos[:, :], w_raw[:, :], ALU.add).then_inc(w_ready, 1)
            dve.wait_ge(pe_embT, 5)
            dve.tensor_copy(wT[0:KW, :], bank[5][0:KW, 0:D]).then_inc(embT_ready, 1)
            dve.wait_ge(s_sel, 1)
            link(dve.tensor_copy(row_id[:, :], row_i[:, :]))
            dve.wait_ge(pe_tab, 1)
            link(dve.tensor_copy(tab_f[:, :, :], bank[6][:, 0:NC * D].rearrange("p (c d) -> p c d", d=D)))
            for k in range(3):
                part = dve.tensor_copy(tab[:, :, k, :], tab_f[:, :, :])
                if k == 2:
                    part.then_inc(tab_ready, 1)
                    break
                link(part)
                link(dve.tensor_tensor(tab_f[:, :, :], tab_f[:, :, :], tab[:, :, k, :], ALU.subtract))

            def one_hot(g, u):
                for c in range(NC):
                    if c == 0:
                        dve.wait_ge(spread, g * NC + 1)
                        src = bank[0][:, :]
                    else:
                        dve.wait_ge(copied, g * 3 + c)
                        src = idx_c[:, u, c, :]
                    dve.tensor_scalar(hot[:, u, c, :], src, row_id[:, c:c + 1], None, ALU.is_equal).then_inc(hot_ready, 1)

            def z_moments(g):
                dve.wait_ge(z_ready, g + 1)
                for t in range(TG):
                    tt = bass.ds(g * TG + t, 1)
                    dve.bn_stats(row(stats[:, tt, :]), row(z[:, tt, :])).then_inc(z_stats, 1)

            def scales(x, y):
                link(dve.tensor_scalar(peak_all[:, x:y], peak_all[:, x:y], 1e-30, None, ALU.max))
                link(dve.tensor_scalar(pow2[:, x:y].bitcast(I32), peak_all[:, x:y].bitcast(I32), 0x7F800000, None,
                                       ALU.bitwise_and))
                link(dve.reciprocal(up[:, x:y], pow2[:, x:y]))
                for k in range(x, y):
                    dve.tensor_scalar(up[:, k:k + 1], up[:, k:k + 1], LIFT[k], None, ALU.mult).then_inc(scale_ready, 1)
                    st.done(dve.tensor_scalar(down[:, k:k + 1], pow2[:, k:k + 1], 1.0 / LIFT[k], None, ALU.mult))
                st.settle()

            one_hot(0, 0)
            one_hot(1, 1)
            dve.wait_ge(s_wgt, N_WGT)
            dve.tensor_reduce(peak[:, 0:1], q_raw[:, :, :], AX.XY, ALU.max, apply_absolute_value=True).then_inc(s_peak, 1)
            link(dve.tensor_copy(beta_row[:, :], fb[0:D, 0:1].broadcast_to([D, P])))
            dve.wait_ge(s_amax, 1)
            scales(0, 1)
            dve.wait_ge(q_hi_ready, 1)
            dve.scalar_tensor_tensor(out=q_lo[:, :], in0=q_raw[:, :, :].rearrange("p h j -> p (h j)"),
                                     scalar=up[:, 0:1], in1=q_hi[:, :], op0=ALU.mult,
                                     op1=ALU.subtract).then_inc(q_ready, 1)
            dve.wait_ge(s_pool, 1)
            link(dve.tensor_scalar(causal_q[:, :], causal[:, :], down[:, 0:1], None, ALU.mult))
            with dve.Fori(1, NG // 2 - 1) as i:
                for u in range(2):
                    dve.wait_ge(z_done, i * 2 + u - 1)
                    one_hot(i * 2 + u, u)
                    z_moments(i * 2 + u - 2)

            ch = Steps(dve, dve_ln)

            def moments(stats, mean, a, b):
                def f(k):
                    return stats[:, a:b, k]
                ch.done(dve.tensor_tensor(mean[:, a:b], f(1), f(4), ALU.add))
                ch.done(dve.tensor_tensor(tmp[:, a:b], f(1), f(4), ALU.subtract))
                ch.done(dve.tensor_tensor(var[:, a:b], f(2), f(5), ALU.add))
                ch.settle()
                ch.done(dve.tensor_scalar(mean[:, a:b], mean[:, a:b], 0.5, None, ALU.mult))
                ch.done(dve.scalar_tensor_tensor(out=tmp[:, a:b], in0=tmp[:, a:b], scalar=0.25, in1=tmp[:, a:b],
                                                 op0=ALU.mult, op1=ALU.mult))
                ch.settle()
                ch.done(dve.scalar_tensor_tensor(out=var[:, a:b], in0=var[:, a:b], scalar=1.0 / D, in1=tmp[:, a:b],
                                                 op0=ALU.mult, op1=ALU.add))
                ch.settle()

            def over(a, x, y):
                return a[:, x:y].unsqueeze(2).broadcast_to([P, y - x, D])

            def add_eps(x, y):
                dve.tensor_scalar(tmp[:, x:y], var[:, x:y], EPS, None, ALU.add).then_inc(batch_var, 1)

            def embed_scalars(x, y, root, n):
                dve.wait_ge(batch_sd, root)
                dve.reciprocal(rstd1[:, x:y], tmp2[:, x:y]).then_inc(ln1_ready, 1)
                dve.wait_ge(ln1_ready, n)

            def h_moments(g):
                wait(dve, h_ready, g)
                for t in range(TG):
                    tt = bass.ds(g * TG + t, 1)
                    dve.bn_stats(row(hstats[:, tt, :]), row(h[:, tt, :])).then_inc(h_stats, 1)

            def first_moments(g):
                x, y = g * TG, (g + 1) * TG
                h_moments(g)
                dve.wait_ge(h_stats, y)
                moments(hstats, mean, x, y)
                add_eps(x, y)

            def first_normal(g, root):
                x, y = g * TG, (g + 1) * TG
                dve.wait_ge(batch_sd, root)
                ch.done(dve.reciprocal(rstd[:, x:y], tmp2[:, x:y]))
                ch.done(dve.tensor_tensor(s32[:, g, :, :], h[:, x:y, :], over(mean, x, y), ALU.subtract))
                ch.settle()
                ch.done(dve.tensor_tensor(s32[:, g, :, :], s32[:, g, :, :], over(rstd, x, y), ALU.mult))
                ch.settle()
                twice = s32[:, g, :, :].unsqueeze(2).broadcast_to([P, TG, 2, D])
                wait(dve, t_done, g)
                ch.done(dve.tensor_copy(s16[:, :, 0:2, :], twice))
                ch.settle()
                dve.tensor_tensor(s16[:, :, 2:4, :], twice, s16[:, :, 0:2, :], ALU.subtract).then_inc(s_ready, 1)

            NA = (NG - 4) * TG
            dve.wait_ge(z_done, NG - 3)
            one_hot(NG - 2, 0)
            dve.wait_ge(z_stats, NA)
            moments(stats, mean1, 0, NA)
            add_eps(0, NA)
            z_moments(NG - 4)
            embed_scalars(0, NA, 1, 1)
            dve.wait_ge(s_gam, 32)
            dve.wait_ge(z_done, NG - 2)
            one_hot(NG - 1, 1)
            z0, h0 = z[:, 0:TG, :], h[:, 0:TG, :]
            ch.done(dve.tensor_tensor(z0, z0, over(mean1, 0, TG), ALU.subtract))
            ch.settle()
            ch.done(dve.tensor_tensor(z0, z0, over(rstd1, 0, TG), ALU.mult))
            ch.settle()
            ch.done(dve.tensor_tensor(z0, z0, gam[:, :].unsqueeze(1).broadcast_to([P, TG, D]), ALU.mult))
            ch.settle()
            ch.done(dve.tensor_tensor(h0, z0, bet[:, :].unsqueeze(1).broadcast_to([P, TG, D]), ALU.add))
            ch.settle()
            first_moments(0)
            z_moments(NG - 3)
            first_normal(0, 2)
            dve.wait_ge(pe_bias, 1)
            link(dve.tensor_copy(b1_f[:, :], bank[7][:, 0:NX]))
            st.done(dve.tensor_tensor(b1_f[:, :], b1_f[:, :], bank[7][:, NX:2 * NX], ALU.add))
            st.done(dve.tensor_copy(br_f[:, :], bank[7][:, 2 * NX:3 * NX]))
            dve.tensor_copy(eT[:, :, :], bank[7][:, 256:256 + HP * D].rearrange("p (a d) -> p a d", d=D)).then_inc(e_ready, 1)
            z_moments(NG - 2)
            z_moments(NG - 1)
            dve.wait_ge(z_stats, NT)
            moments(stats, mean1, NA, NT)
            add_eps(NA, NT)
            first_moments(1)
            embed_scalars(NA, NT, 3, 2)

            def mask(g, t):
                wait(dve, a_done, (g - 1) * TG + t + 1)
                dve.wait_ge(om_done, g * TG + t + 1)
                for n in (2 * t, 2 * t + 1):
                    dve.tensor_tensor(om8[:, n, :, :], bank[5 + OM_BANK[n]][:, :].rearrange("p (h t) -> p h t", t=P),
                                      causal_q[:, :].unsqueeze(1).broadcast_to([P, HP, P]), ALU.mult).then_inc(om_ready, 1)

            def back(g):
                dve.wait_ge(back_done, g + 1)
                dve.tensor_tensor(h[:, tiles(g), :], h[:, tiles(g), :],
                                  bank[1][:, 256:512].rearrange("p (t d) -> p t d", d=D), ALU.add).then_inc(back_ready, 1)

            def sum_stats(g):
                dve.wait_ge(back_ready, g + 1)
                for t in range(TG):
                    tt = bass.ds(g * TG + t, 1)
                    dve.bn_stats(row(stats[:, tt, :]), row(h[:, tt, :])).then_inc(h2_stats, 1)

            def deviation(g):
                dve.wait_ge(sd_ready, g - 1)
                dve.reciprocal(rstd[:, tiles(g)], sd[:, tiles(g)]).then_inc(rstd_ready, 1)

            def s_lower(g):
                dve.wait_ge(s_hi_ready, g - 1)
                dve.tensor_tensor(s16[:, :, 2:4, :], sn[:, :, :].unsqueeze(2).broadcast_to([P, TG, 2, D]),
                                  s16[:, :, 0:2, :], ALU.subtract).then_inc(s_ready, 1)

            def q_lower(g, u, n):
                dve.wait_ge(qh_ready, g * HP + n + 1)
                dve.tensor_tensor(ql[:, u, n, :], q_bank(g, n)[:, :], qh[:, u, n, :], ALU.subtract).then_inc(q_used, 1)

            def attend(g, u, first=False):
                left = NG - 1 - g if isinstance(g, int) else NG
                mask(g, 0)
                if left >= 1:
                    q_lower(g + 1, 1 - u, 0)
                if left >= 2:
                    deviation(g + 2)
                mask(g, 1)
                if left >= 1:
                    q_lower(g + 1, 1 - u, 1)
                mask(g, 2)
                if not first:
                    back(g - 1)
                if left >= 2:
                    s_lower(g + 2)
                if left >= 1:
                    q_lower(g + 1, 1 - u, 2)
                if left >= 3:
                    h_moments(g + 3)
                mask(g, 3)
                if left >= 1:
                    q_lower(g + 1, 1 - u, 3)
                if not first:
                    sum_stats(g - 1)

            for n in range(HP):
                q_lower(0, 0, n)
            first_normal(1, 4)
            h_moments(2)
            attend(0, 0, first=True)
            with dve.Fori(0, (NG - 4) // 2) as i:
                for u in (1, 0):
                    attend(i * 2 + (1 if u else 2), u)
            attend(NG - 3, 1)
            dve.wait_ge(w1_scaled, 2)
            dve.tensor_reduce(peak[:, 1:2], w1_raw[:, :, :], AX.XY, ALU.max, apply_absolute_value=True).then_inc(s_peak, 1)
            dve.tensor_reduce(peak[:, 2:3], wr_raw[:, :], AX.X, ALU.max, apply_absolute_value=True).then_inc(s_peak, 1)
            dve.wait_ge(s_b2, 96)
            link(dve.tensor_copy(b2_h[:, :], b2_raw[:, :]))
            link(dve.tensor_tensor(b2_raw[:, :], b2_raw[:, :], b2_h[:, :], ALU.subtract))
            link(dve.tensor_copy(b2_m[:, :], b2_raw[:, :]))
            link(dve.tensor_tensor(b2_raw[:, :], b2_raw[:, :], b2_m[:, :], ALU.subtract))
            dve.tensor_copy(b2_p[0:32, :], b2_h[0:32, :]).then_inc(b2_ready, 1)
            dve.tensor_copy(b2_p[32:64, :], b2_m[32:64, :]).then_inc(b2_ready, 1)
            dve.tensor_copy(b2_p[64:96, :], b2_raw[64:96, :]).then_inc(b2_ready, 1)
            link(dve.tensor_copy(rank[:, :], rank_i[:, :]))
            attend(NG - 2, 0)
            dve.wait_ge(s_amax, 2)
            scales(1, 3)
            attend(NG - 1, 1)
            dve.wait_ge(w1_hi_ready, 2)
            dve.scalar_tensor_tensor(out=w1_lo[:, :, :], in0=w1_raw[:, :, :], scalar=up[:, 1:2], in1=w1_hi[:, :, :],
                                     op0=ALU.mult, op1=ALU.subtract).then_inc(w1_ready, 1)
            dve.scalar_tensor_tensor(out=wr_lo[:, :], in0=wr_raw[:, :], scalar=up[:, 2:3], in1=wr_hi[:, :],
                                     op0=ALU.mult, op1=ALU.subtract).then_inc(w1_ready, 1)
            back(NG - 1)
            sum_stats(NG - 1)

            dve.wait_ge(h2_stats, NT)
            def twice_normal(x, y, root):
                moments(stats, mean3, x, y)
                dve.tensor_scalar(tmp[:, x:y], var[:, x:y], EPS, None, ALU.add).then_inc(batch_var, 1)
                dve.wait_ge(batch_sd, root)
                ch.done(dve.reciprocal(rstd3[:, x:y], tmp2[:, x:y]))
                ch.settle()
                ch.done(dve.tensor_tensor(tmp[:, x:y], rstd3[:, x:y], rstd3[:, x:y], ALU.mult))
                ch.settle()
                ch.done(dve.tensor_tensor(tmp[:, x:y], tmp[:, x:y], var[:, x:y], ALU.mult))
                ch.settle()
                dve.tensor_scalar(tmp[:, x:y], tmp[:, x:y], EPS, None, ALU.add).then_inc(batch_var, 1)
                dve.wait_ge(batch_sd, root + 1)
                ch.done(dve.reciprocal(tmp[:, x:y], tmp2[:, x:y]))
                ch.settle()
                ch.done(dve.tensor_tensor(rstd3[:, x:y], rstd3[:, x:y], tmp[:, x:y], ALU.mult))
                ch.settle()

            twice_normal(0, NT, 5)

            SP = 3

            def expert_input(g, u, first=False):
                lc = Steps(dve, dve_ln3, g * SP, SP)
                if not first:
                    dve.wait_ge(xt_done, g - 1)
                    dve.wait_ge(x_ready, g - 1)
                lc.done(dve.tensor_tensor(x32[:, u, :, :], h[:, tiles(g), :],
                                          mean3[:, tiles(g)].unsqueeze(2).broadcast_to([P, TG, D]), ALU.subtract))
                lc.settle()
                lc.done(dve.tensor_tensor(x32[:, u, :, :], x32[:, u, :, :],
                                          rstd3[:, tiles(g)].unsqueeze(2).broadcast_to([P, TG, D]), ALU.mult))
                lc.settle()
                lc.done(dve.tensor_copy(x16[:, u, :, 0, :], x32[:, u, :, :]))
                lc.settle()
                lc.close()
                dve.tensor_tensor(x16[:, u, :, 1, :], x32[:, u, :, :], x16[:, u, :, 0, :],
                                  ALU.subtract).then_inc(x_ready, 1)

            expert_input(0, 0, True)
            expert_input(1, 1, True)
            with dve.Fori(1, NG // 2) as i:
                for u in range(2):
                    expert_input(i * 2 + u, u)

            gs = Steps(dve, dve_gate)
            halves = [slice(0, NT // 2), slice(NT // 2, NT)]

            def both(f):
                for x in halves:
                    gs.done(f(x))
                gs.settle()

            def wide(a, x):
                return a[:, x].unsqueeze(2).broadcast_to([P, NT // 2, NX])

            rank_w = rank[:, :].unsqueeze(1).broadcast_to([P, NT // 2, NX])
            dve.wait_ge(lg_done, NG)
            dve.tensor_scalar(lg[:, :, :], bank[2][:, 0:NT * NX].rearrange("p (t e) -> p t e", e=NX),
                              down[:, 2:3], None, ALU.mult).then_inc(lg_read, 1)
            dve.wait_ge(lg_read, 1)
            both(lambda x: dve.tensor_tensor(lg[:, x, :], lg[:, x, :],
                                             br_f[:, :].unsqueeze(1).broadcast_to([P, NT // 2, NX]), ALU.add))

            def pick_top(src, top, chosen):
                both(lambda x: dve.tensor_reduce(top[:, x], src[:, x, :], AX.X, ALU.max))
                both(lambda x: dve.tensor_tensor(pick[:, x, :], src[:, x, :], wide(top, x), ALU.is_equal))
                both(lambda x: dve.tensor_tensor(pick[:, x, :], pick[:, x, :], rank_w, ALU.mult))
                both(lambda x: dve.tensor_reduce(best[:, x], pick[:, x, :], AX.X, ALU.max))
                both(lambda x: dve.tensor_tensor(chosen[:, x, :], pick[:, x, :], wide(best, x), ALU.is_equal))

            pick_top(lg, top1, sel1)
            both(lambda x: dve.scalar_tensor_tensor(out=lg2[:, x, :], in0=sel1[:, x, :], scalar=-3e38, in1=lg[:, x, :],
                                                    op0=ALU.mult, op1=ALU.add))
            pick_top(lg2, top2, sel2)
            dve.tensor_tensor(best[:, :], top2[:, :], top1[:, :], ALU.subtract).then_inc(r_exp, 1)
            dve.wait_ge(exp_done, 1)
            both(lambda x: dve.tensor_scalar(wt1[:, x], ratio[:, x], 1.0, None, ALU.add))
            both(lambda x: dve.reciprocal(wt1[:, x], wt1[:, x]))
            both(lambda x: dve.tensor_tensor(wt2[:, x], wt1[:, x], ratio[:, x], ALU.mult))
            for x in halves:
                gs.done(dve.tensor_tensor(sel1[:, x, :], sel1[:, x, :], wide(wt1, x), ALU.mult))
            both(lambda x: dve.tensor_tensor(sel2[:, x, :], sel2[:, x, :], wide(wt2, x), ALU.mult))
            both(lambda x: dve.tensor_tensor(gate[:, x, :], sel1[:, x, :], sel2[:, x, :], ALU.add))
            dve.wait_ge(gate_zero, 2)
            for k in range(3):
                gs.done(dve.tensor_copy(gate16[:, :, k, 0, :], gate[:, :, :]))
            gs.settle()
            for k in range(3):
                dve.tensor_tensor(gate16[:, :, k, 1, :], gate[:, :, :], gate16[:, :, k, 0, :],
                                  ALU.subtract).then_inc(gate_ready, 1)

            def finish(g):
                dve.wait_ge(fin_done, g + 1)
                dve.tensor_tensor(res[:, tiles(g), :], h[:, tiles(g), :],
                                  bank[7][:, 0:256].rearrange("p (t d) -> p t d", d=D), ALU.add).then_inc(res_ready, 1)

            def gated(g, first=False):
                for e in range(NX):
                    dve.wait_ge(hid_ready, g * NX + e + 1)
                    dve.wait_ge(w_done, g * NX + e + 1)
                    if not first:
                        dve.wait_ge(y_part, (g - 1) * NX + e + 1)
                    dve.tensor_tensor(hw[:, e, :], hid[:, e, :], bank[3 + e % 2][:, :], ALU.mult).then_inc(hw_ready, 1)
                    if e == 4 and not first:
                        finish(g - 1)

            gated(0, True)
            with dve.Fori(1, NG) as g:
                gated(g)
            finish(NG - 1)

        @block.scalar
        def _(act):
            act.dma_start(w_raw[:, :], W).then_inc(s_w, 16)
            act.dma_start(wT[KW:KW + 1, :], b.rearrange("(a n) -> a n", a=1)).then_inc(s_emb, 16)
            act.wait_ge(s_ones, 1)
            act.activation(tmp2[:, 0:1], ones[:, 0:1], ACT.Sqrt)
            act.wait_ge(s_idx, 96)
            act.wait_ge(idx_zero, 1)
            act.activation(idx_b[0:6, N // 2:N], idx_i[:, N // 2:N], ACT.Copy).then_inc(idx_ready, 1)
            for c in range(NC):
                act.wait_ge(pe_embT, c + 1)
                act.activation(embT[:, c, :], bank[1 + c][0:KW + 1, 0:P], ACT.Copy).then_inc(embT_ready, 1)

            def copies(g, u, first=False):
                for c in range(1, NC):
                    if not first:
                        act.wait_ge(hot_ready, (g - 2) * NC + c + 1)
                    act.wait_ge(spread, g * NC + c + 1)
                    act.activation(idx_c[:, u, c, :], bank[c][:, :], ACT.Copy).then_inc(copied, 1)

            def z_copy(g, u):
                act.wait_ge(z_done, g + 1)
                act.activation(z[:, tiles(g), :], bank[4 + u][:, 0:TG * D].rearrange("p (t d) -> p t d", d=D),
                               ACT.Copy).then_inc(z_ready, 1)

            copies(0, 0, True)
            copies(1, 1, True)
            act.wait_ge(scale_ready, 1)
            act.activation(q_hi[:, :], q_raw[:, :, :].rearrange("p h j -> p (h j)"), ACT.Copy,
                           scale=up[:, 0:1]).then_inc(q_hi_ready, 1)
            with act.Fori(1, NG // 2 - 1) as i:
                for u in range(2):
                    copies(i * 2 + u, u)
                    z_copy(i * 2 + u - 2, u)

            def root(n, x, y):
                act.wait_ge(batch_var, n)
                act.activation(tmp2[:, x:y], tmp[:, x:y], ACT.Sqrt).then_inc(batch_sd, 1)

            NA = (NG - 4) * TG
            copies(NG - 2, 0)
            z_copy(NG - 4, 0)
            root(1, 0, NA)
            copies(NG - 1, 1)
            z_copy(NG - 3, 1)
            root(2, 0, TG)
            z_copy(NG - 2, 0)
            z_copy(NG - 1, 1)

            def deviation(g):
                act.wait_ge(var_ready, g - 1)
                act.activation(sd[:, tiles(g)], var[:, tiles(g)], ACT.Sqrt).then_inc(sd_ready, 1)

            def sT_copy(g, u):
                act.wait_ge(t_done, g + 1)
                wait(act, q_done, (g - 1) * HP)
                act.activation(sTm[:, u, :], bank[0][:, 0:256].bitcast(F16), ACT.Copy).then_inc(sTm_ready, 1)
                wait(act, om_done, (g - 1) * TG)
                act.activation(sTh[:, u, :], bank[0][:, 256:512].bitcast(F16), ACT.Copy).then_inc(sT_ready, 1)
                act.activation(sTl[:, u, :], bank[1][:, 0:256].bitcast(F16), ACT.Copy).then_inc(sT_ready, 1)

            def s_upper(g):
                act.wait_ge(sn_ready, g - 1)
                act.wait_ge(t_done, g)
                act.activation(s16[:, :, 0:2, :], sn[:, :, :].unsqueeze(2).broadcast_to([P, TG, 2, D]),
                               ACT.Copy).then_inc(s_hi_ready, 1)

            def q_upper(g, u, n):
                act.wait_ge(q_done, g * HP + n + 1)
                wait(act, om_done, (g - 1) * TG)
                act.activation(qh[:, u, n, :], q_bank(g, n)[:, :], ACT.Copy).then_inc(qh_ready, 1)

            def a_copy(g, t):
                act.wait_ge(a_done, g * TG + t + 1)
                wait(act, r_done, g)
                act.activation(aT[:, :, t * P:(t + 1) * P], bank[3][:, :].rearrange("p (a t) -> p a t", t=P),
                               ACT.Copy).then_inc(a_ready, 1)

            def r_copy(g):
                act.wait_ge(r_done, g + 1)
                wait(act, back_done, g)
                act.activation(rT[:, :], bank[2][:, :], ACT.Copy).then_inc(rT_ready, 1)

            def attend(g, u, first=False):
                left = NG - 1 - g if isinstance(g, int) else NG
                if left >= 1:
                    q_upper(g + 1, 1 - u, 0)
                if left >= 2:
                    deviation(g + 2)
                if not first:
                    r_copy(g - 1)
                if left >= 1:
                    q_upper(g + 1, 1 - u, 1)
                a_copy(g, 0)
                if left >= 2:
                    s_upper(g + 2)
                if left >= 1:
                    q_upper(g + 1, 1 - u, 2)
                a_copy(g, 1)
                if left >= 1:
                    q_upper(g + 1, 1 - u, 3)
                a_copy(g, 2)
                if left >= 2:
                    sT_copy(g + 2, u)
                a_copy(g, 3)

            sT_copy(0, 0)
            root(3, NA, NT)
            root(4, TG, 2 * TG)
            for n in range(HP):
                q_upper(0, 0, n)
            sT_copy(1, 1)
            attend(0, 0, first=True)
            act.wait_ge(pe_bias, 1)
            act.activation(w1_raw[:, :, :], w1_raw[:, :, :], ACT.Copy, scale=fg[:, 0:1]).then_inc(w1_scaled, 1)
            act.activation(wr_raw[:, :], wr_raw[:, :], ACT.Copy, scale=fg[:, 0:1]).then_inc(w1_scaled, 1)
            with act.Fori(0, (NG - 4) // 2) as i:
                for u in (1, 0):
                    attend(i * 2 + (1 if u else 2), u)
            attend(NG - 3, 1)
            attend(NG - 2, 0)
            attend(NG - 1, 1)
            act.wait_ge(scale_ready, 3)
            act.activation(w1_hi[:, :, :], w1_raw[:, :, :], ACT.Copy, scale=up[:, 1:2]).then_inc(w1_hi_ready, 1)
            act.activation(wr_hi[:, :], wr_raw[:, :], ACT.Copy, scale=up[:, 2:3]).then_inc(w1_hi_ready, 1)
            r_copy(NG - 1)

            root(5, 0, NT)
            root(6, 0, NT)
            with act.Fori(0, NG // 2) as i:
                for u in range(2):
                    g = i * 2 + u
                    act.wait_ge(xt_done, g + 1)
                    act.activation(xT[:, bass.ds(g * GC, GC)], bank[u][:, 0:256].bitcast(F16),
                                   ACT.Copy).then_inc(xT_ready, 1)
            act.wait_ge(r_exp, 1)
            act.activation(ratio[:, :], best[:, :], ACT.Exp).then_inc(exp_done, 1)

            def gT_copy(g, u):
                act.wait_ge(gt_done, g + 1)
                wait(act, w_done, (g - 1) * NX)
                act.activation(gT[:, u, :], bank[7][0:96, 256:512].bitcast(F16), ACT.Copy).then_inc(gT_ready, 1)

            def yT_copy(g, u):
                act.wait_ge(y_part, (g + 1) * NX)
                wait(act, fin_done, g)
                act.activation(yT[:, :], bank[5 + u][:, :], ACT.Copy).then_inc(yT_ready, 1)

            def gelus(g, u, first=False, last=False):
                for e in range(NX):
                    act.wait_ge(hid_done, g * NX + e + 1)
                    if not first:
                        act.wait_ge(hw_ready, (g - 1) * NX + e + 1)
                    act.activation(hid[:, e, :], bank[e % 3][:, :], ACT.Gelu, bias=b1_f[:, e:e + 1],
                                   scale=down[:, 1:2]).then_inc(hid_ready, 1)
                    if first and e == 2:
                        gT_copy(0, 0)
                    if e == 1 and not first:
                        yT_copy(g - 1, 1 - u)
                    if e == 6 and not last:
                        gT_copy(g + 1, 1 - u)

            gelus(0, 0, first=True)
            with act.Fori(0, (NG - 2) // 2) as i:
                for u in (1, 0):
                    gelus(i * 2 + (1 if u else 2), u)
            gelus(NG - 1, 1, last=True)
            yT_copy(NG - 1, 1)

        @block.tensor
        def _(pe):
            pe.wait_ge(w_sum, 1)
            pe.wait_ge(s_ones, 1)
            pe.matmul(bank[0][:, 0:1], ones[0:D, :], w_abs[:, :], start=True, stop=True).then_inc(pe_wabs, 1)
            pe.wait_ge(s_id, 1)
            pe.wait_ge(s_emb, 16 * 7)
            pe.wait_ge(one_ready, 1)
            for c in range(NC):
                pe.transpose(bank[1 + c][0:KW + 1, 0:P], emb[:, c, :], ident[:, :]).then_inc(pe_embT, 1)
            pe.wait_ge(w_ready, 1)
            pe.transpose(bank[5][0:KW, 0:D], w_pos[:, :], ident[0:D, 0:D]).then_inc(pe_embT, 1)
            pe.wait_ge(embT_ready, 5)
            for c in range(NC):
                mm = pe.matmul(bank[6][:, c * D:(c + 1) * D], embT[:, c, :], wT[:, :], start=True, stop=True)
            mm.then_inc(pe_tab, 1)

            def spread_idx(g, first=False):
                for c in range(NC):
                    if not first:
                        if c == 0:
                            pe.wait_ge(hot_ready, (g - 1) * NC + 1)
                        else:
                            pe.wait_ge(copied, (g - 1) * 3 + c)
                    pe.matmul(bank[c][:, :], sel[:, c * P:(c + 1) * P],
                              idx_b[:, g * GC:(g + 1) * GC] if isinstance(g, int) else idx_b[:, bass.ds(g * GC, GC)],
                              start=True, stop=True).then_inc(spread, 1)

            def look_up(g, u):
                pe.wait_ge(hot_ready, (g + 1) * NC)
                wait(pe, z_ready, g - 1)
                for t in range(TG):
                    for c in range(NC):
                        for k in range(3):
                            mm = pe.matmul(bank[4 + u][:, t * D:(t + 1) * D], hot[:, u, c, t * P:(t + 1) * P],
                                           tab[:, c, k, :], start=(c == 0 and k == 0), stop=(c == NC - 1 and k == 2))
                mm.then_inc(z_done, 1)

            pe.wait_ge(idx_ready, 2)
            pe.wait_ge(s_sel, 1)
            spread_idx(0, True)
            spread_idx(1)
            pe.wait_ge(tab_ready, 1)
            look_up(0, 0)
            with pe.Fori(1, NG // 2 - 1) as i:
                for u in range(2):
                    spread_idx(i * 2 + u)
                    look_up(i * 2 + u - 1, 1 - u)
            spread_idx(NG - 2)
            look_up(NG - 3, 1)
            spread_idx(NG - 1)
            pe.wait_ge(s_wgt, N_WGT)
            pe.wait_ge(q_ready, 1)
            pe.transpose(bank[7][:, 0:NX], b1_raw[:, :], ident[0:NX, 0:NX])
            for e in range(NX):
                pe.matmul(bank[7][:, NX + e:NX + e + 1], w1_raw[0:D, e, :], fb[0:D, 0:1], start=True, stop=True)
            pe.matmul(bank[7][:, 2 * NX:3 * NX], beta_row[:, :], wr_raw[0:D, :], start=True, stop=False)
            pe.matmul(bank[7][:, 2 * NX:3 * NX], ones[0:1, :], br_raw[:, :], start=False, stop=True)
            for n in range(HP):
                mm = pe.transpose(bank[7][:, 256 + n * D:256 + (n + 1) * D],
                                  e_raw[:, 2 * n:2 * n + 2, :].rearrange("p h d -> p (h d)"), ident[0:D, 0:D])
            mm.then_inc(pe_bias, 1)
            look_up(NG - 2, 0)
            look_up(NG - 1, 1)

            def turn(g):
                pe.wait_ge(s_ready, g + 1)
                wait(pe, back_ready, g - 2)
                wait(pe, sT_ready, 2 * g)
                for dst, k in ((bank[0][:, 0:256], 1), (bank[0][:, 256:512], 0), (bank[1][:, 0:256], 2)):
                    for t in range(TG):
                        mm = pe.transpose(dst[:, t * 64:(t + 1) * 64].bitcast(F16),
                                          s16[:, t, k:k + 2, :].rearrange("p k d -> p (k d)"), ident16[:, :])
                mm.then_inc(t_done, 1)

            def project(g, u, n):
                pe.wait_ge(sTm_ready, g + 1)
                wait(pe, q_used, g * HP + n if not isinstance(g, int) or g > 0 else 0)
                for k, w in enumerate((q_hi, q_lo)):
                    mm = pe.matmul(q_bank(g, n)[:, :], w[:, n * P:(n + 1) * P], sTm[:, u, :],
                                   start=(k == 0), stop=(k == 1))
                mm.then_inc(q_done, 1)

            def omega(g, u, t):
                wait(pe, om_ready, g * 2 * TG + [0, 1, 3, 5][t])
                if t == 0:
                    pe.wait_ge(sT_ready, 2 * (g + 1))
                    pe.wait_ge(q_used, (g + 1) * HP)
                tt = slice(t * P, (t + 1) * P)
                for k, (sx, qx) in enumerate(((sTh, qh), (sTh, ql), (sTl, qh))):
                    for par in range(2):
                        r = slice(par * D, par * D + D)
                        mm = pe.matmul(bank[5 + OM_BANK[2 * t + par]][:, :], sx[r, u, tt], qx[r, u, :, tt],
                                       start=(k == 0), stop=(k == 2))
                mm.then_inc(om_done, 1)

            def weigh(g, u, t):
                if t == 0:
                    wait(pe, s32_ready, g - 1)
                wait(pe, a_ready, g * TG + t)
                pe.wait_ge(om_ready, (g * TG + t + 1) * 2)
                for par in range(2):
                    mm = pe.matmul(bank[3][par * D:par * D + D, :], s32[:, u, t, :],
                                   om8[:, 2 * t + par, :, :].rearrange("p a t -> p (a t)"), start=True, stop=True)
                mm.then_inc(a_done, 1)

            def mix(g):
                pe.wait_ge(a_ready, (g + 1) * TG)
                wait(pe, rT_ready, g)
                for n in range(HP):
                    o = n % 2 * D
                    mm = pe.matmul(bank[2][o:o + D, :], eT[:, n, :], aT[:, n, :], start=(n < 2), stop=(n >= 2))
                mm.then_inc(r_done, 1)

            def back(g):
                pe.wait_ge(rT_ready, g + 1)
                for t in range(TG):
                    mm = pe.matmul(bank[1][:, 256 + t * D:256 + (t + 1) * D], rT[:, t * P:(t + 1) * P], fold[:, :],
                                   start=True, stop=True)
                mm.then_inc(back_done, 1)

            def attend(g, u, first=False):
                left = NG - 1 - g if isinstance(g, int) else NG
                omega(g, u, 0)
                if first:
                    turn(1)
                if left >= 1:
                    project(g + 1, 1 - u, 0)
                if not first:
                    mix(g - 1)
                omega(g, u, 1)
                if left >= 1:
                    project(g + 1, 1 - u, 1)
                weigh(g, u, 0)
                if not first:
                    back(g - 1)
                omega(g, u, 2)
                if left >= 1:
                    project(g + 1, 1 - u, 2)
                weigh(g, u, 1)
                omega(g, u, 3)
                if left >= 1:
                    project(g + 1, 1 - u, 3)
                weigh(g, u, 2)
                if left >= 2:
                    turn(g + 2)
                weigh(g, u, 3)

            turn(0)
            pe.wait_ge(z_ready, NG)
            for n in range(HP):
                project(0, 0, n)
            pe.wait_ge(e_ready, 1)
            attend(0, 0, first=True)
            with pe.Fori(0, (NG - 4) // 2) as i:
                for u in (1, 0):
                    attend(i * 2 + (1 if u else 2), u)
            for g in range(NG - 3, NG):
                attend(g, g % 2)
            mix(NG - 1)
            back(NG - 1)

            pe.wait_ge(w1_ready, 2)
            pe.wait_ge(back_ready, NG)

            def logits(g):
                pe.wait_ge(xT_ready, g + 1)
                for t in range(TG):
                    k = g * TG + t
                    o = bank[2][:, bass.ds(k * NX, NX)]
                    pe.matmul(o, xT[:, bass.ds(k * P, P)], wr_hi[:, :], start=True, stop=False)
                    mm = pe.matmul(o, xT[:, bass.ds(k * P, P)], wr_lo[:, :], start=False, stop=True)
                mm.then_inc(lg_done, 1)

            def turn_x(g, u):
                pe.wait_ge(x_ready, g + 1)
                for t in range(TG):
                    mm = pe.transpose(bank[u][:, t * 64:(t + 1) * 64].bitcast(F16),
                                      x16[:, u, t, :, :].rearrange("p k d -> p (k d)"), ident16[:, :])
                mm.then_inc(xt_done, 1)

            turn_x(0, 0)
            turn_x(1, 1)
            with pe.Fori(1, NG // 2) as i:
                for u in range(2):
                    logits(i * 2 + u - 2)
                    turn_x(i * 2 + u, u)
            logits(NG - 2)
            logits(NG - 1)

            def hidden(g, e):
                wait(pe, hid_ready, g * NX + [-1, 0, -2, 1, 2, 3, 4, 5][e])
                rhs = xT[:, g * GC:(g + 1) * GC] if isinstance(g, int) else xT[:, bass.ds(g * GC, GC)]
                for k, w in enumerate((w1_hi, w1_lo)):
                    mm = pe.matmul(bank[e % 3][:, :], w[:, e, :], rhs, start=(k == 0), stop=(k == 1))
                mm.then_inc(hid_done, 1)

            def turn_gate(g):
                wait(pe, res_ready, g - 1)
                for t in range(TG):
                    src = gate16[:, bass.ds(g * TG + t, 1), :, :, :].rearrange("p a x y e -> p (a x y e)")
                    mm = pe.transpose(bank[7][0:96, 256 + t * 64:256 + (t + 1) * 64].bitcast(F16), src, ident16[:, :])
                mm.then_inc(gt_done, 1)

            def spread_gate(g, u, e):
                if e == 0:
                    pe.wait_ge(gT_ready, g + 1)
                wait(pe, hw_ready, g * NX + e - 1)
                pe.matmul(bank[3 + e % 2][:, :], sel_w[:, e, :], gT[:, u, :], start=True, stop=True).then_inc(w_done, 1)

            def outer(g, u, e):
                pe.wait_ge(hw_ready, g * NX + e + 1)
                o = e % 2 * D
                if e == 0:
                    wait(pe, yT_ready, g - 1)
                    pe.matmul(bank[5 + u][0:D, :], b2_p[:, :], gT[:, u, :], start=True, stop=False)
                mm = pe.matmul(bank[5 + u][o:o + D, :], w2[:, e, :], hw[:, e, :], start=(e == 1), stop=(e >= NX - 2))
                mm.then_inc(y_part, 1)

            def finish(g):
                pe.wait_ge(yT_ready, g + 1)
                for t in range(TG):
                    mm = pe.matmul(bank[7][:, t * D:(t + 1) * D], yT[:, t * P:(t + 1) * P], fold[:, :],
                                   start=True, stop=True)
                mm.then_inc(fin_done, 1)

            def experts(g, u, first=False, last=False):
                for e in range(NX):
                    hidden(g, e)
                    if first and e < 2:
                        continue
                    if first and e == 2:
                        pe.wait_ge(gate_ready, 3)
                        turn_gate(0)
                        for n in range(2):
                            spread_gate(g, u, n)
                    spread_gate(g, u, e)
                    if e >= 2:
                        outer(g, u, e - 2)
                    elif not first:
                        outer(g - 1, 1 - u, NX - 2 + e)
                    if e == 4 and not first:
                        finish(g - 1)
                    if e == 6 and not last:
                        turn_gate(g + 1)

            pe.wait_ge(b2_ready, 3)
            pe.wait_ge(gate_zero, 1)
            pe.wait_ge(lg_read, 1)
            experts(0, 0, first=True)
            with pe.Fori(0, (NG - 2) // 2) as i:
                for u in (1, 0):
                    experts(i * 2 + (1 if u else 2), u)
            experts(NG - 1, 1, last=True)
            outer(NG - 1, 1, NX - 2)
            outer(NG - 1, 1, NX - 1)
            finish(NG - 1)


_INS = ['x', 'itok_BS_0_255', 'itok_BS_0_511', 'itok_BS_0_127', 'itok_BS_0_63', 'itok_BS_0_3',
        'L0_tok_E_et', 'L0_tok_E_fc', 'L0_tok_E_sc', 'L0_tok_E_of', 'L0_tok_E_tt', 'L0_tok_E_rc',
        'L0_tok_W', 'L0_tok_b', 'L0_tok_gamma', 'L0_tok_beta', 'L0_attn_Q', 'L0_attn_E',
        'L0_ffn_gamma', 'L0_ffn_beta', 'L0_ffn_Wr', 'L0_ffn_br', 'L0_ffn_W1', 'L0_ffn_b1', 'L0_ffn_W2', 'L0_ffn_b2']


def kernel(**inputs):
    import numpy as _np
    import concourse.bacc as _bacc
    from concourse import mybir as _mybir
    from concourse.bass_utils import run_bass_kernel_spmd as _run

    nc = _bacc.Bacc("TRN2", target_bir_lowering=False, num_devices=1)
    arrays, args = {}, []
    for name in _INS:
        a = _np.ascontiguousarray(inputs[name])
        arrays[f"in_{name}_dram"] = a
        args.append(nc.dram_tensor(f"in_{name}_dram", a.shape, _mybir.dt.from_np(a.dtype), kind="ExternalInput").ap())
    B, S = inputs['x'].shape
    D = inputs['L0_tok_W'].shape[0]
    out = nc.dram_tensor("out_dram", (B, S, D), _mybir.dt.float32, kind="ExternalOutput").ap()
    lm_tower(nc, args[0:6], args[6:12], *args[12:], out)
    r = _run(nc, [arrays], core_ids=[0])
    return r.results[0]["out_dram"]
```

```python
from contextlib import ExitStack

import concourse.bass as bass
from concourse import mybir

P = 128
ALU = mybir.AluOpType
ACT = mybir.ActivationFunctionType
AX = mybir.AxisListType
F32 = mybir.dt.float32
F16 = mybir.dt.float16
BF16 = mybir.dt.bfloat16
I32 = mybir.dt.int32
RMAX = bass.bass_isa.ReduceOp.max


class Steps:

    def __init__(self, eng, sem, base=0, per_iteration=None):
        self.eng, self.sem, self.base, self.n, self.per = eng, sem, base, 0, per_iteration

    def done(self, instruction):
        instruction.then_inc(self.sem, 1)
        self.n += 1

    def settle(self):
        self.eng.wait_ge(self.sem, self.base + self.n)

    def close(self):
        assert self.per is None or self.n == self.per, (self.n, self.per)


def lm_tower(nc, idx, tables, W, b, gamma, beta, Q, E, fgamma, fbeta, Wr, br, W1, b1, W2, b2, out):
    B, S = idx[0].shape
    N = B * S
    NT = N // P
    TG = 4
    NG = NT // TG
    GC = TG * P
    TR = 2 * TG
    D, KW = W.shape
    EMB = KW // len(tables)
    H = Q.shape[0]
    NX, _, FH = W1.shape
    HP = H // 2
    NC = 4
    EPS = 1e-5
    LIFT = (16.0, 1024.0, 1024.0)
    assert S == P and D == 64 and FH == P and H * D == 512 and NX * D == 512

    place = [(0, 0), (0, 64), (1, 0), (2, 0), (3, 0), (3, 64)]
    half_row = [0, 1, 2, 2, 3, 3, 4, 5]

    with ExitStack() as ctx:
        def sb(name, shape, dt=F32):
            return ctx.enter_context(nc.sbuf_tensor(name, shape, dt))

        def sem(name):
            return ctx.enter_context(nc.semaphore(name))

        bank = [ctx.enter_context(nc.psum_tensor(f"bank{i}", [P, 512], F32)) for i in range(8)]

        ident = sb("ident", [P, P])
        ident16 = sb("ident16", [P, P], F16)
        fold = sb("fold", [P, D])
        causal = sb("causal", [P, P])
        causal_q = sb("causal_q", [P, P])
        ones = sb("ones", [P, P])
        sel = sb("sel", [96, NC * P], BF16)
        row_i = sb("row_i", [P, NC], I32)
        row_id = sb("row_id", [P, NC])
        rank = sb("rank", [P, NX])
        rank_i = sb("rank_i", [P, NX], I32)
        sel_w = sb("sel_w", [96, NX, P], F16)
        hid = sb("hid", [P, NX, GC])
        idx_i = hid[0:6, :, :].rearrange("p e t -> p (e t)").bitcast(I32)
        idx_b = sb("idx_b", [96, N], BF16)
        emb = sb("emb", [P, NC, KW + 1])
        embT = sb("embT", [KW + 1, NC, P])
        w_raw = sb("w_raw", [D, KW])
        w_abs = sb("w_abs", [D, 1])
        w_s = sb("w_s", [P, 4])
        w_pos = sb("w_pos", [D, KW])
        w_neg = sb("w_neg", [D, KW])
        wT = sb("wT", [KW + 1, D])
        tab_f = sb("tab_f", [P, NC, D])
        tab = sb("tab", [P, NC, 3, D], BF16)
        gam = sb("gam", [P, D])
        bet = sb("bet", [P, D])
        q_raw = sb("q_raw", [P, H, D])
        e_raw = sb("e_raw", [D, H, D])
        w1_raw = sb("w1_raw", [P, NX, FH])
        wr_raw = sb("wr_raw", [P, NX])
        fg = sb("fg", [P, 1])
        fb = sb("fb", [P, 1])
        b1_raw = sb("b1_raw", [NX, FH])
        br_raw = sb("br_raw", [1, NX])
        b2_raw = sb("b2_raw", [96, D])
        b2_h = sb("b2_h", [96, D], BF16)
        b2_m = sb("b2_m", [96, D], BF16)
        b2_p = sb("b2_p", [96, D], BF16)
        w2 = sb("w2", [FH, NX, D])
        peak = sb("peak", [P, 3])
        peak_all = sb("peak_all", [P, 3])
        pow2 = sb("pow2", [P, 3])
        up = sb("up", [P, 3])
        down = sb("down", [P, 3])
        q_hi = sb("q_hi", [P, H * D], F16)
        q_lo = sb("q_lo", [P, H * D], F16)
        eT = sb("eT", [P, HP, D])
        w1_hi = sb("w1_hi", [P, NX, FH], F16)
        w1_lo = sb("w1_lo", [P, NX, FH], F16)
        wr_hi = sb("wr_hi", [P, NX], F16)
        wr_lo = sb("wr_lo", [P, NX], F16)
        b1_f = sb("b1_f", [FH, NX])
        br_f = sb("br_f", [P, NX])
        beta_row = sb("beta_row", [D, P])
        z = sb("z", [P, NT, D])
        h = sb("h", [P, NT, D])
        stats = sb("stats", [P, NT, 6])
        hstats = sb("hstats", [P, NT, 6])
        mean1 = sb("mean1", [P, NT])
        rstd1 = sb("rstd1", [P, NT])
        mean = sb("mean", [P, NT])
        var = sb("var", [P, NT])
        rstd = sb("rstd", [P, NT])
        sd = sb("sd", [P, NT])
        mean3 = sb("mean3", [P, NT])
        rstd3 = sb("rstd3", [P, NT])
        tmp = sb("tmp", [P, NT])
        tmp2 = sb("tmp2", [P, NT])
        diff = sb("diff", [P, TG])
        hn = sb("hn", [P, TG, D])
        xT = sb("xT", [P, N], F16)
        hot = sb("hot", [P, 2, NC, GC], BF16)
        zT = sb("zT", [P, 2, GC])
        idx_c = sb("idx_c", [P, 2, NC, GC], BF16)
        s32 = sb("s32", [P, 2, TG, D])
        sn = sb("sn", [P, TG, D])
        s16 = sb("s16", [P, TG, 4, D], F16)
        sTm = sb("sTm", [P, 2, GC], F16)
        sTh = sb("sTh", [P, 2, GC], F16)
        sTl = sb("sTl", [P, 2, GC], F16)
        qh = sb("qh", [P, 2, HP, GC], F16)
        ql = sb("ql", [P, 2, HP, GC], F16)
        om8 = sb("om8", [P, 2 * TG, HP, P])
        aT = sb("aT", [P, HP, GC])
        rT = sb("rT", [P, GC])
        x16 = sb("x16", [P, 2, TG, 2, D], F16)
        hw = sb("hw", [P, NX, GC])
        gT = sb("gT", [96, 2, GC], F16)
        yT = sb("yT", [P, GC])
        res = sb("res", [P, NT, D])
        lg = sb("lg", [P, TR, NX])
        lg2 = sb("lg2", [P, TR, NX])
        pick = sb("pick", [P, TR, NX])
        sel1 = sb("sel1", [P, TR, NX])
        sel2 = sb("sel2", [P, TR, NX])
        both = sb("both", [P, TR, NX])
        diff2 = sb("diff2", [P, TR, NX])
        top1 = sb("top1", [P, TR])
        top2 = sb("top2", [P, TR])
        best = sb("best", [P, TR])
        gap = sb("gap", [P, TR])
        tanh = sb("tanh", [P, TR])
        gate16 = sb("gate16", [P, NT, 3, 4, NX], F16)
        minus_half = sb("minus_half", [P, NT // 2])
        mean_gap3 = sb("mean_gap3", [P, NT // 2])
        var3 = sb("var3", [P, NT // 2])
        once = sb("once", [P, NT // 2])

        s_idx = sem("s_idx"); s_q = sem("s_q"); s_w = sem("s_w"); s_emb = sem("s_emb"); s_wgt = sem("s_wgt")
        s_gam = sem("s_gam"); s_b2 = sem("s_b2"); s_out = sem("s_out")
        s_ones = sem("s_ones"); s_pool = sem("s_pool"); pool_step = sem("pool_step")
        s_sel = sem("s_sel"); s_id = sem("s_id"); s_amax = sem("s_amax"); pool_h = sem("pool_h")
        emb_zero = sem("emb_zero"); b2_zero = sem("b2_zero"); dve_setup = sem("dve_setup")
        pe_wabs = sem("pe_wabs"); w_sum = sem("w_sum"); w_ready = sem("w_ready")
        pe_embT = sem("pe_embT"); embT_ready = sem("embT_ready"); pe_tab = sem("pe_tab")
        tab_ready = sem("tab_ready"); idx_zero = sem("idx_zero"); idx_ready = sem("idx_ready")
        idx_more = sem("idx_more"); fold_ready = sem("fold_ready")
        s_peak = sem("s_peak")
        q_ready = sem("q_ready"); beta_ready = sem("beta_ready"); pe_bias = sem("pe_bias")
        w1_ready = sem("w1_ready"); one_ready = sem("one_ready"); w1_scaled = sem("w1_scaled")
        b2_ready = sem("b2_ready"); scale_ready = sem("scale_ready")
        q_hi_ready = sem("q_hi_ready"); w1_hi_ready = sem("w1_hi_ready")
        spread = sem("spread"); copied = sem("copied"); hot_ready = sem("hot_ready")
        zt_done = sem("zt_done"); zT_read = sem("zT_read"); z_done = sem("z_done"); z_read = sem("z_read")
        z_stats = sem("z_stats")
        batch_var = sem("batch_var"); batch_sd = sem("batch_sd"); sd_ready = sem("sd_ready")
        ln1_ready = sem("ln1_ready"); h_ready = sem("h_ready"); h_stats = sem("h_stats")
        var_ready = sem("var_ready"); rstd_ready = sem("rstd_ready"); sn_ready = sem("sn_ready")
        s_hi_ready = sem("s_hi_ready"); s32_ready = sem("s32_ready"); pool_ln = sem("pool_ln")
        dve_ln = sem("dve_ln"); sn_step = sem("sn_step")
        s_ready = sem("s_ready"); t_done = sem("t_done")
        sTm_ready = sem("sTm_ready"); sT_ready = sem("sT_ready")
        q_done = sem("q_done"); qh_ready = sem("qh_ready"); q_used = sem("q_used")
        om_done = sem("om_done"); om_ready = sem("om_ready")
        a_done = sem("a_done"); a_ready = sem("a_ready")
        r_done = sem("r_done"); bank2_read = sem("bank2_read"); back_done = sem("back_done")
        back_ready = sem("back_ready"); h2_stats = sem("h2_stats")
        xn_ready = sem("xn_ready"); xn_step = sem("xn_step"); x_hi = sem("x_hi"); pool_ln3 = sem("pool_ln3")
        x_ready = sem("x_ready")
        xt_done = sem("xt_done"); xT_ready = sem("xT_ready"); lg_done = sem("lg_done")
        tanh_ready = sem("tanh_ready")
        dve_gate = sem("dve_gate"); gate_zero = sem("gate_zero")
        gt_done = sem("gt_done"); gT_ready = sem("gT_ready")
        hid_done = sem("hid_done"); hid_ready = sem("hid_ready"); w_done = sem("w_done")
        hw_ready = sem("hw_ready"); y_part = sem("y_part")
        yT_ready = sem("yT_ready"); fin_done = sem("fin_done"); res_ready = sem("res_ready")

        block = ctx.enter_context(nc.Block())

        N_WGT = 16 * 11
        ROUTE = 19
        OM_BANK = [0, 1, 2, 0, 1, 2, 0, 1]

        def q_bank(g, n):
            return bank[(3, 4, 7, 5)[n]] if isinstance(g, int) and g == 0 else bank[4]

        def a_bank(g, t):
            return bank[0] if isinstance(g, int) and g >= NG - 2 and t == 2 else bank[3]

        def tiles(g):
            return bass.ds(g * TG, TG)

        def wait(eng, s, value):
            if not isinstance(value, int) or value > 0:
                eng.wait_ge(s, value)

        @block.sync
        def _(sp):
            sp.wait_ge(emb_zero, 1)
            for n, (t, (c, r)) in enumerate(zip(tables, place)):
                v = t.shape[0]
                sp.dma_start(emb[r:r + v, c, n * EMB:(n + 1) * EMB], t).then_inc(s_emb, 16)
            for n, a in enumerate(idx):
                sp.dma_start(idx_i[n:n + 1, :], a.rearrange("(a b) s -> a (b s)", a=1)).then_inc(s_idx, 16)
            sp.dma_start(q_raw[0:D, :, :], Q.rearrange("h i j -> i h j")).then_inc(s_q, 16)
            sp.dma_start(q_raw[D:P, :, :], Q.rearrange("h i j -> i h j")).then_inc(s_q, 16)
            sp.dma_start(gam[:, :], gamma.rearrange("(a n) -> a n", a=1).broadcast_to([P, D])).then_inc(s_gam, 16)
            sp.dma_start(bet[:, :], beta.rearrange("(a n) -> a n", a=1).broadcast_to([P, D])).then_inc(s_gam, 16)
            sp.dma_start(e_raw[:, :, :], E.rearrange("h i j -> i h j")).then_inc(s_wgt, 16)
            for a in range(2):
                sp.dma_start(w1_raw[a * D:a * D + D, :, :], W1.rearrange("e d f -> d e f")).then_inc(s_wgt, 16)
                sp.dma_start(wr_raw[a * D:a * D + D, :], Wr).then_inc(s_wgt, 16)
                sp.dma_start(fg[a * D:a * D + D, :], fgamma.rearrange("(d a) -> d a", a=1)).then_inc(s_wgt, 16)
            sp.dma_start(fb[0:D, :], fbeta.rearrange("(d a) -> d a", a=1)).then_inc(s_wgt, 16)
            sp.dma_start(b1_raw[:, :], b1).then_inc(s_wgt, 16)
            sp.dma_start(br_raw[:, :], br.rearrange("(a n) -> a n", a=1)).then_inc(s_wgt, 16)
            sp.dma_start(w2[:, :, :], W2.rearrange("e f d -> f e d")).then_inc(s_wgt, 16)
            sp.wait_ge(b2_zero, 1)
            for k in (0, 8, 32, 40, 64, 72):
                sp.dma_start(b2_raw[k:k + NX, :], b2).then_inc(s_b2, 16)
            out_v = out.rearrange("(g t) p d -> p g t d", t=TG)
            res_v = res[:, :, :].rearrange("p (g t) d -> p g t d", t=TG)
            with sp.Fori(0, NG) as g:
                sp.wait_ge(res_ready, g + 1)
                sp.dma_start(out_v[:, bass.ds(g, 1), :, :].rearrange("p g t d -> p (g t) d"),
                             res_v[:, bass.ds(g, 1), :, :].rearrange("p g t d -> p (g t) d")).then_inc(s_out, 16)
            sp.wait_ge(s_out, 16 * NG)

        @block.gpsimd
        def _(pool):
            st = Steps(pool, pool_step)

            def link(ins):
                st.done(ins)
                st.settle()

            def select(a, pattern, base, slope, compare=ALU.not_equal, fill=1.0):
                link(pool.affine_select(out=a, in_=a, compare_op=compare, fill=fill, base=base, pattern=pattern,
                                        channel_multiplier=slope))

            pool.memset(emb[:, :, :], 0.0).then_inc(emb_zero, 1)
            link(pool.memset(ones[:, :], 1.0))
            pool.sem_inc(s_ones, 1)
            link(pool.memset(ident[:, :], 0.0))
            select(ident[:, :], [[-1, P]], 0, 1)
            pool.sem_inc(s_id, 1)
            link(pool.iota(row_i[:, :], pattern=[[0, NC]], base=0, channel_multiplier=1))
            for c in (0, 3):
                link(pool.iota(row_i[64:P, c:c + 1], pattern=[[0, 1]], base=0, channel_multiplier=1))
            link(pool.memset(sel[:, :], 0.0))
            for k, r in enumerate(half_row):
                select(sel[:, k * 64:(k + 1) * 64], [[0, 64]], -r, 1)
            pool.sem_inc(s_sel, 1)
            link(pool.memset(fold[:, :], 0.0))
            select(fold[:, :], [[-1, D]], 0, 1)
            select(fold[:, :], [[-1, D]], -D, 1)
            pool.sem_inc(fold_ready, 1)
            pool.memset(b2_raw[:, :], 0.0).then_inc(b2_zero, 1)
            link(pool.tensor_copy(ident16[:, :], ident[:, :]))
            pool.wait_ge(s_idx, 96)
            pool.wait_ge(idx_zero, 1)

            def convert(k):
                x = slice(2 * k * GC, 2 * (k + 1) * GC)
                pool.tensor_copy(idx_b[0:6, x], idx_i[:, x]).then_inc(idx_more, 1)

            convert(1)
            pool.wait_ge(s_peak, 1)
            pool.wait_ge(idx_more, 1)
            pool.partition_all_reduce(peak_all[:, 0:1], peak[:, 0:1], P, RMAX).then_inc(s_amax, 1)
            pool.wait_ge(s_amax, 1)
            convert(2)
            pool.wait_ge(idx_more, 2)
            convert(3)
            pool.wait_ge(idx_more, 3)
            link(pool.memset(causal[:, :], 1.0))
            select(causal[:, :], [[1, P]], 0, -1, ALU.is_ge, 0.0)
            link(pool.iota(rank_i[:, :], pattern=[[-1, NX]], base=NX, channel_multiplier=0))
            pool.sem_inc(s_pool, 1)
            pool.wait_ge(s_gam, 32)
            LN1, LN2, LN3 = 3, 7, 15

            def over(a, g):
                return a[:, g * TG:(g + 1) * TG].unsqueeze(2).broadcast_to([P, TG, D])

            def embed_norm(g):
                lc = Steps(pool, pool_h, (g - 1) * LN1, LN1)
                wait(pool, h_ready, g - 1)
                lc.done(pool.tensor_tensor(hn[:, :, :], z[:, g * TG:(g + 1) * TG, :], over(mean1, g), ALU.subtract))
                lc.settle()
                lc.done(pool.tensor_tensor(hn[:, :, :], hn[:, :, :], over(rstd1, g), ALU.mult))
                lc.settle()
                lc.done(pool.tensor_tensor(hn[:, :, :], hn[:, :, :], gam[:, :].unsqueeze(1).broadcast_to([P, TG, D]),
                                           ALU.mult))
                lc.settle()
                lc.close()
                pool.tensor_tensor(h[:, g * TG:(g + 1) * TG, :], hn[:, :, :], bet[:, :].unsqueeze(1).broadcast_to([P, TG, D]),
                                   ALU.add).then_inc(h_ready, 1)

            def h_variance(g):
                lc = Steps(pool, pool_ln, (g - 2) * LN2, LN2)

                def f(k):
                    return hstats[:, g * TG:(g + 1) * TG, k]
                pool.wait_ge(h_stats, (g + 1) * TG)
                wait(pool, var_ready, g - 2)
                lc.done(pool.tensor_tensor(mean[:, g * TG:(g + 1) * TG], f(1), f(4), ALU.add))
                lc.settle()
                lc.done(pool.tensor_tensor(diff[:, :], f(1), f(4), ALU.subtract))
                lc.settle()
                lc.done(pool.tensor_tensor(var[:, g * TG:(g + 1) * TG], f(2), f(5), ALU.add))
                lc.settle()
                lc.done(pool.tensor_scalar(mean[:, g * TG:(g + 1) * TG], mean[:, g * TG:(g + 1) * TG], 0.5, None, ALU.mult))
                lc.settle()
                lc.done(pool.tensor_tensor(diff[:, :], diff[:, :], diff[:, :], ALU.mult))
                lc.settle()
                lc.done(pool.tensor_scalar(diff[:, :], diff[:, :], 0.25, None, ALU.mult))
                lc.settle()
                lc.done(pool.tensor_scalar(var[:, g * TG:(g + 1) * TG], var[:, g * TG:(g + 1) * TG], 1.0 / D, EPS, ALU.mult, ALU.add))
                lc.settle()
                lc.close()
                pool.tensor_tensor(var[:, g * TG:(g + 1) * TG], var[:, g * TG:(g + 1) * TG], diff[:, :], ALU.add).then_inc(var_ready, 1)

            def normal(g):
                pool.wait_ge(rstd_ready, g - 1)
                wait(pool, s_ready, g)
                pool.wait_ge(s32_ready, g)
                pool.tensor_tensor(sn[:, :, :], h[:, g * TG:(g + 1) * TG, :], over(mean, g), ALU.subtract).then_inc(sn_step, 1)
                pool.wait_ge(sn_step, g - 1)
                pool.tensor_tensor(sn[:, :, :], sn[:, :, :], over(rstd, g), ALU.mult).then_inc(sn_ready, 1)

            def keep(g, u):
                pool.wait_ge(sn_ready, g - 1)
                pool.wait_ge(a_done, (g - 1) * TG)
                pool.tensor_copy(s32[:, u, :, :], sn[:, :, :]).then_inc(s32_ready, 1)

            pool.wait_ge(ln1_ready, 1)
            embed_norm(1)
            embed_norm(2)
            h_variance(2)
            pool.memset(minus_half[:, :], -0.5).then_inc(pool_ln3, 1)
            for g in range(NG - 1):
                if g >= 1:
                    keep(g + 1, (g + 1) % 2)
                if g + 2 < NG:
                    normal(g + 2)
                if g == 1:
                    pool.wait_ge(ln1_ready, 2)
                if g + 3 < NG:
                    embed_norm(g + 3)
                    h_variance(g + 3)

            def twice_normal(half):
                x, y = half * NT // 2, (half + 1) * NT // 2
                lc = Steps(pool, pool_ln3, 1 + half * LN3, LN3)
                m, r = mean3[:, x:y], rstd3[:, x:y]
                d, v, q = mean_gap3[:, :], var3[:, :], once[:, :]

                def f(k):
                    return stats[:, x:y, k]

                def step(ins):
                    lc.done(ins)
                    lc.settle()
                pool.wait_ge(h2_stats, y)
                lc.settle()
                step(pool.tensor_tensor(m, f(1), f(4), ALU.add))
                step(pool.tensor_tensor(d, f(1), f(4), ALU.subtract))
                step(pool.tensor_tensor(v, f(2), f(5), ALU.add))
                step(pool.tensor_scalar(m, m, 0.5, None, ALU.mult))
                step(pool.tensor_tensor(d, d, d, ALU.mult))
                step(pool.tensor_scalar(d, d, 0.25, None, ALU.mult))
                step(pool.tensor_scalar(v, v, 1.0 / D, None, ALU.mult))
                step(pool.tensor_tensor(v, v, d, ALU.add))
                step(pool.tensor_scalar(q, v, EPS, None, ALU.add))
                step(pool.tensor_tensor(r, q, minus_half[:, :], ALU.pow))
                step(pool.tensor_tensor(q, r, r, ALU.mult))
                step(pool.tensor_tensor(q, q, v, ALU.mult))
                step(pool.tensor_scalar(q, q, EPS, None, ALU.add))
                step(pool.tensor_tensor(q, q, minus_half[:, :], ALU.pow))
                step(pool.tensor_tensor(r, r, q, ALU.mult))
                lc.close()
                for g in range(x // TG, y // TG):
                    xg = z[:, g * TG:(g + 1) * TG, :]
                    pool.tensor_tensor(xg, h[:, g * TG:(g + 1) * TG, :], over(mean3, g), ALU.subtract).then_inc(xn_step, 1)
                    pool.wait_ge(xn_step, g + 1)
                    pool.tensor_tensor(xg, xg, over(rstd3, g), ALU.mult).then_inc(xn_ready, 1)

            link(pool.memset(sel_w[:, :, :], 0.0))
            for k in (0, NX):
                select(sel_w[:, :, :], [[-1, NX], [0, P]], -k, 1)
            pool.sem_inc(gate_zero, 1)
            pool.memset(gate16[:, :, :, :, :], 0.0).then_inc(gate_zero, 1)
            pool.wait_ge(gate_zero, 2)
            pool.wait_ge(s_peak, 3)
            pool.partition_all_reduce(peak_all[:, 1:3], peak[:, 1:3], P, RMAX).then_inc(s_amax, 1)
            pool.wait_ge(s_amax, 2)
            twice_normal(0)
            twice_normal(1)

        @block.vector
        def _(dve):
            st = Steps(dve, dve_setup)

            def link(ins):
                st.done(ins)
                st.settle()

            def row(a):
                return a.rearrange("p a d -> p (a d)")

            dve.memset(idx_b[:, :].bitcast(I32), 0).then_inc(idx_zero, 1)
            dve.wait_ge(emb_zero, 1)
            dve.memset(emb[64:68, 3, KW:KW + 1], 1.0).then_inc(one_ready, 1)
            dve.wait_ge(s_w, 16)
            dve.tensor_reduce(w_abs[:, :], w_raw[:, :], AX.X, ALU.add, apply_absolute_value=True).then_inc(w_sum, 1)
            dve.wait_ge(pe_wabs, 1)
            link(dve.tensor_scalar(w_s[:, 0:1], bank[0][:, 0:1], 1.0 / (D * KW), None, ALU.mult))
            st.done(dve.tensor_scalar(w_s[:, 1:2], w_s[:, 0:1], 1e-8, 0.5, ALU.add, ALU.mult))
            link(dve.tensor_scalar(w_s[:, 2:3], w_s[:, 0:1], 1e-8, -0.5, ALU.add, ALU.mult))
            st.done(dve.tensor_scalar(w_pos[:, :], w_raw[:, :], w_s[0:D, 1:2], None, ALU.is_gt))
            link(dve.tensor_scalar(w_neg[:, :], w_raw[:, :], w_s[0:D, 2:3], None, ALU.is_lt))
            link(dve.tensor_tensor(w_pos[:, :], w_pos[:, :], w_neg[:, :], ALU.subtract))
            link(dve.scalar_tensor_tensor(out=w_pos[:, :], in0=w_pos[:, :], scalar=w_s[0:D, 0:1], in1=w_raw[:, :],
                                          op0=ALU.mult, op1=ALU.subtract))
            dve.tensor_tensor(w_pos[:, :], w_pos[:, :], w_raw[:, :], ALU.add).then_inc(w_ready, 1)
            dve.wait_ge(pe_embT, 5)
            dve.tensor_copy(wT[0:KW, :], bank[5][0:KW, 0:D]).then_inc(embT_ready, 1)
            dve.wait_ge(s_sel, 1)
            link(dve.tensor_copy(row_id[:, :], row_i[:, :]))
            dve.wait_ge(pe_tab, 1)
            product = bank[6][:, 0:NC * D].rearrange("p (c d) -> p c d", d=D)
            link(dve.tensor_copy(tab[:, :, 0, :], product))
            dve.tensor_tensor(tab_f[:, :, :], product, tab[:, :, 0, :], ALU.subtract).then_inc(z_read, 1)
            dve.wait_ge(z_read, 1)
            link(dve.tensor_copy(tab[:, :, 1, :], tab_f[:, :, :]))
            dve.tensor_tensor(tab[:, :, 2, :], tab_f[:, :, :], tab[:, :, 1, :], ALU.subtract).then_inc(tab_ready, 1)

            def one_hot(g, u):
                for c in range(NC):
                    if c == 0:
                        dve.wait_ge(spread, g * NC + 1)
                        src = bank[0][:, :]
                    else:
                        dve.wait_ge(copied, g * 3 + c)
                        src = idx_c[:, u, c, :]
                    dve.tensor_scalar(hot[:, u, c, :], src, row_id[:, c:c + 1], None, ALU.is_equal).then_inc(hot_ready, 1)

            def z_moments(g):
                dve.wait_ge(z_read, g + 2)
                for t in range(TG):
                    tt = bass.ds(g * TG + t, 1)
                    dve.bn_stats(row(stats[:, tt, :]), row(z[:, tt, :])).then_inc(z_stats, 1)

            def scales(x, y):
                link(dve.tensor_scalar(peak_all[:, x:y], peak_all[:, x:y], 1e-30, None, ALU.max))
                link(dve.tensor_scalar(pow2[:, x:y].bitcast(I32), peak_all[:, x:y].bitcast(I32), 0x7F800000, None,
                                       ALU.bitwise_and))
                link(dve.reciprocal(up[:, x:y], pow2[:, x:y]))
                for k in range(x, y):
                    dve.tensor_scalar(up[:, k:k + 1], up[:, k:k + 1], LIFT[k], None, ALU.mult).then_inc(scale_ready, 1)
                    st.done(dve.tensor_scalar(down[:, k:k + 1], pow2[:, k:k + 1], 1.0 / LIFT[k], None, ALU.mult))
                st.settle()

            one_hot(0, 0)
            dve.wait_ge(s_q, 32)
            dve.tensor_reduce(peak[:, 0:1], q_raw[:, :, :], AX.XY, ALU.max, apply_absolute_value=True).then_inc(s_peak, 1)
            one_hot(1, 1)
            dve.wait_ge(s_amax, 1)
            scales(0, 1)
            with dve.Fori(1, NG // 2 - 1) as i:
                for u in range(2):
                    dve.wait_ge(zt_done, i * 2 + u - 1)
                    one_hot(i * 2 + u, u)
                    z_moments(i * 2 + u - 2)

            ch = Steps(dve, dve_ln)

            def moments(stats, mean, a, b):
                def f(k):
                    return stats[:, a:b, k]
                ch.done(dve.tensor_tensor(mean[:, a:b], f(1), f(4), ALU.add))
                ch.done(dve.tensor_tensor(tmp[:, a:b], f(1), f(4), ALU.subtract))
                ch.done(dve.tensor_tensor(var[:, a:b], f(2), f(5), ALU.add))
                ch.settle()
                ch.done(dve.tensor_scalar(mean[:, a:b], mean[:, a:b], 0.5, None, ALU.mult))
                ch.done(dve.scalar_tensor_tensor(out=tmp[:, a:b], in0=tmp[:, a:b], scalar=0.25, in1=tmp[:, a:b],
                                                 op0=ALU.mult, op1=ALU.mult))
                ch.settle()
                ch.done(dve.scalar_tensor_tensor(out=var[:, a:b], in0=var[:, a:b], scalar=1.0 / D, in1=tmp[:, a:b],
                                                 op0=ALU.mult, op1=ALU.add))
                ch.settle()

            def over(a, x, y):
                return a[:, x:y].unsqueeze(2).broadcast_to([P, y - x, D])

            def add_eps(x, y):
                dve.tensor_scalar(tmp[:, x:y], var[:, x:y], EPS, None, ALU.add).then_inc(batch_var, 1)

            def embed_scalars(x, y, root, n):
                dve.wait_ge(batch_sd, root)
                dve.reciprocal(rstd1[:, x:y], tmp2[:, x:y]).then_inc(ln1_ready, 1)
                dve.wait_ge(ln1_ready, n)

            def h_moments(g):
                wait(dve, h_ready, g)
                for t in range(TG):
                    tt = bass.ds(g * TG + t, 1)
                    dve.bn_stats(row(hstats[:, tt, :]), row(h[:, tt, :])).then_inc(h_stats, 1)

            def first_normal(g):
                x, y = g * TG, (g + 1) * TG
                ch.done(dve.tensor_tensor(s32[:, g, :, :], h[:, x:y, :], over(mean, x, y), ALU.subtract))
                ch.settle()
                dve.tensor_tensor(s32[:, g, :, :], s32[:, g, :, :], over(rstd, x, y), ALU.mult).then_inc(s32_ready, 1)
                dve.wait_ge(s32_ready, g + 1)
                twice = s32[:, g, :, :].unsqueeze(2).broadcast_to([P, TG, 2, D])
                wait(dve, t_done, g)
                ch.done(dve.tensor_copy(s16[:, :, 0:2, :], twice))
                ch.settle()
                dve.tensor_tensor(s16[:, :, 2:4, :], twice, s16[:, :, 0:2, :], ALU.subtract).then_inc(s_ready, 1)

            NA = (NG - 4) * TG
            dve.wait_ge(s_wgt, N_WGT)
            dve.tensor_copy(beta_row[:, :], fb[0:D, 0:1].broadcast_to([D, P])).then_inc(beta_ready, 1)
            dve.wait_ge(zt_done, NG - 3)
            one_hot(NG - 2, 0)
            dve.wait_ge(z_stats, NA)
            moments(stats, mean1, 0, NA)
            add_eps(0, NA)
            dve.wait_ge(q_hi_ready, 1)
            dve.scalar_tensor_tensor(out=q_lo[:, :], in0=q_raw[:, :, :].rearrange("p h j -> p (h j)"),
                                     scalar=up[:, 0:1], in1=q_hi[:, :], op0=ALU.mult,
                                     op1=ALU.subtract).then_inc(q_ready, 1)
            embed_scalars(0, NA, 1, 1)
            dve.wait_ge(zt_done, NG - 2)
            one_hot(NG - 1, 1)
            dve.wait_ge(s_gam, 32)
            z0, h0 = z[:, 0:TG, :], h[:, 0:TG, :]
            ch.done(dve.tensor_tensor(z0, z0, over(mean1, 0, TG), ALU.subtract))
            ch.settle()
            ch.done(dve.tensor_tensor(z0, z0, over(rstd1, 0, TG), ALU.mult))
            ch.settle()
            ch.done(dve.tensor_tensor(z0, z0, gam[:, :].unsqueeze(1).broadcast_to([P, TG, D]), ALU.mult))
            ch.settle()
            ch.done(dve.tensor_tensor(h0, z0, bet[:, :].unsqueeze(1).broadcast_to([P, TG, D]), ALU.add))
            ch.settle()
            h_moments(0)
            h_moments(1)
            dve.wait_ge(h_stats, 2 * TG)
            moments(hstats, mean, 0, 2 * TG)
            add_eps(0, 2 * TG)
            z_moments(NG - 4)
            dve.wait_ge(batch_sd, 2)
            ch.done(dve.reciprocal(rstd[:, 0:2 * TG], tmp2[:, 0:2 * TG]))
            ch.settle()
            first_normal(0)
            dve.wait_ge(s_pool, 1)
            st.done(dve.tensor_scalar(causal_q[:, :], causal[:, :], down[:, 0:1], None, ALU.mult))
            first_normal(1)

            def mask(g, t):
                wait(dve, a_done, (g - 1) * TG + t + 1)
                dve.wait_ge(om_done, g * TG + t + 1)
                for n in (2 * t, 2 * t + 1):
                    dve.tensor_tensor(om8[:, n, :, :], bank[5 + OM_BANK[n]][:, :].rearrange("p (h t) -> p h t", t=P),
                                      causal_q[:, :].unsqueeze(1).broadcast_to([P, HP, P]), ALU.mult).then_inc(om_ready, 1)

            def back(g, src):
                dve.wait_ge(back_done, g + 1)
                dve.tensor_tensor(h[:, tiles(g), :], h[:, tiles(g), :],
                                  src.rearrange("p (t d) -> p t d", d=D), ALU.add).then_inc(back_ready, 1)

            def sum_stats(g):
                dve.wait_ge(back_ready, g + 1)
                for t in range(TG):
                    tt = bass.ds(g * TG + t, 1)
                    dve.bn_stats(row(stats[:, tt, :]), row(h[:, tt, :])).then_inc(h2_stats, 1)

            def deviation(g):
                dve.wait_ge(sd_ready, g - 1)
                dve.reciprocal(rstd[:, tiles(g)], sd[:, tiles(g)]).then_inc(rstd_ready, 1)

            def s_lower(g):
                dve.wait_ge(s_hi_ready, g - 1)
                dve.tensor_tensor(s16[:, :, 2:4, :], sn[:, :, :].unsqueeze(2).broadcast_to([P, TG, 2, D]),
                                  s16[:, :, 0:2, :], ALU.subtract).then_inc(s_ready, 1)

            def q_lower(g, u, n):
                dve.wait_ge(qh_ready, g * HP + n + 1)
                dve.tensor_tensor(ql[:, u, n, :], q_bank(g, n)[:, :], qh[:, u, n, :], ALU.subtract).then_inc(q_used, 1)

            def expert_input(g, u):
                dve.wait_ge(xn_ready, g + 1)
                dve.wait_ge(x_hi, g + 1)
                dve.tensor_tensor(x16[:, u, :, 1, :], z[:, tiles(g), :], x16[:, u, :, 0, :],
                                  ALU.subtract).then_inc(x_ready, 1)

            def route(p, k, src):
                if k > 0:
                    dve.wait_ge(dve_gate, p * ROUTE + k)

                def wide(a):
                    return a[:, :].unsqueeze(2).broadcast_to([P, TR, NX])
                rank_w = rank[:, :].unsqueeze(1).broadcast_to([P, TR, NX])
                gates = gate16[:, bass.ds(p * TR, TR), :, :, :]
                thrice = both[:, :, :].unsqueeze(2).broadcast_to([P, TR, 3, NX])
                if k == 0:
                    dve.wait_ge(lg_done, (p + 1) * 2)
                    wait(dve, dve_gate, p * ROUTE)
                    ins = dve.scalar_tensor_tensor(out=lg[:, :, :],
                                                   in0=src[:, 256:256 + TR * NX].rearrange("p (t e) -> p t e", e=NX),
                                                   scalar=down[:, 2:3],
                                                   in1=br_f[:, :].unsqueeze(1).broadcast_to([P, TR, NX]),
                                                   op0=ALU.mult, op1=ALU.add)
                elif k == 1:
                    ins = dve.tensor_reduce(top1[:, :], lg[:, :, :], AX.X, ALU.max)
                elif k == 2:
                    ins = dve.tensor_tensor(pick[:, :, :], lg[:, :, :], wide(top1), ALU.is_equal)
                elif k in (3, 10):
                    ins = dve.tensor_tensor(pick[:, :, :], pick[:, :, :], rank_w, ALU.mult)
                elif k in (4, 11):
                    ins = dve.tensor_reduce(best[:, :], pick[:, :, :], AX.X, ALU.max)
                elif k == 5:
                    ins = dve.tensor_tensor(sel1[:, :, :], pick[:, :, :], wide(best), ALU.is_equal)
                elif k == 6:
                    ins = dve.scalar_tensor_tensor(out=lg2[:, :, :], in0=sel1[:, :, :], scalar=-3e38, in1=lg[:, :, :],
                                                   op0=ALU.mult, op1=ALU.add)
                elif k == 7:
                    ins = dve.tensor_reduce(top2[:, :], lg2[:, :, :], AX.X, ALU.max)
                elif k == 8:
                    ins = dve.tensor_tensor(gap[:, :], top2[:, :], top1[:, :], ALU.subtract)
                elif k == 9:
                    ins = dve.tensor_tensor(pick[:, :, :], lg2[:, :, :], wide(top2), ALU.is_equal)
                elif k == 12:
                    ins = dve.tensor_tensor(sel2[:, :, :], pick[:, :, :], wide(best), ALU.is_equal)
                elif k == 13:
                    ins = dve.tensor_tensor(both[:, :, :], sel1[:, :, :], sel2[:, :, :], ALU.add)
                elif k == 14:
                    ins = dve.tensor_tensor(diff2[:, :, :], sel2[:, :, :], sel1[:, :, :], ALU.subtract)
                elif k == 15:
                    dve.wait_ge(tanh_ready, p + 1)
                    ins = dve.scalar_tensor_tensor(out=diff2[:, :, :], in0=diff2[:, :, :], scalar=0.5, in1=wide(tanh),
                                                   op0=ALU.mult, op1=ALU.mult)
                elif k == 16:
                    ins = dve.scalar_tensor_tensor(out=both[:, :, :], in0=both[:, :, :], scalar=0.5,
                                                   in1=diff2[:, :, :], op0=ALU.mult, op1=ALU.add)
                elif k == 17:
                    ins = dve.tensor_copy(gates[:, :, :, 0, :], thrice)
                elif k == 18:
                    ins = dve.tensor_tensor(gates[:, :, :, 1, :], thrice, gates[:, :, :, 0, :], ALU.subtract)
                ins.then_inc(dve_gate, 1)

            def attend(g, u, first=False):
                left = NG - 1 - g if isinstance(g, int) else NG
                mask(g, 0)
                if left == 0:
                    dve.wait_ge(w1_hi_ready, 2)
                    dve.scalar_tensor_tensor(out=w1_lo[:, :, :], in0=w1_raw[:, :, :], scalar=up[:, 1:2],
                                             in1=w1_hi[:, :, :], op0=ALU.mult, op1=ALU.subtract).then_inc(w1_ready, 1)
                    dve.scalar_tensor_tensor(out=wr_lo[:, :], in0=wr_raw[:, :], scalar=up[:, 2:3],
                                             in1=wr_hi[:, :], op0=ALU.mult, op1=ALU.subtract).then_inc(w1_ready, 1)
                if left >= 1:
                    q_lower(g + 1, 1 - u, 0)
                if left >= 2:
                    deviation(g + 2)
                mask(g, 1)
                if left >= 1:
                    q_lower(g + 1, 1 - u, 1)
                if left == 1:
                    dve.wait_ge(s_amax, 2)
                    scales(1, 3)
                if left == 0:
                    expert_input(0, 0)
                mask(g, 2)
                if left >= 1:
                    q_lower(g + 1, 1 - u, 2)
                if not first:
                    back(g - 1, bank[1][:, 256:512])
                if left == 0:
                    expert_input(1, 1)
                if left >= 2:
                    s_lower(g + 2)
                if left >= 3:
                    h_moments(g + 3)
                mask(g, 3)
                if left >= 1:
                    q_lower(g + 1, 1 - u, 3)
                if left and not first:
                    sum_stats(g - 1)

            for n in range(HP):
                q_lower(0, 0, n)
            h_moments(2)
            attend(0, 0, first=True)
            dve.wait_ge(pe_bias, 1)
            link(dve.tensor_copy(b1_f[:, :], bank[2][:, 0:NX]))
            st.done(dve.tensor_tensor(b1_f[:, :], b1_f[:, :], bank[2][:, NX:2 * NX], ALU.add))
            st.done(dve.tensor_copy(br_f[:, :], bank[2][:, 2 * NX:3 * NX]))
            dve.tensor_copy(eT[:, :, :], bank[2][:, 256:256 + HP * D].rearrange("p (a d) -> p a d", d=D)).then_inc(bank2_read, 1)
            z_moments(NG - 3)
            z_moments(NG - 2)
            z_moments(NG - 1)
            dve.wait_ge(z_stats, NT)
            moments(stats, mean1, NA, NT)
            add_eps(NA, NT)
            embed_scalars(NA, NT, 3, 2)
            with dve.Fori(0, (NG - 4) // 2) as i:
                for u in (1, 0):
                    attend(i * 2 + (1 if u else 2), u)
            attend(NG - 3, 1)
            dve.wait_ge(w1_scaled, 2)
            dve.tensor_reduce(peak[:, 1:2], w1_raw[:, :, :], AX.XY, ALU.max, apply_absolute_value=True).then_inc(s_peak, 1)
            dve.tensor_reduce(peak[:, 2:3], wr_raw[:, :], AX.X, ALU.max, apply_absolute_value=True).then_inc(s_peak, 1)
            dve.wait_ge(s_b2, 96)
            link(dve.tensor_copy(b2_h[:, :], b2_raw[:, :]))
            link(dve.tensor_tensor(b2_raw[:, :], b2_raw[:, :], b2_h[:, :], ALU.subtract))
            link(dve.tensor_copy(b2_m[:, :], b2_raw[:, :]))
            link(dve.tensor_tensor(b2_raw[:, :], b2_raw[:, :], b2_m[:, :], ALU.subtract))
            dve.tensor_copy(b2_p[0:32, :], b2_h[0:32, :]).then_inc(b2_ready, 1)
            dve.tensor_copy(b2_p[32:64, :], b2_m[32:64, :]).then_inc(b2_ready, 1)
            dve.tensor_copy(b2_p[64:96, :], b2_raw[64:96, :]).then_inc(b2_ready, 1)
            link(dve.tensor_copy(rank[:, :], rank_i[:, :]))
            attend(NG - 2, 0)
            attend(NG - 1, 1)
            sum_stats(NG - 2)
            for k in range(ROUTE):
                route(0, k, bank[4])
            back(NG - 1, bank[6][:, 0:256])
            sum_stats(NG - 1)

            def finish(g):
                dve.wait_ge(fin_done, g + 1)
                dve.tensor_tensor(res[:, tiles(g), :], h[:, tiles(g), :],
                                  bank[7][:, 0:256].rearrange("p (t d) -> p t d", d=D), ALU.add).then_inc(res_ready, 1)

            def gated(g, e, first=False):
                dve.wait_ge(hid_ready, g * NX + e + 1)
                dve.wait_ge(w_done, g * NX + e + 1)
                if not first:
                    dve.wait_ge(y_part, (g - 1) * NX + e + 1)
                dve.tensor_tensor(hw[:, e, :], hid[:, e, :], bank[3 + e % 2][:, :], ALU.mult).then_inc(hw_ready, 1)
                if e == 4 and not first:
                    finish(g - 1)

            SLOTS = {5: (0, 2), 6: (2, 5), 7: (5, 7), 8: (7, 10), 9: (10, 12), 10: (12, 15), 11: (15, 17), 12: (17, 19)}

            def experts(p, first=False, more=True):
                for n in range(2 * NX):
                    if more and n < 2:
                        expert_input(p * 2 + 2 + n, n)
                    gated(p * 2 + n // NX, n % NX, first and n < NX)
                    if more and n in SLOTS:
                        for k in range(*SLOTS[n]):
                            route(p + 1, k, bank[2])

            experts(0, first=True)
            with dve.Fori(1, NG // 2 - 1) as p:
                experts(p)
            experts(NG // 2 - 1, more=False)
            finish(NG - 1)

        @block.scalar
        def _(act):
            act.dma_start(w_raw[:, :], W).then_inc(s_w, 16)
            act.dma_start(wT[KW:KW + 1, :], b.rearrange("(a n) -> a n", a=1)).then_inc(s_emb, 16)
            act.wait_ge(s_ones, 1)
            act.activation(tmp2[:, 0:1], ones[:, 0:1], ACT.Sqrt)
            for c in range(NC):
                act.wait_ge(pe_embT, c + 1)
                act.activation(embT[:, c, :], bank[1 + c][0:KW + 1, 0:P],
                               ACT.Copy).then_inc(embT_ready if c < NC - 1 else zT_read, 1)

            act.wait_ge(s_idx, 96)
            act.wait_ge(idx_zero, 1)
            for g in range(2):
                act.activation(idx_b[0:6, g * GC:(g + 1) * GC], idx_i[:, g * GC:(g + 1) * GC],
                               ACT.Copy).then_inc(idx_ready, 1)

            def copies(g, u, first=False):
                for c in range(1, NC):
                    if not first:
                        act.wait_ge(hot_ready, (g - 2) * NC + c + 1)
                    act.wait_ge(spread, g * NC + c + 1)
                    act.activation(idx_c[:, u, c, :], bank[c][:, :], ACT.Copy).then_inc(copied, 1)

            def zT_copy(g, u):
                act.wait_ge(zt_done, g + 1)
                act.activation(zT[:, u, :], bank[4 + u][:, :], ACT.Copy).then_inc(zT_read, 1)

            def z_copy(g):
                act.wait_ge(z_done, g + 1)
                act.activation(z[:, tiles(g), :], bank[6][:, 0:TG * D].rearrange("p (t d) -> p t d", d=D),
                               ACT.Copy).then_inc(z_read, 1)

            copies(0, 0, True)
            copies(1, 1, True)
            act.wait_ge(scale_ready, 1)
            act.activation(q_hi[:, :], q_raw[:, :, :].rearrange("p h j -> p (h j)"), ACT.Copy,
                           scale=up[:, 0:1]).then_inc(q_hi_ready, 1)
            with act.Fori(1, NG // 2 - 1) as i:
                for u in range(2):
                    zT_copy(i * 2 + u - 2, u)
                    copies(i * 2 + u, u)
                    z_copy(i * 2 + u - 2)

            def root(n, x, y):
                act.wait_ge(batch_var, n)
                act.activation(tmp2[:, x:y], tmp[:, x:y], ACT.Sqrt).then_inc(batch_sd, 1)

            NA = (NG - 4) * TG
            zT_copy(NG - 4, 0)
            copies(NG - 2, 0)
            z_copy(NG - 4)
            zT_copy(NG - 3, 1)
            root(1, 0, NA)
            copies(NG - 1, 1)
            z_copy(NG - 3)
            zT_copy(NG - 2, 0)
            z_copy(NG - 2)
            zT_copy(NG - 1, 1)
            root(2, 0, 2 * TG)

            def deviation(g):
                act.wait_ge(var_ready, g - 1)
                act.activation(sd[:, tiles(g)], var[:, tiles(g)], ACT.Sqrt).then_inc(sd_ready, 1)

            def sT_copy(g, u):
                act.wait_ge(t_done, g + 1)
                wait(act, q_done, (g - 1) * HP)
                act.activation(sTm[:, u, :], bank[0][:, 0:256].bitcast(F16), ACT.Copy).then_inc(sTm_ready, 1)
                wait(act, om_done, (g - 1) * TG)
                act.activation(sTh[:, u, :], bank[0][:, 256:512].bitcast(F16), ACT.Copy).then_inc(sT_ready, 1)
                act.activation(sTl[:, u, :], bank[1][:, 0:256].bitcast(F16), ACT.Copy).then_inc(sT_ready, 1)

            def s_upper(g):
                act.wait_ge(sn_ready, g - 1)
                act.wait_ge(t_done, g)
                act.activation(s16[:, :, 0:2, :], sn[:, :, :].unsqueeze(2).broadcast_to([P, TG, 2, D]),
                               ACT.Copy).then_inc(s_hi_ready, 1)

            def q_upper(g, u, n):
                act.wait_ge(q_done, g * HP + n + 1)
                wait(act, om_done, (g - 1) * TG)
                act.activation(qh[:, u, n, :], q_bank(g, n)[:, :], ACT.Copy).then_inc(qh_ready, 1)

            def a_copy(g, t):
                act.wait_ge(a_done, g * TG + t + 1)
                wait(act, r_done, g)
                act.activation(aT[:, :, t * P:(t + 1) * P], a_bank(g, t)[:, :].rearrange("p (a t) -> p a t", t=P),
                               ACT.Copy).then_inc(a_ready, 1)

            def r_copy(g):
                act.wait_ge(r_done, g + 1)
                act.activation(rT[:, :], bank[2][:, :], ACT.Copy).then_inc(bank2_read, 1)

            def attend(g, u, first=False):
                left = NG - 1 - g if isinstance(g, int) else NG
                if left >= 1:
                    q_upper(g + 1, 1 - u, 0)
                if left >= 2:
                    deviation(g + 2)
                if not first:
                    r_copy(g - 1)
                if left >= 1:
                    q_upper(g + 1, 1 - u, 1)
                if left == 0:
                    x_upper(0, 0)
                    x_upper(1, 1)
                a_copy(g, 0)
                if left >= 2:
                    s_upper(g + 2)
                if left >= 1:
                    q_upper(g + 1, 1 - u, 2)
                a_copy(g, 1)
                if left >= 1:
                    q_upper(g + 1, 1 - u, 3)
                if left == 0:
                    xT_copy(0, bank[4])
                a_copy(g, 2)
                if left == 0:
                    xT_copy(1, bank[4])
                if left >= 2:
                    sT_copy(g + 2, u)
                a_copy(g, 3)

            act.wait_ge(t_done, 1)
            act.activation(sTm[:, 0, :], bank[0][:, 0:256].bitcast(F16), ACT.Copy).then_inc(sTm_ready, 1)
            act.activation(sTh[:, 0, :], bank[0][:, 256:512].bitcast(F16), ACT.Copy).then_inc(sT_ready, 1)
            q_upper(0, 0, 0)
            act.activation(sTl[:, 0, :], bank[1][:, 0:256].bitcast(F16), ACT.Copy).then_inc(sT_ready, 1)
            q_upper(0, 0, 1)
            q_upper(0, 0, 2)
            z_copy(NG - 1)
            q_upper(0, 0, 3)
            sT_copy(1, 1)
            attend(0, 0, first=True)
            root(3, NA, NT)
            act.wait_ge(pe_bias, 1)
            act.activation(w1_raw[:, :, :], w1_raw[:, :, :], ACT.Copy, scale=fg[:, 0:1]).then_inc(w1_scaled, 1)
            act.activation(wr_raw[:, :], wr_raw[:, :], ACT.Copy, scale=fg[:, 0:1]).then_inc(w1_scaled, 1)
            with act.Fori(0, (NG - 4) // 2) as i:
                for u in (1, 0):
                    attend(i * 2 + (1 if u else 2), u)
            attend(NG - 3, 1)
            attend(NG - 2, 0)
            act.wait_ge(batch_sd, 3)
            act.activation(tmp2[:, 0:1], ones[:, 0:1], ACT.Gelu)
            act.wait_ge(scale_ready, 3)
            act.activation(wr_hi[:, :], wr_raw[:, :], ACT.Copy, scale=up[:, 2:3]).then_inc(w1_hi_ready, 1)
            act.activation(w1_hi[:, :, :], w1_raw[:, :, :], ACT.Copy, scale=up[:, 1:2]).then_inc(w1_hi_ready, 1)

            def x_upper(g, u):
                act.wait_ge(xn_ready, g + 1)
                wait(act, xt_done, g - 1)
                act.activation(x16[:, u, :, 0, :], z[:, tiles(g), :], ACT.Copy).then_inc(x_hi, 1)

            def xT_copy(g, src):
                act.wait_ge(xt_done, g + 1)
                act.activation(xT[:, bass.ds(g * GC, GC)], src[:, 0:256].bitcast(F16), ACT.Copy).then_inc(xT_ready, 1)

            def tanh_gap(p):
                act.wait_ge(dve_gate, p * ROUTE + 9)
                act.activation(tanh[:, :], gap[:, :], ACT.Tanh, scale=0.5).then_inc(tanh_ready, 1)

            attend(NG - 1, 1)

            def gelu(g, e, first=False):
                act.wait_ge(hid_done, g * NX + e + 1)
                if not first:
                    act.wait_ge(hw_ready, (g - 1) * NX + e + 1)
                act.activation(hid[:, e, :], bank[e % 2][:, :], ACT.Gelu, bias=b1_f[:, e:e + 1],
                               scale=down[:, 1:2]).then_inc(hid_ready, 1)

            def gT_copy(g, u):
                act.wait_ge(gt_done, g + 1)
                wait(act, w_done, (g - 1) * NX)
                act.activation(gT[:, u, :], bank[7][0:96, 256:512].bitcast(F16), ACT.Copy).then_inc(gT_ready, 1)

            def yT_copy(g, u):
                act.wait_ge(y_part, (g + 1) * NX)
                wait(act, fin_done, g)
                act.activation(yT[:, :], bank[5 + u][:, :], ACT.Copy).then_inc(yT_ready, 1)

            def experts(p, first=False, more=True):
                for n in range(2 * NX):
                    u, e = n // NX, n % NX
                    g = p * 2 + u
                    start = first and u == 0
                    if start and e == 0:
                        x_upper(2, 0)
                        gelu(0, 0, True)
                        r_copy(NG - 1)
                        tanh_gap(0)
                        continue
                    if more and n in ((4, 6) if start else (2, 4)):
                        xT_copy(g + 2 + (n == (6 if start else 4)), bank[2])
                    if more and n == NX + 2:
                        tanh_gap(p + 1)
                    if more and n < 2:
                        x_upper(p * 2 + 2 + n, n)
                    gelu(g, e, start)
                    if start and e == 2:
                        gT_copy(0, 0)
                    if e == 1 and not start:
                        yT_copy(g - 1, 1 - u)
                    if n == (7 if start else 6) or (more and n == 2 * NX - 2):
                        gT_copy(g + 1, 1 - u)

            experts(0, first=True)
            with act.Fori(1, NG // 2 - 1) as p:
                experts(p)
            experts(NG // 2 - 1, more=False)
            yT_copy(NG - 1, 1)

        @block.tensor
        def _(pe):
            def stay_warm(n):
                for _ in range(n):
                    pe.matmul(bank[7][:, 0:P], ones[:, :], ones[:, :], start=True, stop=True)

            pe.wait_ge(w_sum, 1)
            pe.wait_ge(s_ones, 1)
            pe.matmul(bank[0][:, 0:1], ones[0:D, :], w_abs[:, :], start=True, stop=True).then_inc(pe_wabs, 1)
            pe.wait_ge(s_id, 1)
            pe.wait_ge(s_emb, 16 * 7)
            pe.wait_ge(one_ready, 1)
            for c in range(NC):
                pe.transpose(bank[1 + c][0:KW + 1, 0:P], emb[:, c, :], ident[:, :]).then_inc(pe_embT, 1)
            pe.wait_ge(w_ready, 1)
            pe.transpose(bank[5][0:KW, 0:D], w_pos[:, :], ident[0:D, 0:D]).then_inc(pe_embT, 1)
            pe.wait_ge(embT_ready, 4)
            pe.wait_ge(zT_read, 1)
            for c in range(NC):
                mm = pe.matmul(bank[6][:, c * D:(c + 1) * D], embT[:, c, :], wT[:, :], start=True, stop=True)
            mm.then_inc(pe_tab, 1)

            def spread_idx(g, first=False):
                for c in range(NC):
                    if not first:
                        if c == 0:
                            pe.wait_ge(hot_ready, (g - 1) * NC + 1)
                        else:
                            pe.wait_ge(copied, (g - 1) * 3 + c)
                    pe.matmul(bank[c][:, :], sel[:, c * P:(c + 1) * P],
                              idx_b[:, g * GC:(g + 1) * GC] if isinstance(g, int) else idx_b[:, bass.ds(g * GC, GC)],
                              start=True, stop=True).then_inc(spread, 1)

            def look_up(g, u):
                pe.wait_ge(hot_ready, (g + 1) * NC)
                wait(pe, zT_read, g)
                for c in range(NC):
                    pe.matmul(bank[4 + u][:, :], tab[:, c, 0:2, :].rearrange("p k d -> p (k d)"), hot[:, u, c, :],
                              start=(c == 0), stop=False)
                for c in range(NC):
                    o = c % 2 * D
                    mm = pe.matmul(bank[4 + u][o:o + D, :], tab[:, c, 2, :], hot[:, u, c, :],
                                   start=False, stop=(c >= NC - 2))
                mm.then_inc(zt_done, 1)

            def fold_z(g, u):
                pe.wait_ge(zT_read, g + 2)
                pe.wait_ge(z_read, g + 1)
                for t in range(TG):
                    mm = pe.matmul(bank[6][:, t * D:(t + 1) * D], zT[:, u, t * P:(t + 1) * P], fold[:, :],
                                   start=True, stop=True)
                mm.then_inc(z_done, 1)

            pe.wait_ge(idx_ready, 1)
            pe.wait_ge(s_sel, 1)
            spread_idx(0, True)
            pe.wait_ge(idx_ready, 2)
            spread_idx(1)
            pe.wait_ge(tab_ready, 1)
            look_up(0, 0)
            pe.wait_ge(fold_ready, 1)
            with pe.Fori(1, NG // 2 - 1) as i:
                pe.wait_ge(idx_more, i)
                for u in range(2):
                    spread_idx(i * 2 + u)
                    fold_z(i * 2 + u - 2, u)
                    look_up(i * 2 + u - 1, 1 - u)
            pe.wait_ge(idx_more, NG // 2 - 1)
            spread_idx(NG - 2)
            fold_z(NG - 4, 0)
            look_up(NG - 3, 1)
            spread_idx(NG - 1)
            fold_z(NG - 3, 1)
            look_up(NG - 2, 0)
            fold_z(NG - 2, 0)
            look_up(NG - 1, 1)

            def turn(g):
                pe.wait_ge(s_ready, g + 1)
                wait(pe, back_ready, g - 2)
                wait(pe, sT_ready, 2 * g)
                for dst, k in ((bank[0][:, 0:256], 1), (bank[0][:, 256:512], 0), (bank[1][:, 0:256], 2)):
                    for t in range(TG):
                        mm = pe.transpose(dst[:, t * 64:(t + 1) * 64].bitcast(F16),
                                          s16[:, t, k:k + 2, :].rearrange("p k d -> p (k d)"), ident16[:, :])
                mm.then_inc(t_done, 1)

            def project(g, u, n):
                pe.wait_ge(sTm_ready, g + 1)
                wait(pe, q_used, g * HP + n if not isinstance(g, int) or g > 0 else 0)
                for k, w in enumerate((q_hi, q_lo)):
                    mm = pe.matmul(q_bank(g, n)[:, :], w[:, n * P:(n + 1) * P], sTm[:, u, :],
                                   start=(k == 0), stop=(k == 1))
                mm.then_inc(q_done, 1)

            def omega(g, u, t):
                wait(pe, om_ready, g * 2 * TG + [0, 1, 3, 5][t])
                if t == 0:
                    pe.wait_ge(sT_ready, 2 * (g + 1))
                    pe.wait_ge(q_used, (g + 1) * HP)
                tt = slice(t * P, (t + 1) * P)
                for k, (sx, qx) in enumerate(((sTh, qh), (sTh, ql), (sTl, qh))):
                    for par in range(2):
                        r = slice(par * D, par * D + D)
                        mm = pe.matmul(bank[5 + OM_BANK[2 * t + par]][:, :], sx[r, u, tt], qx[r, u, :, tt],
                                       start=(k == 0), stop=(k == 2))
                mm.then_inc(om_done, 1)

            def weigh(g, u, t):
                if t == 0:
                    pe.wait_ge(s32_ready, g + 1)
                free = t - 1 if isinstance(g, int) and g >= NG - 2 and t >= 2 else t
                wait(pe, a_ready, g * TG + free)
                pe.wait_ge(om_ready, (g * TG + t + 1) * 2)
                for par in range(2):
                    mm = pe.matmul(a_bank(g, t)[par * D:par * D + D, :], s32[:, u, t, :],
                                   om8[:, 2 * t + par, :, :].rearrange("p a t -> p (a t)"), start=True, stop=True)
                mm.then_inc(a_done, 1)

            def mix(g):
                pe.wait_ge(a_ready, (g + 1) * TG)
                pe.wait_ge(bank2_read, g + 1)
                for n in range(HP):
                    o = n % 2 * D
                    mm = pe.matmul(bank[2][o:o + D, :], eT[:, n, :], aT[:, n, :], start=(n < 2), stop=(n >= 2))
                mm.then_inc(r_done, 1)

            def back(g, dst):
                pe.wait_ge(bank2_read, g + 2)
                for t in range(TG):
                    mm = pe.matmul(dst[:, t * D:(t + 1) * D], rT[:, t * P:(t + 1) * P], fold[:, :],
                                   start=True, stop=True)
                mm.then_inc(back_done, 1)

            def turn_x(g, u, dst):
                pe.wait_ge(x_ready, g + 1)
                wait(pe, xT_ready, g)
                for t in range(TG):
                    mm = pe.transpose(dst[:, t * 64:(t + 1) * 64].bitcast(F16),
                                      x16[:, u, t, :, :].rearrange("p k d -> p (k d)"), ident16[:, :])
                mm.then_inc(xt_done, 1)

            def logits(g, u, p, dst):
                pe.wait_ge(xT_ready, g + 1)
                wait(pe, dve_gate, p * ROUTE - (ROUTE - 1))
                for t in range(TG):
                    o = dst[:, 256 + (u * TG + t) * NX:256 + (u * TG + t + 1) * NX]
                    x = xT[:, bass.ds(g * GC + t * P, P)]
                    pe.matmul(o, x, wr_hi[:, :], start=True, stop=False)
                    mm = pe.matmul(o, x, wr_lo[:, :], start=False, stop=True)
                mm.then_inc(lg_done, 1)

            def hidden(g, e):
                wait(pe, hid_ready, g * NX + e - 1)
                rhs = xT[:, g * GC:(g + 1) * GC] if isinstance(g, int) else xT[:, bass.ds(g * GC, GC)]
                for k, w in enumerate((w1_hi, w1_lo)):
                    mm = pe.matmul(bank[e % 2][:, :], w[:, e, :], rhs, start=(k == 0), stop=(k == 1))
                mm.then_inc(hid_done, 1)

            def attend(g, u, first=False):
                left = NG - 1 - g if isinstance(g, int) else NG
                omega(g, u, 0)
                if left >= 1:
                    project(g + 1, 1 - u, 0)
                if not first:
                    mix(g - 1)
                omega(g, u, 1)
                if left >= 1:
                    project(g + 1, 1 - u, 1)
                weigh(g, u, 0)
                if not first:
                    back(g - 1, bank[1][:, 256:512])
                omega(g, u, 2)
                if left >= 1:
                    project(g + 1, 1 - u, 2)
                weigh(g, u, 1)
                if left == 0:
                    turn_x(0, 0, bank[4])
                omega(g, u, 3)
                if left >= 1:
                    project(g + 1, 1 - u, 3)
                if left == 0:
                    pe.wait_ge(w1_ready, 2)
                    logits(0, 0, 0, bank[4])
                weigh(g, u, 2)
                if left >= 2:
                    turn(g + 2)
                if left == 0:
                    turn_x(1, 1, bank[4])
                weigh(g, u, 3)
                if left == 0:
                    logits(1, 1, 0, bank[4])
                    hidden(0, 0)

            def fold_beta():
                pe.wait_ge(s_wgt, N_WGT)
                pe.wait_ge(beta_ready, 1)
                pe.transpose(bank[2][:, 0:NX], b1_raw[:, :], ident[0:NX, 0:NX])
                for e in range(NX):
                    pe.matmul(bank[2][:, NX + e:NX + e + 1], w1_raw[0:D, e, :], fb[0:D, 0:1], start=True, stop=True)
                pe.matmul(bank[2][:, 2 * NX:3 * NX], beta_row[:, :], wr_raw[0:D, :], start=True, stop=False)
                pe.matmul(bank[2][:, 2 * NX:3 * NX], ones[0:1, :], br_raw[:, :], start=False, stop=True)
                for n in range(HP):
                    mm = pe.transpose(bank[2][:, 256 + n * D:256 + (n + 1) * D],
                                      e_raw[:, 2 * n:2 * n + 2, :].rearrange("p h d -> p (h d)"), ident[0:D, 0:D])
                mm.then_inc(pe_bias, 1)

            stay_warm(4)
            fold_beta()
            turn(0)
            pe.wait_ge(q_ready, 1)
            fold_z(NG - 1, 1)
            for n in range(HP):
                project(0, 0, n)
            turn(1)
            pe.wait_ge(z_read, NG + 1)
            attend(0, 0, first=True)
            with pe.Fori(0, (NG - 4) // 2) as i:
                for u in (1, 0):
                    attend(i * 2 + (1 if u else 2), u)
            for g in range(NG - 3, NG):
                attend(g, g % 2)
            mix(NG - 1)
            pe.wait_ge(back_ready, NG - 1)
            hidden(0, 1)
            back(NG - 1, bank[6][:, 0:256])
            def turn_gate(g, p):
                pe.wait_ge(dve_gate, (p + 1) * ROUTE)
                wait(pe, res_ready, g - 1)
                for t in range(TG):
                    src = gate16[:, bass.ds(g * TG + t, 1), :, :, :].rearrange("p a x y e -> p (a x y e)")
                    mm = pe.transpose(bank[7][0:96, 256 + t * 64:256 + (t + 1) * 64].bitcast(F16), src, ident16[:, :])
                mm.then_inc(gt_done, 1)

            def spread_gate(g, u, e):
                if e == 0:
                    pe.wait_ge(gT_ready, g + 1)
                wait(pe, hw_ready, g * NX + e - 1)
                pe.matmul(bank[3 + e % 2][:, :], sel_w[:, e, :], gT[:, u, :], start=True, stop=True).then_inc(w_done, 1)

            def outer(g, u, e):
                pe.wait_ge(hw_ready, g * NX + e + 1)
                o = e % 2 * D
                if e == 0:
                    wait(pe, yT_ready, g - 1)
                    pe.matmul(bank[5 + u][0:D, :], b2_p[:, :], gT[:, u, :], start=True, stop=False)
                mm = pe.matmul(bank[5 + u][o:o + D, :], w2[:, e, :], hw[:, e, :], start=(e == 1), stop=(e >= NX - 2))
                mm.then_inc(y_part, 1)

            def finish(g):
                pe.wait_ge(yT_ready, g + 1)
                for t in range(TG):
                    mm = pe.matmul(bank[7][:, t * D:(t + 1) * D], yT[:, t * P:(t + 1) * P], fold[:, :],
                                   start=True, stop=True)
                mm.then_inc(fin_done, 1)

            def experts(p, first=False, more=True):
                if first:
                    hidden(0, 2)
                    turn_gate(0, 0)
                    hidden(0, 3)
                for n in range(2 * NX):
                    u, e = n // NX, n % NX
                    g = p * 2 + u
                    start = first and u == 0
                    if not start:
                        hidden(g, e)
                    elif 2 <= e < NX - 2:
                        hidden(g, e + 2)
                    spread_gate(g, u, e)
                    if e >= 2:
                        outer(g, u, e - 2)
                    elif not start:
                        outer(g - 1, 1 - u, NX - 2 + e)
                    if more and n in (1, 3):
                        turn_x(g + 2 + n // 2, n // 2, bank[2])
                    if more and n in (2, 4):
                        logits(g + 1 + n // 2, n // 2 - 1, p + 1, bank[2])
                    if e == 4 and not start:
                        finish(g - 1)
                    if n == 6:
                        turn_gate(g + 1, p)
                    if more and n == 2 * NX - 2:
                        turn_gate(g + 1, p + 1)

            pe.wait_ge(b2_ready, 3)
            pe.wait_ge(gate_zero, 1)
            experts(0, first=True)
            with pe.Fori(1, NG // 2 - 1) as p:
                experts(p)
            experts(NG // 2 - 1, more=False)
            outer(NG - 1, 1, NX - 2)
            outer(NG - 1, 1, NX - 1)
            finish(NG - 1)


_INS = ['x', 'itok_BS_0_255', 'itok_BS_0_511', 'itok_BS_0_127', 'itok_BS_0_63', 'itok_BS_0_3',
        'L0_tok_E_et', 'L0_tok_E_fc', 'L0_tok_E_sc', 'L0_tok_E_of', 'L0_tok_E_tt', 'L0_tok_E_rc',
        'L0_tok_W', 'L0_tok_b', 'L0_tok_gamma', 'L0_tok_beta', 'L0_attn_Q', 'L0_attn_E',
        'L0_ffn_gamma', 'L0_ffn_beta', 'L0_ffn_Wr', 'L0_ffn_br', 'L0_ffn_W1', 'L0_ffn_b1', 'L0_ffn_W2', 'L0_ffn_b2']


def kernel(**inputs):
    import numpy as _np
    import concourse.bacc as _bacc
    from concourse import mybir as _mybir
    from concourse.bass_utils import run_bass_kernel_spmd as _run

    nc = _bacc.Bacc("TRN2", target_bir_lowering=False, num_devices=1)
    arrays, args = {}, []
    for name in _INS:
        a = _np.ascontiguousarray(inputs[name])
        arrays[f"in_{name}_dram"] = a
        args.append(nc.dram_tensor(f"in_{name}_dram", a.shape, _mybir.dt.from_np(a.dtype), kind="ExternalInput").ap())
    B, S = inputs['x'].shape
    D = inputs['L0_tok_W'].shape[0]
    out = nc.dram_tensor("out_dram", (B, S, D), _mybir.dt.float32, kind="ExternalOutput").ap()
    lm_tower(nc, args[0:6], args[6:12], *args[12:], out)
    r = _run(nc, [arrays], core_ids=[0])
    return r.results[0]["out_dram"]
```
